# Optimizing a Trainium2 kernel written in Bass

```python
import numpy as np
import jax
import jax.numpy as jnp

def _softmax(x, axis=-1):
    return jax.nn.softmax(x, axis=axis)
def _gelu(x):
    return jax.nn.gelu(x, approximate=True)
def _silu(x):
    return jax.nn.silu(x)
def _sigmoid(x):
    return jax.nn.sigmoid(x)
def _layernorm(x, axis=-1, eps=1e-5):
    m = jnp.mean(x, axis=axis, keepdims=True)
    v = jnp.var(x, axis=axis, keepdims=True)
    return (x - m) / jnp.sqrt(v + eps)
def _scatter_add(tgt, idx, src, axis=0):
    return tgt.at[idx].add(src)
def _segment_sum(src, seg, n):
    return jax.ops.segment_sum(src, seg, n)

kernel_name = 'mk_conv_preact_d2_conv_nchw256_23fb9d'

def setup_inputs(seed: int = 0):
    np.random.seed(seed)
    _w = jnp.asarray
    def _rec_inputs():
        import jax
        import jax.numpy as jnp
        _gk = jax.random.key(seed)
        x = -0.0003929 + 0.9999 * jax.random.normal(jax.random.fold_in(_gk, 1), (16, 256, 64, 64), jnp.float32)
        return x
    x = _rec_inputs()
    def _L0_conv_setup():
        import jax, jax.numpy as jnp
        import numpy as np
        import math

        def _rotate_one(kernel, angle):
            kH, kW = (kernel.shape[2], kernel.shape[3])
            cy, cx = ((kH - 1) / 2.0, (kW - 1) / 2.0)
            y = jnp.arange(kH, dtype=kernel.dtype) - cy
            x = jnp.arange(kW, dtype=kernel.dtype) - cx
            yy, xx = jnp.meshgrid(y, x, indexing='ij')
            c, s = (jnp.cos(angle), jnp.sin(angle))
            x_rot = xx * c + yy * s + cx
            y_rot = -xx * s + yy * c + cy
            x0 = jnp.clip(jnp.floor(x_rot), 0, kW - 2)
            y0 = jnp.clip(jnp.floor(y_rot), 0, kH - 2)
            x1 = x0 + 1
            y1 = y0 + 1
            w00 = (x1 - x_rot) * (y1 - y_rot)
            w01 = (x1 - x_rot) * (y_rot - y0)
            w10 = (x_rot - x0) * (y1 - y_rot)
            w11 = (x_rot - x0) * (y_rot - y0)
            x0i = x0.astype(jnp.int32)
            y0i = y0.astype(jnp.int32)
            x1i = x1.astype(jnp.int32)
            y1i = y1.astype(jnp.int32)
            return w00 * kernel[..., y0i, x0i] + w01 * kernel[..., y1i, x0i] + w10 * kernel[..., y0i, x1i] + w11 * kernel[..., y1i, x1i]
        key = jax.random.key(seed)
        ks = jax.random.split(key, 6)
        B, C, H, W = (16, 256, 64, 64)
        G, Cg, K = (8, 32, 3)
        HID = C // 4
        fan_out = Cg * K * K
        return {'x': jax.random.normal(ks[0], (B, C, H, W), jnp.float32), 'base_kernel': jax.random.normal(ks[1], (G, Cg, Cg, K, K), jnp.float32) * np.sqrt(2.0 / fan_out), 'ap_w1': jax.random.normal(ks[2], (HID, C), jnp.float32) * np.sqrt(1.0 / C), 'ap_b1': jnp.zeros((HID,), jnp.float32), 'ap_w2': jax.random.normal(ks[3], (G, HID), jnp.float32) * np.sqrt(1.0 / HID), 'ap_b2': jnp.zeros((G,), jnp.float32), 'meta_w1': jax.random.normal(ks[4], (HID, C), jnp.float32) * np.sqrt(1.0 / C), 'meta_b1': jnp.zeros((HID,), jnp.float32), 'meta_w2': jax.random.normal(ks[5], (C, HID), jnp.float32) * np.sqrt(1.0 / HID), 'meta_b2': jnp.zeros((C,), jnp.float32)}
    _L0_conv_all = _L0_conv_setup()
    _L0_conv_in = {k: v for k, v in _L0_conv_all.items() if k in ('base_kernel', 'ap_w1', 'ap_b1', 'ap_w2', 'ap_b2', 'meta_w1', 'meta_b1', 'meta_w2', 'meta_b2', )}
    del _L0_conv_all

    def _L1_conv_setup():
        import jax, jax.numpy as jnp
        import numpy as np
        from jax import lax
        NUM_HEADS = 8
        FOCUSING_FACTOR = 3.0
        KERNEL_SIZE = 5
        key = jax.random.key(seed)
        ks = jax.random.split(key, 9)
        B, C, H, W = (16, 256, 64, 64)
        s = 0.02
        return {'x': jax.random.normal(ks[0], (B, C, H, W), dtype=jnp.float32), 'Wq': jax.random.normal(ks[1], (C, C), dtype=jnp.float32) * s, 'bq': jax.random.normal(ks[2], (C,), dtype=jnp.float32) * s, 'Wkv': jax.random.normal(ks[3], (2 * C, C), dtype=jnp.float32) * s, 'bkv': jax.random.normal(ks[4], (2 * C,), dtype=jnp.float32) * s, 'Wproj': jax.random.normal(ks[5], (C, C), dtype=jnp.float32) * s, 'bproj': jax.random.normal(ks[6], (C,), dtype=jnp.float32) * s, 'dwc_w': jax.random.normal(ks[7], (C // NUM_HEADS, 1, KERNEL_SIZE, KERNEL_SIZE), dtype=jnp.float32) * s, 'dwc_b': jax.random.normal(ks[8], (C // NUM_HEADS,), dtype=jnp.float32) * s, 'scale_param': jnp.zeros((1, 1, C), dtype=jnp.float32)}
    _L1_conv_all = _L1_conv_setup()
    _L1_conv_in = {k: v for k, v in _L1_conv_all.items() if k in ('Wq', 'bq', 'Wkv', 'bkv', 'Wproj', 'bproj', 'dwc_w', 'dwc_b', 'scale_param', )}
    del _L1_conv_all

    return {
        "x": x,
        "L0_conv_base_kernel": _L0_conv_in["base_kernel"],
        "L0_conv_ap_w1": _L0_conv_in["ap_w1"],
        "L0_conv_ap_b1": _L0_conv_in["ap_b1"],
        "L0_conv_ap_w2": _L0_conv_in["ap_w2"],
        "L0_conv_ap_b2": _L0_conv_in["ap_b2"],
        "L0_conv_meta_w1": _L0_conv_in["meta_w1"],
        "L0_conv_meta_b1": _L0_conv_in["meta_b1"],
        "L0_conv_meta_w2": _L0_conv_in["meta_w2"],
        "L0_conv_meta_b2": _L0_conv_in["meta_b2"],
        "L1_conv_Wq": _L1_conv_in["Wq"],
        "L1_conv_bq": _L1_conv_in["bq"],
        "L1_conv_Wkv": _L1_conv_in["Wkv"],
        "L1_conv_bkv": _L1_conv_in["bkv"],
        "L1_conv_Wproj": _L1_conv_in["Wproj"],
        "L1_conv_bproj": _L1_conv_in["bproj"],
        "L1_conv_dwc_w": _L1_conv_in["dwc_w"],
        "L1_conv_dwc_b": _L1_conv_in["dwc_b"],
        "L1_conv_scale_param": _L1_conv_in["scale_param"],
    }

def reference(x, L0_conv_base_kernel, L0_conv_ap_w1, L0_conv_ap_b1, L0_conv_ap_w2, L0_conv_ap_b2, L0_conv_meta_w1, L0_conv_meta_b1, L0_conv_meta_w2, L0_conv_meta_b2, L1_conv_Wq, L1_conv_bq, L1_conv_Wkv, L1_conv_bkv, L1_conv_Wproj, L1_conv_bproj, L1_conv_dwc_w, L1_conv_dwc_b, L1_conv_scale_param):
    import jax
    import jax.numpy as jnp
    def _L0_conv_ref(x, base_kernel, ap_w1, ap_b1, ap_w2, ap_b2, meta_w1, meta_b1, meta_w2, meta_b2):
        import jax, jax.numpy as jnp
        import numpy as np
        import math

        def _rotate_one(kernel, angle):
            kH, kW = (kernel.shape[2], kernel.shape[3])
            cy, cx = ((kH - 1) / 2.0, (kW - 1) / 2.0)
            y = jnp.arange(kH, dtype=kernel.dtype) - cy
            x = jnp.arange(kW, dtype=kernel.dtype) - cx
            yy, xx = jnp.meshgrid(y, x, indexing='ij')
            c, s = (jnp.cos(angle), jnp.sin(angle))
            x_rot = xx * c + yy * s + cx
            y_rot = -xx * s + yy * c + cy
            x0 = jnp.clip(jnp.floor(x_rot), 0, kW - 2)
            y0 = jnp.clip(jnp.floor(y_rot), 0, kH - 2)
            x1 = x0 + 1
            y1 = y0 + 1
            w00 = (x1 - x_rot) * (y1 - y_rot)
            w01 = (x1 - x_rot) * (y_rot - y0)
            w10 = (x_rot - x0) * (y1 - y_rot)
            w11 = (x_rot - x0) * (y_rot - y0)
            x0i = x0.astype(jnp.int32)
            y0i = y0.astype(jnp.int32)
            x1i = x1.astype(jnp.int32)
            y1i = y1.astype(jnp.int32)
            return w00 * kernel[..., y0i, x0i] + w01 * kernel[..., y1i, x0i] + w10 * kernel[..., y0i, x1i] + w11 * kernel[..., y1i, x1i]
        B, C, H, W = x.shape
        G, Cg = (base_kernel.shape[0], base_kernel.shape[1])
        K = base_kernel.shape[-1]
        pad = (K - 1) // 2
        pooled = x.mean(axis=(2, 3))
        h = jax.nn.relu(pooled @ ap_w1.T + ap_b1)
        angles = jnp.tanh(h @ ap_w2.T + ap_b2) * (math.pi / 4)
        rot = jax.vmap(jax.vmap(_rotate_one), in_axes=(None, 0))(base_kernel, angles)
        w = rot.reshape(B * C, Cg, K, K)
        out = jax.lax.conv_general_dilated(x.reshape(1, B * C, H, W), w, window_strides=(1, 1), padding=[(pad, pad), (pad, pad)], dimension_numbers=('NCHW', 'OIHW', 'NCHW'), feature_group_count=B * G)
        feat = out.reshape(B, C, H, W)
        m = jax.nn.relu(pooled @ meta_w1.T + meta_b1)
        mod = jax.nn.sigmoid(m @ meta_w2.T + meta_b2)
        return feat * mod[:, :, None, None]

    def _L1_conv_ref(x, Wq, bq, Wkv, bkv, Wproj, bproj, dwc_w, dwc_b, scale_param):
        import jax, jax.numpy as jnp
        import numpy as np
        from jax import lax
        NUM_HEADS = 8
        FOCUSING_FACTOR = 3.0
        KERNEL_SIZE = 5
        B, C, H, W = x.shape
        nh = NUM_HEADS
        hd = C // nh
        N = H * W
        num = int(round(N ** 0.5))
        xt = x.reshape(B, C, N).transpose(0, 2, 1)
        q = xt @ Wq.T + bq
        kv = xt @ Wkv.T + bkv
        k, v = (kv[..., :C], kv[..., C:])
        scale = jax.nn.softplus(scale_param)
        q = (jax.nn.relu(q) + 1e-06) / scale
        k = (jax.nn.relu(k) + 1e-06) / scale
        q_norm = jnp.linalg.norm(q, axis=-1, keepdims=True)
        k_norm = jnp.linalg.norm(k, axis=-1, keepdims=True)
        q = q ** FOCUSING_FACTOR
        k = k ** FOCUSING_FACTOR
        q = q / jnp.linalg.norm(q, axis=-1, keepdims=True) * q_norm
        k = k / jnp.linalg.norm(k, axis=-1, keepdims=True) * k_norm

        def split_heads(t):
            return t.reshape(B, N, nh, hd).transpose(0, 2, 1, 3).reshape(B * nh, N, hd)
        q, k, v = (split_heads(q), split_heads(k), split_heads(v))
        z = 1.0 / (jnp.einsum('bic,bc->bi', q, k.sum(axis=1)) + 1e-06)
        kv_state = jnp.einsum('bjc,bjd->bcd', k, v)
        out = jnp.einsum('bic,bcd->bid', q, kv_state) * z[..., None]
        fm = v.transpose(0, 2, 1).reshape(B * nh, hd, num, num)
        fm = lax.conv_general_dilated(fm, dwc_w, window_strides=(1, 1), padding=[(KERNEL_SIZE // 2, KERNEL_SIZE // 2)] * 2, dimension_numbers=('NCHW', 'OIHW', 'NCHW'), feature_group_count=hd) + dwc_b[None, :, None, None]
        fm = fm.reshape(B * nh, hd, N).transpose(0, 2, 1)
        out = out + fm
        out = out.reshape(B, nh, N, hd).transpose(0, 2, 1, 3).reshape(B, N, C)
        out = out @ Wproj.T + bproj
        return out.transpose(0, 2, 1).reshape(B, C, H, W)

    def _gn(v, G=32, eps=1e-5):
        B_, C_, H_, W_ = v.shape
        g = v.reshape(B_, G, C_ // G, H_, W_)
        m = jnp.mean(g, axis=(2, 3, 4), keepdims=True)
        s = jnp.var(g, axis=(2, 3, 4), keepdims=True)
        return ((g - m) / jnp.sqrt(s + eps)).reshape(v.shape)

    def _ln_c(v, eps=1e-6):
        m = jnp.mean(v, axis=1, keepdims=True)
        s = jnp.var(v, axis=1, keepdims=True)
        return (v - m) / jnp.sqrt(s + eps)

    def _ln_t(v, eps=1e-5):
        m = jnp.mean(v, axis=-1, keepdims=True)
        s = jnp.var(v, axis=-1, keepdims=True)
        return (v - m) / jnp.sqrt(s + eps)

    def _to_tokens(v):
        B_, C_, H_, W_ = v.shape
        return v.reshape(B_, C_, H_ * W_).transpose(0, 2, 1)
    def _from_tokens(t, like):
        B_, C_, H_, W_ = like.shape
        return t.transpose(0, 2, 1).reshape(B_, C_, H_, W_)

    x = x + _L0_conv_ref(_gn(x), L0_conv_base_kernel, L0_conv_ap_w1, L0_conv_ap_b1, L0_conv_ap_w2, L0_conv_ap_b2, L0_conv_meta_w1, L0_conv_meta_b1, L0_conv_meta_w2, L0_conv_meta_b2)
    x = x + _L1_conv_ref(_gn(x), L1_conv_Wq, L1_conv_bq, L1_conv_Wkv, L1_conv_bkv, L1_conv_Wproj, L1_conv_bproj, L1_conv_dwc_w, L1_conv_dwc_b, L1_conv_scale_param)
    return x


_drawn_inputs = setup_inputs


def setup_inputs(seed=0):
    import zlib

    import numpy as np

    out = dict(_drawn_inputs(seed))
    spreads = {'L0_conv_ap_b1': (0.0, 0.306),
     'L0_conv_ap_b2': (0.0, 0.267),
     'L0_conv_meta_b1': (0.0, 0.468),
     'L0_conv_meta_b2': (0.0, 0.275),
     'L1_conv_scale_param': (0.0, 0.8)}
    factors = {'L0_conv_ap_w1': 8.0,
     'L0_conv_meta_w1': 8.0,
     'L0_conv_meta_w2': 3.506,
     'L1_conv_Wq': 8.0,
     'L1_conv_bq': 36.529,
     'L1_conv_Wkv': 5.61,
     'L1_conv_bkv': 8.0,
     'L1_conv_Wproj': 4.52,
     'L1_conv_bproj': 3.29,
     'L1_conv_dwc_w': 6.798,
     'L1_conv_dwc_b': 8.0}
    for name, (base, spread) in spreads.items():
        noise = np.random.default_rng([zlib.crc32(name.encode()), seed]).standard_normal(out[name].shape)
        drawn = base * np.exp(spread * noise) if base else spread * noise
        out[name] = jnp.asarray(drawn.astype(out[name].dtype))
    for name, factor in factors.items():
        out[name] = (out[name] * factor).astype(out[name].dtype)
    return out
```

```python
import concourse.bass as bass
from concourse import mybir
from contextlib import ExitStack


def conv_then_focused_attention(
    nc: bass.Bass,
    x: bass.AP,
    conv_w: bass.AP,
    mlp_w1: bass.AP,
    mlp_b1: bass.AP,
    mlp_w2: bass.AP,
    mlp_b2: bass.AP,
    wqkv: bass.AP,
    bqkv: bass.AP,
    head_scale: bass.AP,
    wproj: bass.AP,
    bproj: bass.AP,
    dw_rows: bass.AP,
    dw_taps: bass.AP,
    dw_b: bass.AP,
    out: bass.AP,
):
    f32, f16, bf16 = mybir.dt.float32, mybir.dt.float16, mybir.dt.bfloat16
    ALU = mybir.AluOpType
    ACT = mybir.ActivationFunctionType
    AX = mybir.AxisListType
    RMAX = bass.bass_isa.ReduceOp.max

    B, C, N = x.shape
    P = 128
    HALVES = C // P
    IMG = 64
    UNIT = 512
    NU = N // UNIT
    TPU = UNIT // P
    NT = N // P
    HD = 32
    HEADS = C // HD
    HPH = HEADS // HALVES
    TAPS = 9
    STRIP = 16
    NS = IMG // STRIP
    SROWS, SCOLS = STRIP + 2, IMG + 2
    PROWS = SROWS // 2
    NPARTS = 2 * HALVES * NS
    CHUNKS = 2 * HALVES * NS
    PAIRS = 2 * NU
    XS = 64.0
    GN_EPS = 1e-5
    FOCUS_EPS = 1e-6
    TINY = 1e-30
    KVC = P + HPH
    QUARTER_PI = 0.7853981633974483
    HALF_PI = 1.5707963267948966

    ctx = ExitStack()
    with ctx:
        def sb(name, shape, dt=f32):
            return ctx.enter_context(nc.sbuf_tensor(name, shape, dt))

        def pb(name):
            return ctx.enter_context(nc.psum_tensor(name, [P, 512], f32))

        def sem(name):
            return ctx.enter_context(nc.semaphore(name))

        X = sb("X", [P, HALVES, N])
        XHL = sb("XHL", [P, 2, HALVES, N], f16)
        V = sb("V", [P, HD, 2, NT * HEADS], f16)
        FM = V[:, :, :, :].rearrange("p c a n -> p (c a n)").bitcast(f32).rearrange("p (c n) -> p c n", c=HD)
        TP = sb("TP", [P, HD, 3, 2, P], f16)
        WQ = sb("WQ", [P, 2, HALVES, 3 * C], f16)
        BQ = sb("BQ", [P, 3 * C], f16)
        ONES = sb("ONES", [P, P], f16)
        WP = sb("WP", [P, 2, HALVES, C], f16)
        FL = sb("FL", [P, C])
        BD = sb("BD", [P, 2, HALVES, TAPS, P], f16)
        ZEROS = BD[0:32, 0, 0, 0:2, 32:32 + P // 2 + 1]
        KB = sb("KB", [P, HALVES, TAPS, HD])
        W1 = sb("W1", [P, HALVES, P])
        W2 = sb("W2", [P, C])
        GM = sb("GM", [P, P])
        ID = sb("ID", [P, P])
        KVS = sb("KVS", [P, HALVES, KVC])
        COEF = sb("COEF", [P, TAPS, HALVES * TAPS])
        WK = sb("WK", [P, 3 * 1024])
        K0 = WK[:, 0:1024].rearrange("p (a n) -> p a n", a=2)
        K2 = WK[:, 1024:2048].rearrange("p (a n) -> p a n", a=2)
        K3 = WK[:, 2048:3072].rearrange("p (a n) -> p a n", a=2)
        SN = 2 * 2 * SROWS * SCOLS // 2
        S = WK[:, 0:SN].bitcast(f16).rearrange("p (g a r c) -> p g a r c", g=2, a=2, r=SROWS)
        VT = sb("VT", [P, 2, 2, HALVES, P + 2])
        QT = VT[:, :, :, :, :].rearrange("p a b c d -> p (a b c d)")[:, 0:1024].rearrange(
            "p (a h n) -> p a h n", a=2, h=HALVES)
        XN = sb("XN", [P, 2, PROWS * IMG])
        ROT = XN[:, 0, :].rearrange("p (h t o) -> p h t o", h=HALVES, t=TAPS)
        RTMP = XN[:, 1, :].rearrange("p (h t o) -> p h t o", h=HALVES, t=TAPS)
        O = sb("O", [P, 2, 2 * C])
        OT = sb("OT", [P, 2, HALVES, UNIT], f16)
        Y = sb("Y", [P, HALVES, UNIT])
        TR = sb("TR", [P, UNIT])
        B1 = sb("B1", [P, 1])
        B2 = sb("B2", [P, 2, HALVES])
        BP = sb("BP", [P, HALVES])
        DWB = sb("DWB", [P, HD])
        CK = sb("CK", [P, 2])
        XX = sb("XX", [P, 2, TAPS])
        ST = sb("ST", [P, HALVES, NU, 6])
        MV = sb("MV", [P, HALVES, 2])
        GS = sb("GS", [P, 8, HALVES])
        MEAN, DEV, SPREAD, VAR, ROOT, STD, RSTD, POOLED = (GS[:, i, :] for i in range(8))
        PR = sb("PR", [P, 9, HALVES])
        SC0, BI0, SC1, BI1, MODA, STDN, CBN, STDC, CBC = (PR[:, i, :] for i in range(9))
        HID = sb("HID", [P, 3])
        ZB = sb("ZB", [P, 4, HALVES])
        SIN = sb("SIN", [P, 3, HALVES])
        TT = sb("TT", [P, 2, HALVES, TAPS])
        TW = sb("TW", [P, 3, 2, HALVES * TAPS])
        S2 = sb("S2", [P, TPU])
        S6 = sb("S6", [P, TPU])
        RATIO = sb("RATIO", [P, 2, TPU])
        NORM = sb("NORM", [P, TPU])
        Z = sb("Z", [P, 2, HEADS])
        SCAL = sb("SCAL", [P, 24])

        def col(i):
            return SCAL[:, i:i + 1]
        (m_w, m_v, m_k, m_p) = (col(i) for i in range(4))
        (m_b, m_bv, m_db, s_t, m_t, a_w, inv_a, inv_a2, den_eps, a_v, v_fac, a_t, fm_fac, a_o, a_p, out_fac,
         a_r, conv_fac, v_bound, spare) = (col(4 + i) for i in range(20))

        F = [pb("F0"), pb("F1")]
        VA = [pb("VA0"), pb("VA1")]
        T = [pb("T0"), pb("T1")]
        PP = pb("PP")
        SM = pb("SM")

        w_in = sem("w_in")
        taps_in = sem("taps_in")
        x_in = sem("x_in")
        y_out = [sem("y_out0"), sem("y_out1")]
        set_dve = sem("set_dve")
        set_act = sem("set_act")
        soft_rdy = sem("soft_rdy")
        set_pool = sem("set_pool")
        rev_full = sem("rev_full")
        tp_act = sem("tp_act")
        tp_dve = sem("tp_dve")
        stats_rdy = sem("stats_rdy")
        z_rdy = sem("z_rdy")
        carried = sem("carried")
        ready = sem("ready")
        chain = sem("chain")
        mean_rdy, mean_mm = sem("mean_rdy"), sem("mean_mm")
        spread_rdy, spread_mm = sem("spread_rdy"), sem("spread_mm")
        var_rdy, root_rdy = sem("var_rdy"), sem("root_rdy")
        norm_rdy = sem("norm_rdy")
        pooled_rdy, hid_mm = sem("pooled_rdy"), sem("hid_mm")
        hid_rdy, z_mm = sem("hid_rdy"), sem("z_mm")
        zb_rdy, trig_rdy = sem("zb_rdy"), sem("trig_rdy")
        squash_rdy = sem("squash_rdy")
        rot_rdy, bd_hi, bd_lo = sem("rot_rdy"), sem("bd_hi"), sem("bd_lo")
        xn_rdy, h_rdy, l_rdy = sem("xn_rdy"), sem("h_rdy"), sem("l_rdy")
        border = sem("border")
        conv_full, x1_rdy = sem("conv_full"), sem("x1_rdy")
        f_full, f_max, f_sq = sem("f_full"), sem("f_max"), sem("f_sq")
        f_cube, f_six, f_ratio, f_root = sem("f_cube"), sem("f_six"), sem("f_ratio"), sem("f_root")
        k_scaled, cube_used = sem("k_scaled"), sem("cube_used")
        v_full, v_hi, v_true, v_lo = sem("v_full"), sem("v_hi"), sem("v_true"), sem("v_lo")
        ones_rdy = sem("ones_rdy")
        state_full, state_rdy = sem("state_full"), sem("state_rdy")
        dw_full, fm_rdy = sem("dw_full"), sem("fm_rdy")
        qt_rdy, attn_full, o_rdy = sem("qt_rdy"), sem("attn_full"), sem("o_rdy")
        ot_full, oh_rdy, ol_rdy = sem("ot_full"), sem("oh_rdy"), sem("ol_rdy")
        y_full, y_act, y_rdy = sem("y_full"), sem("y_act"), sem("y_rdy")
        tr_rdy, kept = sem("tr_rdy"), sem("kept")

        L_CR, X1_CR, MAX_CR, CUBE_CR, USED_CR, SIX_CR = 2, 2, 2, 2, 2, 4
        VLO_CR, FM_CR, O_CR, OL_CR, YA_CR = 2, 2, 2, 2, 1
        Y_CR, AT_CR, OUT_CR = 1, 1, 1
        N_W = 12
        N_CHAIN = 59

        block = ctx.enter_context(nc.Block())

        VF = V[:, :, :, :].rearrange("p c a n -> p (c a n)").bitcast(f32)
        wq32 = VF[:, 0:1536].rearrange("p (h n) -> p h n", h=HALVES)
        bq32 = VF[:, 1536:2304]
        sc32 = VF[:, 2304:2560]
        wp32 = VF[:, 2560:3072].rearrange("p (h n) -> p h n", h=HALVES)
        dt32 = VF[:, 3072:3872]
        W_A, W_B, W_C, W_D, W_E, W_F = (VF[:, 4096 + 256 * i:4352 + 256 * i] for i in range(6))
        bh16 = VF[:, 6144:6528].bitcast(f16)
        bl16 = VF[:, 6528:6912].bitcast(f16)
        dsum = VF[:, 6912:6944]
        CH2 = HD // 2
        TS = XHL[:, :, :, :].rearrange("p a h n -> p (a h n)").bitcast(f32)[:, 0:CH2 * 3 * P].rearrange(
            "p (c k n) -> p c k n", c=CH2, k=3)

        REVS = CH2 * 3 * P // 512
        REV = XN[:, 1, 0:P]
        TPM = TP[:, :, :, :, :].rearrange("p c k a n -> p (c k) a n")

        def strip_rows(s, p):
            lo, hi = PROWS * p, PROWS * (p + 1)
            if s == 0 and p == 0:
                lo = 1
            if s == NS - 1 and p == 1:
                hi -= 1
            return lo, hi, STRIP * s - 1 + lo

        def carry(eng):
            eng.sem_inc(carried, 1)

        @block.sync
        def _(sp):
            for h in range(HALVES):
                sp.sem_inc(y_out[h], 16 * OUT_CR)
            sp.dma_start(wq32, wqkv.rearrange("(h p) n -> p h n", p=P)).then_inc(w_in, 16)
            sp.dma_start(bq32, bqkv[0, :].partition_broadcast(P)).then_inc(w_in, 16)
            sp.dma_start(sc32, head_scale[0, :].partition_broadcast(P)).then_inc(w_in, 16)
            sp.dma_start(wp32, wproj.rearrange("(h p) n -> p h n", p=P)).then_inc(w_in, 16)
            sp.dma_start(dt32, dw_taps[0, :].partition_broadcast(P)).then_inc(w_in, 16)
            sp.dma_start(DWB[:, :], dw_b[0, :].partition_broadcast(P)).then_inc(w_in, 16)
            sp.dma_start(KB[:, :, :, :], conv_w.rearrange("(h p) t o -> p h t o", p=P)).then_inc(w_in, 16)
            sp.dma_start(W1[:, :, :], mlp_w1.rearrange("(h p) n -> p h n", p=P)).then_inc(w_in, 16)
            sp.dma_start(W2[:, :], mlp_w2).then_inc(w_in, 16)
            sp.dma_start(B1[:, :], mlp_b1).then_inc(w_in, 16)
            sp.dma_start(B2[:, :, :].rearrange("p k h -> p (k h)"), mlp_b2).then_inc(w_in, 16)
            sp.dma_start(BP[:, :], bproj).then_inc(w_in, 16)
            xv = x.rearrange("b (h p) n -> b p h n", p=P)
            ov = out.rearrange("b (h p) n -> b p h n", p=P)

            def load(c, u):
                sp.dma_start(X[:, :, bass.ds(u * UNIT, UNIT)],
                             xv[bass.ds(c, 1), :, :, bass.ds(u * UNIT, UNIT)].rearrange("b p h n -> p (b h) n")
                             ).then_inc(x_in, 16)

            def store(b, u):
                for h in range(HALVES):
                    sp.wait_ge(y_rdy, (b * NU + u) * HALVES + h + 1 + Y_CR)
                    sp.dma_start(ov[bass.ds(b, 1), :, h, bass.ds(u * UNIT, UNIT)].rearrange("b p n -> p (b n)"),
                                 Y[:, h, :]).then_inc(y_out[h], 16)

            def load_next(c, u):
                sp.wait_ge(xn_rdy, (c - 1) * 2 * NPARTS + NPARTS + HALVES * (u + 1))
                load(c, u)

            with sp.Fori(0, NU) as u:
                load(0, u)
            for rnd in range(2):
                if rnd == 1:
                    sp.wait_ge(rev_full, REVS)
                for rin in range(2):
                    for rout in range(2):
                        for k in range(3):
                            dy = 2 * (k - 1) + rin - rout + 3
                            src = bass.AP(dw_rows.tensor, (rnd * CH2 * 7 + dy) * P,
                                          [[1, IMG], [7 * P, CH2], [1, IMG]])
                            sp.dma_start(TS[IMG * rin:IMG * (rin + 1), :, k, IMG * rout:IMG * (rout + 1)],
                                         src).then_inc(taps_in, 16)
            with sp.Fori(0, NU) as u:
                load_next(1, u)
            with sp.Fori(0, B - 2) as b:
                with sp.Fori(0, NU) as u:
                    store(b, u)
                    load_next(b + 2, u)
            for b in (B - 2, B - 1):
                with sp.Fori(0, NU) as u:
                    store(b, u)
            for h in range(HALVES):
                sp.wait_ge(y_out[h], 16 * (B * NU + OUT_CR))

        @block.gpsimd
        def _(pool):
            g = nc.gpsimd
            g.memset(ID[:, :], 0.0).then_inc(set_pool, 1)
            g.memset(GM[:, :], 1.0 / 8).then_inc(set_pool, 1)
            pool.wait_ge(set_pool, 2)
            g.affine_select(out=ID[:, :], in_=ID[:, :], compare_op=ALU.not_equal, fill=1.0, base=0,
                            pattern=[[-1, P]], channel_multiplier=1).then_inc(set_pool, 1)
            gv = GM[:, :].rearrange("p (g e) -> p g e", e=8)
            g.affine_select(out=gv, in_=gv, compare_op=ALU.is_ge, fill=0.0, base=0,
                            pattern=[[-8, P // 8], [0, 8]], channel_multiplier=1).then_inc(set_pool, 1)
            pool.wait_ge(set_pool, 4)
            g.affine_select(out=gv, in_=gv, compare_op=ALU.is_ge, fill=0.0, base=7,
                            pattern=[[8, P // 8], [0, 8]], channel_multiplier=-1).then_inc(set_pool, 1)
            g.memset(REV, 0.0).then_inc(set_pool, 1)
            for k in (IMG - 1, 3 * IMG - 1):
                pool.wait_ge(set_pool, 6 + k // IMG // 2)
                g.affine_select(out=REV, in_=REV, compare_op=ALU.not_equal, fill=1.0, base=-k,
                                pattern=[[1, P]], channel_multiplier=1).then_inc(set_pool, 1)
            pool.wait_ge(set_dve, 1)
            g.partition_all_reduce(SCAL[:, 0:4], S6[:, 0:4], P, RMAX).then_inc(set_pool, 1)
            pool.sem_inc(l_rdy, L_CR)
            pool.wait_ge(ready, 1)

            def low(n, dst, hi, src):
                pool.wait_ge(xn_rdy, n + 1)
                pool.wait_ge(h_rdy, n + 1)
                carry(pool)
                g.tensor_tensor(dst, src, hi, ALU.subtract).then_inc(l_rdy, 1)

            def conv_inputs(c, first):
                if not first:
                    pool.wait_ge(cube_used, (c - 1) * 2 * PAIRS + PAIRS + USED_CR)
                    carry(pool)
                for h in range(HALVES):
                    for s in range(NS):
                        i = h * NS + s
                        gi = c * HALVES * NS + i
                        if not first or i >= 2:
                            pool.wait_ge(conv_full, 2 * gi - 2)
                            carry(pool)
                        buf = S[:, i % 2, :, :, :]
                        for e in (0, SCOLS - 1):
                            g.memset(buf[:, :, :, e:e + 1], 0.0).then_inc(border, 1)
                        if s in (0, NS - 1):
                            edge = 0 if s == 0 else SROWS - 1
                            g.memset(buf[:, :, edge, 1:SCOLS - 1], 0.0).then_inc(border, 1)
                        else:
                            pool.sem_inc(border, 1)
                        for p in range(2):
                            lo, hi, _ = strip_rows(s, p)
                            low(c * 2 * NPARTS + 2 * i + p, buf[:, 1, lo:hi, 1:SCOLS - 1],
                                buf[:, 0, lo:hi, 1:SCOLS - 1],
                                XN[:, p, 0:(hi - lo) * IMG].rearrange("p (r c) -> p r c", c=IMG))

            def attn_inputs(c, u, first):
                for h in range(HALVES):
                    if not first:
                        pool.wait_ge(tr_rdy, ((c - 1) * NU + u + 1) * HALVES)
                        pool.wait_ge(f_full, (c - 1) * 2 * PAIRS + PAIRS + 2 * (u + 1))
                    low(c * 2 * NPARTS + NPARTS + HALVES * u + h, XHL[:, 1, h, bass.ds(u * UNIT, UNIT)],
                        XHL[:, 0, h, bass.ds(u * UNIT, UNIT)], XN[:, h, 0:UNIT])

            def residual(b, u):
                for h in range(HALVES):
                    pool.wait_ge(y_rdy, (b * NU + u) * HALVES + h + Y_CR)
                    carry(pool)
                    g.tensor_tensor(TR[:, :], XHL[:, 0, h, bass.ds(u * UNIT, UNIT)],
                                    XHL[:, 1, h, bass.ds(u * UNIT, UNIT)], ALU.add).then_inc(tr_rdy, 1)

            def batch(b, last):
                pool.wait_ge(attn_full, b * NT + AT_CR)
                carry(pool)
                g.memset(VT[:, :, :, :, P:P + 1], 1.0).then_inc(ones_rdy, 1)
                if not last:
                    conv_inputs(b + 1, False)
                    with pool.Fori(0, NU) as u:
                        residual(b, u)
                        attn_inputs(b + 1, u, False)
                else:
                    with pool.Fori(0, NU) as u:
                        residual(b, u)

            conv_inputs(0, True)
            with pool.Fori(0, NU) as u:
                attn_inputs(0, u, True)
            with pool.Fori(0, B - 1) as b:
                batch(b, False)
            batch(B - 1, True)

        @block.vector
        def _(dve):
            v = nc.vector
            steps = [0, 0]

            def setup(ins):
                steps[0] += 1
                ins.then_inc(chain, 1)
                dve.wait_ge(chain, steps[0])

            for t in (ONES, BQ, KVS, BD, HID):
                setup(v.memset(t[:], XS if t is ONES else 0.0))
            setup(v.memset(CK[:, :], HALF_PI))
            for t in range(TAPS):
                setup(v.memset(XX[:, 0, t:t + 1], float(t % 3 - 1)))
                setup(v.memset(XX[:, 1, t:t + 1], float(t // 3 - 1)))
            for s, n in ((x1_rdy, X1_CR), (f_max, MAX_CR), (f_cube, CUBE_CR), (v_lo, VLO_CR), (o_rdy, O_CR),
                         (ol_rdy, OL_CR), (cube_used, USED_CR),
                         (y_rdy, Y_CR), (attn_full, AT_CR)):
                dve.sem_inc(s, n)
            dve.wait_ge(w_in, 16 * N_W)
            setup(v.tensor_scalar(W_A, sc32, -1.0, None, ALU.mult))
            setup(v.tensor_tensor(W_A, W_A, sc32, ALU.min))
            dve.sem_inc(soft_rdy, 1)
            dve.wait_ge(set_act, 1)
            v.tensor_scalar(W_D, W_C, 1.0, None, ALU.add).then_inc(soft_rdy, 1)
            dve.wait_ge(soft_rdy, 2)
            setup(v.tensor_scalar(W_B, W_D, -1.0, None, ALU.add))
            setup(v.tensor_scalar(W_F, W_B, 0.0, None, ALU.is_equal))
            setup(v.tensor_tensor(W_B, W_B, W_F, ALU.add))
            setup(v.reciprocal(W_B, W_B))
            setup(v.tensor_tensor(W_B, W_B, W_C, ALU.mult))
            dve.wait_ge(set_act, 2)
            setup(v.tensor_tensor(W_B, W_B, W_E, ALU.mult))
            setup(v.tensor_tensor(W_F, W_F, W_C, ALU.mult))
            setup(v.tensor_tensor(W_B, W_B, W_F, ALU.add))
            setup(v.tensor_scalar(W_A, sc32, 0.0, None, ALU.max))
            setup(v.tensor_tensor(W_B, W_B, W_A, ALU.add))
            setup(v.reciprocal(W_B, W_B))
            for h in range(HALVES):
                for j in range(2):
                    cs = slice(j * C, (j + 1) * C)
                    setup(v.tensor_tensor(wq32[:, h, cs], wq32[:, h, cs], W_B, ALU.mult))
            for j in range(2):
                cs = slice(j * C, (j + 1) * C)
                setup(v.scalar_tensor_tensor(bq32[:, cs], bq32[:, cs], FOCUS_EPS, W_B, ALU.add, ALU.mult))
            for dst, src in ((S6[:, 0:1], wq32), (S6[:, 1:2], wq32[:, :, 2 * C:3 * C]), (S6[:, 3:4], wp32)):
                setup(v.tensor_reduce(dst, src, AX.XY, ALU.max, apply_absolute_value=True))
            setup(v.tensor_reduce(S6[:, 2:3], KB[:, :, :, :].rearrange("p h t o -> p (h t o)"), AX.X, ALU.max,
                                  apply_absolute_value=True))
            setup(v.tensor_reduce(m_b, bq32, AX.X, ALU.max, apply_absolute_value=True))
            setup(v.tensor_reduce(m_bv, bq32[:, 2 * C:3 * C], AX.X, ALU.max, apply_absolute_value=True))
            setup(v.tensor_reduce(m_db, DWB[:, :], AX.X, ALU.max, apply_absolute_value=True))
            setup(v.tensor_reduce(m_t, dt32, AX.X, ALU.max, apply_absolute_value=True))
            setup(v.tensor_reduce(dsum, dt32.rearrange("p (c t) -> p c t", c=HD), AX.X, ALU.add,
                                  apply_absolute_value=True))
            setup(v.tensor_reduce(s_t, dsum, AX.X, ALU.max))
            dve.sem_inc(set_dve, 1)
            dve.wait_ge(set_pool, 9)

            def over(dst, src, top):
                setup(v.tensor_scalar(dst, src, TINY, None, ALU.max))
                setup(v.reciprocal(dst, dst))
                if top != 1.0:
                    setup(v.tensor_scalar(dst, dst, top, None, ALU.mult))

            setup(v.tensor_tensor(m_w, m_w, m_b, ALU.max))
            over(a_w, m_w, 16384.0)
            setup(v.tensor_scalar(inv_a, a_w, XS, None, ALU.mult))
            setup(v.tensor_scalar(den_eps, inv_a, FOCUS_EPS, None, ALU.mult))
            setup(v.tensor_tensor(den_eps, den_eps, den_eps, ALU.mult))
            setup(v.reciprocal(inv_a, inv_a))
            setup(v.tensor_tensor(inv_a2, inv_a, inv_a, ALU.mult))
            setup(v.tensor_scalar(v_bound, m_v, 16600.0, m_bv, ALU.mult, ALU.add))
            over(a_v, v_bound, 32768.0)
            setup(v.tensor_tensor(v_fac, inv_a, a_v, ALU.mult))
            over(a_t, m_t, 16384.0)
            setup(v.tensor_tensor(fm_fac, a_v, a_t, ALU.mult))
            setup(v.reciprocal(fm_fac, fm_fac))
            setup(v.tensor_scalar(spare, s_t, 1.0, None, ALU.add))
            setup(v.tensor_scalar(spare, spare, v_bound, m_db, ALU.mult, ALU.add))
            over(a_o, spare, 32768.0)
            over(a_p, m_p, 16384.0)
            setup(v.tensor_tensor(out_fac, a_o, a_p, ALU.mult))
            setup(v.reciprocal(out_fac, out_fac))
            over(a_r, m_k, 4096.0)
            setup(v.tensor_scalar(conv_fac, a_r, XS, None, ALU.mult))
            setup(v.reciprocal(conv_fac, conv_fac))
            setup(v.tensor_scalar(spare, a_w, XS * FOCUS_EPS, None, ALU.mult))
            setup(v.tensor_scalar(FL[:, :], W_B, spare, None, ALU.mult))
            setup(v.tensor_scalar(KB[:, :, :, :], KB[:, :, :, :], a_r, None, ALU.mult))
            for src, hi, lo, a in ((wq32, WQ[:, 0], WQ[:, 1], a_w), (wp32, WP[:, 0], WP[:, 1], a_p),
                                   (bq32, bh16, bl16, a_w)):
                setup(v.tensor_scalar(src, src, a, None, ALU.mult))
                setup(v.tensor_copy(hi, src))
                setup(v.tensor_tensor(lo, src, hi, ALU.subtract))
            setup(v.tensor_copy(BQ[0:1, :], bh16[0:1, :]))
            setup(v.tensor_copy(BQ[32:33, :], bl16[32:33, :]))
            dve.sem_inc(ready, 1)
            for i in range(2 * REVS):
                dve.wait_ge(tp_act, i + 1)
                hi, lo = (TPM[:, 4 * i:4 * i + 4, j, :] for j in range(2))
                v.scalar_tensor_tensor(lo, F[i % 2][:, :].rearrange("p (m n) -> p m n", m=4), a_t, hi, ALU.mult,
                                       ALU.subtract).then_inc(tp_dve, 1)
            base = steps[0]

            def link(c, ins):
                steps[1] += 1
                ins.then_inc(chain, 1)
                dve.wait_ge(chain, c * N_CHAIN + base + steps[1])

            def statistics(c, layer):
                n = 2 * c + layer
                dve.wait_ge(stats_rdy, (n + 1) * HALVES * NU)
                carry(dve)
                steps[1] += 1
                v.bn_aggr(MV[:, 0, :], ST[:, 0, :, :].rearrange("p u s -> p (u s)")).then_inc(chain, 1)
                link(c, v.bn_aggr(MV[:, 1, :], ST[:, 1, :, :].rearrange("p u s -> p (u s)")))
                v.tensor_copy(DEV, MV[:, :, 0]).then_inc(mean_rdy, 1)
                dve.wait_ge(mean_mm, n + 1)
                link(c, v.tensor_copy(MEAN, SM[:, 0:2]))
                link(c, v.tensor_tensor(DEV, DEV, MEAN, ALU.subtract))
                link(c, v.tensor_tensor(SPREAD, DEV, DEV, ALU.mult))
                v.tensor_tensor(SPREAD, SPREAD, MV[:, :, 1], ALU.add).then_inc(spread_rdy, 1)
                dve.wait_ge(spread_mm, n + 1)
                v.tensor_scalar(VAR, SM[:, 2:4], GN_EPS, None, ALU.add).then_inc(var_rdy, 1)
                dve.wait_ge(root_rdy, n + 1)
                link(c, v.reciprocal(STD, ROOT))
                link(c, v.tensor_tensor(STD, STD, VAR, ALU.mult))
                link(c, v.tensor_tensor(STD, STD, ROOT, ALU.add))
                link(c, v.tensor_scalar(STD, STD, 0.5, None, ALU.mult))
                link(c, v.reciprocal(RSTD, STD))
                sc, bi = (SC0, BI0) if layer == 0 else (SC1, BI1)
                link(c, v.tensor_scalar(sc, RSTD, XS, None, ALU.mult))
                if layer == 1:
                    link(c, v.tensor_scalar(STDN, STD, 1.0 / XS, None, ALU.mult))
                    link(c, v.tensor_tensor(CBN, MEAN, BP[:, :], ALU.add))
                v.scalar_tensor_tensor(bi, MEAN, -1.0, sc, ALU.mult, ALU.mult).then_inc(norm_rdy, 1)

            def rotation(c):
                v.tensor_tensor(POOLED, DEV, RSTD, ALU.mult).then_inc(pooled_rdy, 1)
                dve.wait_ge(hid_mm, c + 1)
                link(c, v.tensor_tensor(HID[:, 2:3], SM[:, 4:5], B1[:, :], ALU.add))
                for k in range(2):
                    r = slice(64 * k, 64 * k + 64)
                    v.tensor_scalar(HID[r, k:k + 1], HID[r, 2:3], 0.0, None, ALU.max).then_inc(hid_rdy, 1)
                dve.wait_ge(z_mm, c + 1)
                v.tensor_tensor(ZB[:, 0:2, :], SM[:, 8:12].rearrange("p (h k) -> p k h", k=2), B2[:, :, :],
                                ALU.add).then_inc(zb_rdy, 1)
                dve.wait_ge(trig_rdy, 2 * (c + 1))
                link(c, v.tensor_scalar(MODA, ZB[:, 3, :], conv_fac, None, ALU.mult))
                link(c, v.tensor_scalar(SIN[:, 2, :], SIN[:, 0, :], -1.0, None, ALU.mult))
                for k in range(2):
                    for h in range(HALVES):
                        link(c, v.tensor_scalar(TT[:, k, h, :], XX[:, k, :], SIN[:, 1, h:h + 1], None, ALU.mult))
                for k in range(2):
                    for h in range(HALVES):
                        s = SIN[:, 0, h:h + 1] if k == 0 else SIN[:, 2, h:h + 1]
                        link(c, v.scalar_tensor_tensor(TT[:, k, h, :], XX[:, 1 - k, :], s, TT[:, k, h, :],
                                                       ALU.mult, ALU.add))
                tt = TT[:, :, :, :].rearrange("p k h t -> p k (h t)")
                link(c, v.tensor_scalar(TW[:, 0], tt, -1.0, 0.0, ALU.mult, ALU.max))
                link(c, v.tensor_scalar(TW[:, 2], tt, 0.0, None, ALU.max))
                link(c, v.tensor_tensor(TW[:, 1], TW[:, 0], TW[:, 2], ALU.add))
                link(c, v.tensor_scalar(TW[:, 1], TW[:, 1], -1.0, 1.0, ALU.mult, ALU.add))
                for jy in range(3):
                    wy = TW[:, jy, 1, :].unsqueeze(1).broadcast_to([P, 3, HALVES * TAPS])
                    link(c, v.tensor_tensor(COEF[:, 3 * jy:3 * jy + 3, :], wy, TW[:, :, 0, :], ALU.mult))
                for j in range(TAPS):
                    cj = COEF[:, j, :].rearrange("p (h t) -> p h t", h=HALVES).unsqueeze(3).broadcast_to(
                        [P, HALVES, TAPS, HD])
                    kj = KB[:, :, j, :].unsqueeze(2).broadcast_to([P, HALVES, TAPS, HD])
                    link(c, v.tensor_tensor(ROT if j == 0 else RTMP, cj, kj, ALU.mult))
                    if j:
                        link(c, v.tensor_tensor(ROT, ROT, RTMP, ALU.add))
                dve.sem_inc(rot_rdy, 1)
                dve.wait_ge(bd_hi, 4 * (c + 1))
                for q in range(4):
                    r = slice(32 * q, 32 * q + 32)
                    v.tensor_tensor(BD[r, 1, :, :, r], ROT[r], BD[r, 0, :, :, r], ALU.subtract).then_inc(bd_lo, 1)

            def x_stats(c, u):
                for h in range(HALVES):
                    v.bn_stats(ST[:, h, bass.ds(u, 1), :].rearrange("p u s -> p (u s)"),
                               X[:, h, bass.ds(u * UNIT, UNIT)]).then_inc(stats_rdy, 1)

            def conv_steps(c, first):
                if not first:
                    dve.wait_ge(cube_used, (c - 1) * 2 * PAIRS + PAIRS + USED_CR)

                def high(i):
                    s = i % NS
                    if not first or i >= 2:
                        dve.wait_ge(conv_full, 2 * (c * HALVES * NS + i) - 2)
                    for p in range(2):
                        n = c * 2 * NPARTS + 2 * i + p
                        lo, hi, _ = strip_rows(s, p)
                        dve.wait_ge(xn_rdy, n + 1)
                        v.tensor_copy(S[:, i % 2, 0, lo:hi, 1:SCOLS - 1],
                                      XN[:, p, 0:(hi - lo) * IMG].rearrange("p (r c) -> p r c", c=IMG)
                                      ).then_inc(h_rdy, 1)

                def evacuate(i):
                    h, s = divmod(i, NS)
                    for q in range(2):
                        n = c * CHUNKS + 2 * i + q
                        tok = slice((2 * s + q) * UNIT, (2 * s + q + 1) * UNIT)
                        dve.wait_ge(conv_full, n + 1)
                        v.scalar_tensor_tensor(X[:, h, tok], VA[q][:, :], MODA[:, h:h + 1], X[:, h, tok],
                                               ALU.mult, ALU.add).then_inc(x1_rdy, 1)
                        dve.wait_ge(x1_rdy, n + 1 + X1_CR)
                        v.bn_stats(ST[:, h, 2 * s + q, :], X[:, h, tok]).then_inc(stats_rdy, 1)

                high(0)
                for i in range(1, HALVES * NS):
                    high(i)
                    evacuate(i - 1)
                evacuate(HALVES * NS - 1)

            def attn_inputs(c, u, first):
                for h in range(HALVES):
                    n = c * 2 * NPARTS + NPARTS + HALVES * u + h
                    if not first:
                        dve.wait_ge(tr_rdy, ((c - 1) * NU + u + 1) * HALVES)
                        dve.wait_ge(f_full, (c - 1) * 2 * PAIRS + PAIRS + 2 * (u + 1))
                    dve.wait_ge(xn_rdy, n + 1)
                    v.tensor_copy(XHL[:, 0, h, bass.ds(u * UNIT, UNIT)], XN[:, h, 0:UNIT]).then_inc(h_rdy, 1)

            def floor_max(n, p):
                dve.wait_ge(f_full, n + 1)
                fl = FL[:, :].unsqueeze(1).broadcast_to([P, 2, C])
                v.tensor_tensor(K0[:, p, :].rearrange("p (t n) -> p t n", t=2),
                                F[p][:, :].rearrange("p (t n) -> p t n", t=2), fl, ALU.max).then_inc(f_max, 1)

            def cube(n, p):
                dve.wait_ge(f_sq, 2 * (n + 1))
                dve.wait_ge(cube_used, n + 1)
                dve.wait_ge(f_six, 2 * n + 2)
                v.tensor_tensor(K3[:, p, :], K2[:, p, :], K0[:, p, :], ALU.mult).then_inc(f_cube, 1)

            def ratio(g, a, b):
                dve.wait_ge(f_six, 4 * (g + 1) + SIX_CR)
                v.reciprocal(RATIO[:, 1, :], b[:, :]).then_inc(f_ratio, 1)
                dve.wait_ge(f_ratio, 2 * g + 1)
                v.tensor_tensor(RATIO[:, 0, :], a[:, :], RATIO[:, 1, :], ALU.mult).then_inc(f_ratio, 1)

            def phase_kv(b, u):
                n0 = b * 2 * PAIRS + 2 * u
                m0 = b * PAIRS + 2 * u
                for p in range(2):
                    floor_max(n0 + p, p)
                for p in range(2):
                    cube(n0 + p, p)
                for p in range(2):
                    dve.wait_ge(v_hi, m0 + p + 1)
                    dve.wait_ge(v_true, m0 + p + 1)
                    for t in range(2):
                        dst = bass.ds((u * TPU + 2 * p + t) * HEADS, HEADS)
                        last = v.scalar_tensor_tensor(
                            V[:, :, 1, dst], VA[p][:, t * C:(t + 1) * C].rearrange("p (c h) -> p c h", c=HD), v_fac,
                            V[:, :, 0, dst], ALU.mult, ALU.subtract)
                    last.then_inc(v_lo, 1)
                ratio(b * 2 * NU + u, S2, S6)
                dve.wait_ge(f_root, b * 2 * NU + u + 1)
                for p in range(2):
                    for t in range(2):
                        ks = K3[:, p, t * C:(t + 1) * C]
                        last = v.tensor_scalar(ks, ks, NORM[:, 2 * p + t:2 * p + t + 1], None, ALU.mult)
                        last.then_inc(k_scaled, 1)

            def keep(b):
                dve.wait_ge(y_rdy, b * NU * HALVES + Y_CR)
                v.tensor_copy(PR[:, 7:9, :], PR[:, 5:7, :]).then_inc(kept, 1)

            def state(b):
                dve.wait_ge(state_full, b + 1)
                for h in range(HALVES):
                    o_v, o_d = (HPH, 0) if h == 0 else (0, P)
                    for q in range(HPH):
                        r = slice(32 * q, 32 * q + 32)
                        v.tensor_copy(KVS[r, h, o_v + q:o_v + P:HPH], T[h][r, q:P:HPH]).then_inc(state_rdy, 1)
                        v.tensor_copy(KVS[r, h, o_d + q:o_d + q + 1], T[h][r, P:P + 1]).then_inc(state_rdy, 1)

            def attend(b, u, t):
                i = b * NT + u * TPU + t
                p, a = t // 2, VA[t % 2]
                dve.wait_ge(attn_full, i + 1 + AT_CR)
                if t == 0:
                    dve.wait_ge(f_root, b * 2 * NU + NU + u + 1)
                zt = Z[:, t % 2, :]
                zh = zt.rearrange("p (h f) -> p h f", h=HALVES)
                av = a[:, :]
                den = bass.AP(av.tensor, av.offset, [list(av.ap[0]), [KVC + P, HALVES], [1, HPH]])
                v.tensor_scalar(zh, den, NORM[:, t:t + 1], None, ALU.add).then_inc(z_rdy, 1)
                dve.wait_ge(z_rdy, 3 * i + 1)
                v.reciprocal(zt, zt).then_inc(z_rdy, 1)
                dve.wait_ge(z_rdy, 3 * i + 2)
                o = O[:, p, (t % 2) * C:(t % 2 + 1) * C]
                v.tensor_tensor(o.rearrange("p (c h f) -> p h c f", c=HD, h=HALVES),
                                a[:, HPH:HPH + C].rearrange("p (h c f) -> p h c f", h=HALVES, c=HD),
                                zh.unsqueeze(2).broadcast_to([P, HALVES, HD, HPH]), ALU.mult).then_inc(z_rdy, 1)
                dve.wait_ge(z_rdy, 3 * i + 3)
                oc = o.rearrange("p (c e) -> p c e", c=HD)
                v.tensor_tensor(oc, oc, FM[:, :, bass.ds((u * TPU + t) * HEADS, HEADS)], ALU.add).then_inc(o_rdy, 1)

            def finish(b, u, h):
                e = (b * NU + u) * HALVES + h
                dve.wait_ge(y_act, e + 1 + YA_CR)
                dve.wait_ge(tr_rdy, e + 1)
                v.scalar_tensor_tensor(Y[:, h, :], TR[:, :], STDC[:, h:h + 1], Y[:, h, :], ALU.mult,
                                       ALU.add).then_inc(y_rdy, 1)

            def low_out(b, u, p):
                m = b * PAIRS + 2 * u + p
                dve.wait_ge(oh_rdy, m + 1)
                hi, lo = (OT[:, i, :, 2 * P * p:2 * P * (p + 1)] for i in range(2))
                v.scalar_tensor_tensor(lo, T[p][:, :].rearrange("p (h n) -> p h n", h=HALVES), a_o, hi, ALU.mult,
                                       ALU.subtract).then_inc(ol_rdy, 1)

            def phase_q(b, u, q, att, fin, nxt):
                n0 = b * 2 * PAIRS + PAIRS + 2 * u
                for p in range(2):
                    if q:
                        floor_max(n0 + p, p)
                    if fin and p == 0:
                        finish(b, u - 2, 0)
                    if att:
                        attend(b, u - 1, 2 * p)
                        attend(b, u - 1, 2 * p + 1)
                    if q:
                        cube(n0 + p, p)
                if fin:
                    finish(b, u - 2, 1)
                if att:
                    for p in range(2):
                        low_out(b, u - 1, p)
                if q:
                    ratio(b * 2 * NU + NU + u, S6, S2)
                if nxt:
                    attn_inputs(b + 1, u - 2, False)

            def batch(b, last):
                keep(b)
                with dve.Fori(0, NU // 2) as u:
                    phase_kv(b, u)
                if not last:
                    dve.wait_ge(x_in, 16 * NU * (b + 2))
                    carry(dve)
                with dve.Fori(NU // 2, NU) as u:
                    phase_kv(b, u)
                    if not last:
                        x_stats(b + 1, 2 * (u - NU // 2))
                        x_stats(b + 1, 2 * (u - NU // 2) + 1)
                state(b)
                if not last:
                    dve.wait_ge(l_rdy, (b + 1) * 2 * NPARTS + L_CR)
                    steps[1] = 0
                    statistics(b + 1, 0)
                    rotation(b + 1)
                    conv_steps(b + 1, False)
                for u in range(2):
                    if u == 1:
                        dve.wait_ge(fm_rdy, HD * (b + 1) + FM_CR)
                    phase_q(b, u, True, u > 0, False, False)
                    if u == 0 and not last:
                        statistics(b + 1, 1)
                        assert steps[1] == N_CHAIN, steps
                with dve.Fori(2, NU) as u:
                    phase_q(b, u, True, True, True, not last)
                phase_q(b, NU, False, True, True, not last)
                phase_q(b, NU + 1, False, False, True, not last)

            dve.wait_ge(x_in, 16 * NU)
            with dve.Fori(0, NU) as u:
                x_stats(0, u)
            steps[1] = 0
            statistics(0, 0)
            rotation(0)
            conv_steps(0, True)
            statistics(0, 1)
            assert steps[1] == N_CHAIN, steps
            with dve.Fori(0, NU) as u:
                attn_inputs(0, u, True)
            with dve.Fori(0, B - 1) as b:
                batch(b, False)
            batch(B - 1, True)

        @block.scalar
        def _(act):
            a = nc.scalar
            act.wait_ge(soft_rdy, 1)
            a.activation(W_C, W_A, ACT.Exp).then_inc(set_act, 1)
            act.wait_ge(soft_rdy, 2)
            a.activation(W_E, W_D, ACT.Ln).then_inc(set_act, 1)
            act.wait_ge(ready, 1)
            for s, n in ((f_six, SIX_CR), (fm_rdy, FM_CR), (y_act, YA_CR)):
                act.sem_inc(s, n)
            for i in range(2 * REVS):
                act.wait_ge(rev_full, i + 1)
                a.activation(TPM[:, 4 * i:4 * i + 4, 0, :], F[i % 2][:, :].rearrange("p (m n) -> p m n", m=4),
                             ACT.Copy, scale=a_t).then_inc(tp_act, 1)

            def root(n):
                act.wait_ge(var_rdy, n + 1)
                a.activation(ROOT, VAR, ACT.Sqrt).then_inc(root_rdy, 1)

            def squash(c):
                act.wait_ge(zb_rdy, c + 1)
                a.activation(ZB[:, 2, :], ZB[:, 0, :], ACT.Tanh).then_inc(squash_rdy, 1)
                a.activation(ZB[:, 3, :], ZB[:, 1, :], ACT.Sigmoid)
                act.wait_ge(squash_rdy, c + 1)
                a.activation(SIN[:, 0, :], ZB[:, 2, :], ACT.Sin, scale=QUARTER_PI).then_inc(trig_rdy, 1)
                a.activation(SIN[:, 1, :], ZB[:, 2, :], ACT.Sin, scale=QUARTER_PI, bias=CK[:, 0:1]
                             ).then_inc(trig_rdy, 1)

            def kernels(c):
                act.wait_ge(rot_rdy, c + 1)
                for q in range(4):
                    r = slice(32 * q, 32 * q + 32)
                    a.copy(BD[r, 0, :, :, r], ROT[r]).then_inc(bd_hi, 1)

            def conv_inputs(c):
                act.wait_ge(norm_rdy, 2 * c + 1)
                act.wait_ge(bd_lo, 4 * (c + 1))
                for h in range(HALVES):
                    for s in range(NS):
                        for p in range(2):
                            n = c * 2 * NPARTS + 2 * (h * NS + s) + p
                            lo, hi, row = strip_rows(s, p)
                            act.wait_ge(l_rdy, n + 1)
                            a.activation(XN[:, p, 0:(hi - lo) * IMG],
                                         X[:, h, row * IMG:(row + hi - lo) * IMG], ACT.Identity,
                                         scale=SC0[:, h:h + 1], bias=BI0[:, h:h + 1]).then_inc(xn_rdy, 1)

            def attn_inputs(c, u):
                for h in range(HALVES):
                    n = c * 2 * NPARTS + NPARTS + HALVES * u + h
                    act.wait_ge(l_rdy, n + 1)
                    a.activation(XN[:, h, 0:UNIT], X[:, h, bass.ds(u * UNIT, UNIT)], ACT.Identity,
                                 scale=SC1[:, h:h + 1], bias=BI1[:, h:h + 1]).then_inc(xn_rdy, 1)

            def squares(n, p):
                act.wait_ge(f_max, n + 1 + MAX_CR)
                act.wait_ge(f_cube, n + 1)
                act.wait_ge(f_six, 2 * n + 2)
                for t in range(2):
                    ts = slice(t * C, (t + 1) * C)
                    a.activation(K2[:, p, ts], K0[:, p, ts], ACT.Square, scale=inv_a,
                                 accum_out=S2[:, 2 * p + t:2 * p + t + 1]).then_inc(f_sq, 1)

            def sixths(n, p):
                act.wait_ge(f_cube, n + 1 + CUBE_CR)
                for t in range(2):
                    a.activation(K2[:, p, t * C:(t + 1) * C], K3[:, p, t * C:(t + 1) * C], ACT.Square, scale=inv_a,
                                 accum_out=S6[:, 2 * p + t:2 * p + t + 1]).then_inc(f_six, 1)

            def norms(g, factor):
                act.wait_ge(f_ratio, 2 * (g + 1))
                a.activation(NORM[:, :], RATIO[:, 0, :], ACT.Sqrt, scale=factor).then_inc(f_root, 1)

            def phase_kv(b, u):
                n0 = b * 2 * PAIRS + 2 * u
                m0 = b * PAIRS + 2 * u
                for p in range(2):
                    squares(n0 + p, p)
                    act.wait_ge(v_full, m0 + p + 1)
                    for t in range(2):
                        last = a.activation(V[:, :, 0, bass.ds((u * TPU + 2 * p + t) * HEADS, HEADS)],
                                            VA[p][:, t * C:(t + 1) * C].rearrange("p (c h) -> p c h", c=HD),
                                            ACT.Copy, scale=v_fac)
                    last.then_inc(v_hi, 1)
                for p in range(2):
                    act.wait_ge(cube_used, n0 + p + 1)
                    for t in range(2):
                        last = a.activation(
                            VT[:, p, t, :, 0:P].rearrange("p h (c f) -> p h c f", c=HD),
                            VA[p][:, t * C:(t + 1) * C].rearrange("p (c h f) -> p h c f", c=HD, h=HALVES),
                            ACT.Copy, scale=inv_a)
                    last.then_inc(v_true, 1)
                for p in range(2):
                    sixths(n0 + p, p)
                norms(b * 2 * NU + u, inv_a2)

            def depthwise(b, c):
                n = b * HD + c
                for q in range(2):
                    act.wait_ge(dw_full, n + q + 1)
                    a.activation(FM[:, bass.ds(c + q, 1), :].rearrange("p c n -> p (c n)"), F[q][:, 0:NT * HEADS],
                                 ACT.Identity, scale=fm_fac, bias=DWB[:, bass.ds(c + q, 1)]).then_inc(fm_rdy, 1)

            def transposed_q(b, u, p):
                act.wait_ge(cube_used, b * 2 * PAIRS + PAIRS + 2 * u + p + 1 + USED_CR)
                a.copy(QT[:, p, :, :], T[p][:, :].rearrange("p (h n) -> p h n", h=HALVES)).then_inc(qt_rdy, 1)

            def output(b, u, h):
                e = (b * NU + u) * HALVES + h
                act.wait_ge(y_full, e + 1)
                act.wait_ge(y_out[h], 16 * (b * NU + u + OUT_CR))
                a.activation(Y[:, h, :], PP[:, :], ACT.Identity, scale=out_fac, bias=CBC[:, h:h + 1]
                             ).then_inc(y_act, 1)

            def high_out(b, u, p):
                act.wait_ge(ot_full, b * PAIRS + 2 * u + p + 1)
                a.activation(OT[:, 0, :, 2 * P * p:2 * P * (p + 1)],
                             T[p][:, :].rearrange("p (h n) -> p h n", h=HALVES), ACT.Copy, scale=a_o
                             ).then_inc(oh_rdy, 1)

            def phase_q(b, u, q, att, fin, nxt):
                n0 = b * 2 * PAIRS + PAIRS + 2 * u
                for p in range(2):
                    if att:
                        transposed_q(b, u - 1, p)
                    if q:
                        squares(n0 + p, p)
                    if fin:
                        output(b, u - 2, p)
                if att:
                    for p in range(2):
                        high_out(b, u - 1, p)
                if q:
                    for p in range(2):
                        sixths(n0 + p, p)
                    norms(b * 2 * NU + NU + u, den_eps)
                if nxt:
                    attn_inputs(b + 1, u - 2)

            def batch(b, last):
                with act.Fori(0, NU) as u:
                    phase_kv(b, u)
                for g in range(4):
                    with act.Fori(0, HD // 8) as i:
                        depthwise(b, g * (HD // 4) + 2 * i)
                    if not last and g == 1:
                        root(2 * (b + 1))
                    if not last and g == 3:
                        squash(b + 1)
                if not last:
                    kernels(b + 1)
                    conv_inputs(b + 1)
                act.wait_ge(kept, b + 1)
                for u in range(2):
                    phase_q(b, u, True, u > 0, False, False)
                    if u == 0 and not last:
                        root(2 * (b + 1) + 1)
                if not last:
                    act.wait_ge(norm_rdy, 2 * (b + 1) + 2)
                with act.Fori(2, NU) as u:
                    phase_q(b, u, True, True, True, not last)
                phase_q(b, NU, False, True, True, not last)
                phase_q(b, NU + 1, False, False, True, not last)

            root(0)
            squash(0)
            kernels(0)
            conv_inputs(0)
            root(1)
            act.wait_ge(norm_rdy, 2)
            with act.Fori(0, NU) as u:
                attn_inputs(0, u)
            with act.Fori(0, B - 1) as b:
                batch(b, False)
            batch(B - 1, True)

        @block.tensor
        def _(pe):
            t_ = nc.tensor

            def group_mean(c, layer):
                pe.wait_ge(mean_rdy, 2 * c + layer + 1)
                t_.matmul(SM[:, 0:2], GM[:, :], DEV, start=True, stop=True).then_inc(mean_mm, 1)

            def group_spread(c, layer):
                pe.wait_ge(spread_rdy, 2 * c + layer + 1)
                t_.matmul(SM[:, 2:4], GM[:, :], SPREAD, start=True, stop=True).then_inc(spread_mm, 1)

            def hidden(c):
                pe.wait_ge(pooled_rdy, c + 1)
                for h in range(HALVES):
                    last = t_.matmul(SM[:, 4:5], W1[:, h, :], POOLED[:, h:h + 1], start=(h == 0), stop=(h == 1))
                last.then_inc(hid_mm, 1)

            def heads(c):
                pe.wait_ge(hid_rdy, 2 * (c + 1))
                for h in range(HALVES):
                    o = 8 + 2 * h
                    last = t_.matmul(SM[:, o:o + 2], W2[:, h * P:(h + 1) * P], HID[:, 0:2], start=True, stop=True)
                last.then_inc(z_mm, 1)

            PASSES = ((0, 0), (0, 1), (1, 0))

            def convolution(c):
                with pe.Fori(0, HALVES) as h:
                    for s in range(NS):
                        i = h * NS + s
                        pe.wait_ge(h_rdy, c * 2 * NPARTS + 2 * i + 2)
                        pe.wait_ge(l_rdy, c * 2 * NPARTS + 2 * i + 2 + L_CR)
                        pe.wait_ge(border, 3 * (c * HALVES * NS + i + 1))
                        for q in range(2):
                            pe.wait_ge(x1_rdy, c * CHUNKS + 2 * i + q + 1)
                            k = 0
                            for wa, xa in PASSES:
                                for t in range(TAPS):
                                    y0 = 8 * q + t // 3
                                    last = t_.matmul(VA[q][:, :], BD[:, wa, bass.ds(h, 1), t, :].rearrange(
                                        "p h o -> p (h o)"), S[:, s % 2, xa, y0:y0 + 8, t % 3:t % 3 + IMG],
                                        start=(k == 0), stop=(k == 3 * TAPS - 1))
                                    k += 1
                            last.then_inc(conv_full, 1)

            def project(b, u, p, banks):
                for t in range(2):
                    at = bass.ds(u * UNIT + (2 * p + t) * P, P)
                    for k, (h, xa) in enumerate(((0, 0), (1, 0), (0, 1), (1, 1))):
                        for bank, c0 in banks:
                            for wa in (0, 1) if xa == 0 else (0,):
                                t_.matmul(bank[p][:, t * C:(t + 1) * C], XHL[:, xa, h, at],
                                          WQ[:, wa, h, c0:c0 + C], start=(k == 0 and wa == 0), stop=False)
                    for bank, c0 in banks:
                        last = t_.matmul(bank[p][:, t * C:(t + 1) * C], ONES[:, :], BQ[:, c0:c0 + C],
                                         start=False, stop=True)
                        if t == 1:
                            last.then_inc(f_full if bank is F else v_full, 1)

            def accumulate_state(b, u):
                for p in range(2):
                    m = b * PAIRS + 2 * u + p
                    pe.wait_ge(k_scaled, 2 * (m + 1))
                    pe.wait_ge(v_true, m + 1)
                    for t in range(2):
                        for h in range(HALVES):
                            last = t_.matmul(T[h][:, 0:P + 1], K3[:, p, t * C + h * P:t * C + (h + 1) * P],
                                             VT[:, p, t, h, 0:P + 1], start=False, stop=False)
                    last.then_inc(cube_used, 1)

            def phase_kv(b, u, kv, acc):
                if kv:
                    for p in range(2):
                        pe.wait_ge(f_max, b * 2 * PAIRS + 2 * u + p + 1)
                        pe.wait_ge(v_lo, b * PAIRS + 2 * u + p + 1)
                        pe.wait_ge(h_rdy, b * 2 * NPARTS + NPARTS + HALVES * (u + 1))
                        pe.wait_ge(l_rdy, b * 2 * NPARTS + NPARTS + HALVES * (u + 1) + L_CR)
                        project(b, u, p, ((F, C), (VA, 2 * C)))
                if acc:
                    accumulate_state(b, u - 1)

            def depthwise(b, c):
                for q in range(2):
                    pe.wait_ge(fm_rdy, b * HD + c + q + 1)
                    k = 0
                    for d in (1, 0, 2):
                        lo, hi = max(0, 1 - d) * HEADS, (NT - max(0, d - 1)) * HEADS
                        for ta, va in PASSES:
                            sh = (d - 1) * HEADS
                            last = t_.matmul(F[q][:, lo:hi],
                                             TP[:, bass.ds(c + q, 1), d, ta, :].rearrange("p c n -> p (c n)"),
                                             V[:, bass.ds(c + q, 1), va, lo + sh:hi + sh].rearrange(
                                                 "p c n -> p (c n)"),
                                             start=(k == 0), stop=(k == 8))
                            k += 1
                    last.then_inc(dw_full, 1)

            def transpose_q(b, u, p):
                n = b * 2 * PAIRS + PAIRS + 2 * u + p
                pe.wait_ge(f_cube, n + 1 + CUBE_CR)
                pe.wait_ge(ol_rdy, b * PAIRS + 2 * u + p + 1)
                for h in range(HALVES):
                    for t in range(2):
                        last = t_.transpose(T[p][:, (2 * h + t) * P:(2 * h + t + 1) * P],
                                            K3[:, p, t * C + h * P:t * C + (h + 1) * P], ID[:, :])
                last.then_inc(cube_used, 1)

            def attention(b, u, p):
                pe.wait_ge(qt_rdy, b * PAIRS + 2 * u + p + 1)
                for t in range(2):
                    pe.wait_ge(o_rdy, b * NT + u * TPU + 2 * p + t + 1)
                    for h in range(HALVES):
                        last = t_.matmul(VA[t][:, h * KVC:(h + 1) * KVC], QT[:, p, h, t * P:(t + 1) * P],
                                         KVS[:, h, :], start=True, stop=True)
                    last.then_inc(attn_full, 1)

            def transpose_o(b, u, p):
                pe.wait_ge(o_rdy, b * NT + u * TPU + 2 * p + 2 + O_CR)
                for h in range(HALVES):
                    for t in range(2):
                        last = t_.transpose(T[p][:, (2 * h + t) * P:(2 * h + t + 1) * P],
                                            O[:, p, t * C + h * P:t * C + (h + 1) * P], ID[:, :])
                last.then_inc(ot_full, 1)

            def output(b, u, h):
                pe.wait_ge(ol_rdy, b * PAIRS + 2 * (u + 1) + OL_CR)
                pe.wait_ge(y_act, (b * NU + u) * HALVES + h + 1)
                k = 0
                for kk in range(HALVES):
                    for wa, xa in PASSES:
                        last = t_.matmul(PP[:, :], WP[:, wa, kk, h * P:(h + 1) * P], OT[:, xa, kk, :],
                                         start=(k == 0), stop=(k == 5))
                        k += 1
                last.then_inc(y_full, 1)

            def phase_q(b, u, q, att, fin):
                def queries(p):
                    if q:
                        pe.wait_ge(f_max, b * 2 * PAIRS + PAIRS + 2 * u + p + 1)
                        project(b, u, p, ((F, 0),))
                queries(0)
                if att:
                    transpose_q(b, u - 1, 0)
                if fin:
                    output(b, u - 2, 0)
                if att:
                    attention(b, u - 1, 0)
                    transpose_q(b, u - 1, 1)
                queries(1)
                if att:
                    attention(b, u - 1, 1)
                if fin:
                    output(b, u - 2, 1)
                if att:
                    transpose_o(b, u - 1, 0)
                    transpose_o(b, u - 1, 1)

            def batch(b, last):
                pe.wait_ge(ol_rdy, b * PAIRS + OL_CR)
                for h in range(HALVES):
                    t_.matmul(T[h][:, 0:P + 2], ONES[0:32, :], ZEROS, start=True, stop=False)
                phase_kv(b, 0, True, False)
                pe.wait_ge(ones_rdy, b + 1)
                carry(pe)
                with pe.Fori(1, NU) as u:
                    phase_kv(b, u, True, True)
                accumulate_state(b, NU - 1)
                for h in range(HALVES):
                    fin = t_.matmul(T[h][:, 0:P + 2], ONES[0:32, :], ZEROS, start=False, stop=True)
                fin.then_inc(state_full, 1)
                pe.wait_ge(v_lo, PAIRS * (b + 1) + VLO_CR)
                pe.wait_ge(f_max, b * 2 * PAIRS + PAIRS + MAX_CR)
                carry(pe)
                for g in range(4):
                    with pe.Fori(0, HD // 8) as i:
                        depthwise(b, g * (HD // 4) + 2 * i)
                    if not last:
                        (group_mean, group_spread, lambda c, _: hidden(c), lambda c, _: heads(c))[g](b + 1, 0)
                if not last:
                    pe.wait_ge(bd_lo, 4 * (b + 2))
                    carry(pe)
                    convolution(b + 1)
                    pe.wait_ge(x1_rdy, CHUNKS * (b + 2) + X1_CR)
                pe.wait_ge(fm_rdy, HD * (b + 1) + FM_CR)
                pe.wait_ge(state_rdy, 4 * HPH * (b + 1))
                for u in range(2):
                    phase_q(b, u, True, u > 0, False)
                    if u == 0 and not last:
                        group_mean(b + 1, 1)
                        group_spread(b + 1, 1)
                with pe.Fori(2, NU) as u:
                    phase_q(b, u, True, True, True)
                phase_q(b, NU, False, True, True)
                phase_q(b, NU + 1, False, False, True)

            pe.wait_ge(ready, 1)
            pe.wait_ge(set_pool, 8)
            tsm = XHL[:, :, :, :].rearrange("p a h n -> p (a h n)").bitcast(f32)
            for i in range(2 * REVS):
                pe.wait_ge(taps_in, 16 * 12 * (i // REVS + 1))
                if i >= 2:
                    pe.wait_ge(tp_dve, i - 1)
                j = i % REVS
                t_.matmul(F[i % 2][:, :], REV, tsm[:, 512 * j:512 * j + 512], start=True, stop=True
                          ).then_inc(rev_full, 1)
            group_mean(0, 0)
            group_spread(0, 0)
            hidden(0)
            heads(0)
            pe.wait_ge(bd_lo, 4)
            convolution(0)
            group_mean(0, 1)
            group_spread(0, 1)
            pe.wait_ge(tp_dve, 2 * REVS)
            with pe.Fori(0, B - 1) as b:
                batch(b, False)
            batch(B - 1, True)


def kernel(x, L0_conv_base_kernel, L0_conv_ap_w1, L0_conv_ap_b1, L0_conv_ap_w2, L0_conv_ap_b2, L0_conv_meta_w1,
           L0_conv_meta_b1, L0_conv_meta_w2, L0_conv_meta_b2, L1_conv_Wq, L1_conv_bq, L1_conv_Wkv, L1_conv_bkv,
           L1_conv_Wproj, L1_conv_bproj, L1_conv_dwc_w, L1_conv_dwc_b, L1_conv_scale_param):
    import numpy as np
    import concourse.bacc as bacc
    from concourse import mybir as mb
    from concourse.bass_utils import run_bass_kernel_spmd

    B, C, H, W = x.shape
    G, HD = L0_conv_base_kernel.shape[0:2]
    order = np.arange(C).reshape(G, HD).T.reshape(-1)
    wkv, bkv = np.asarray(L1_conv_Wkv), np.asarray(L1_conv_bkv)
    taps = np.asarray(L1_conv_dwc_w).reshape(HD, 5, 5)
    arrays = {
        "x": np.asarray(x).reshape(B, C, H * W),
        "conv_w": np.asarray(L0_conv_base_kernel).transpose(0, 2, 3, 4, 1).reshape(C, 9, HD),
        "mlp_w1": np.concatenate([np.asarray(L0_conv_ap_w1), np.asarray(L0_conv_meta_w1)], 0).T,
        "mlp_b1": np.concatenate([np.asarray(L0_conv_ap_b1), np.asarray(L0_conv_meta_b1)]).reshape(-1, 1),
        "mlp_w2": np.concatenate([np.repeat(np.asarray(L0_conv_ap_w2).T, HD, axis=1),
                                  np.asarray(L0_conv_meta_w2).T], 0),
        "mlp_b2": np.concatenate([np.repeat(np.asarray(L0_conv_ap_b2), HD), np.asarray(L0_conv_meta_b2)]
                                 ).reshape(4, C // 2).T,
        "wqkv": np.concatenate([np.asarray(L1_conv_Wq), wkv[:C], wkv[C:][order]], 0).T,
        "bqkv": np.concatenate([np.asarray(L1_conv_bq), bkv[:C], bkv[C:][order]]).reshape(1, -1),
        "head_scale": np.asarray(L1_conv_scale_param).reshape(1, C),
        "wproj": np.asarray(L1_conv_Wproj).T[order],
        "bproj": np.asarray(L1_conv_bproj).reshape(2, C // 2).T,
        "dw_rows": np.pad(taps[:, :, ::-1], ((0, 0), (1, 1), (61, 62))),
        "dw_taps": taps.reshape(1, -1),
        "dw_b": np.asarray(L1_conv_dwc_b).reshape(1, HD),
    }
    arrays = {n: np.ascontiguousarray(v) for n, v in arrays.items()}
    nc = bacc.Bacc("TRN2", target_bir_lowering=False, num_devices=1)
    args = [nc.dram_tensor(n, v.shape, mb.dt.from_np(v.dtype), kind="ExternalInput").ap() for n, v in arrays.items()]
    out = nc.dram_tensor("out", (B, C, H * W), mb.dt.float32, kind="ExternalOutput").ap()
    conv_then_focused_attention(nc, *args, out)
    r = run_bass_kernel_spmd(nc, [arrays], core_ids=[0])
    return r.results[0]["out"].reshape(B, C, H, W)
```

```python
import concourse.bass as bass
from concourse import mybir
from contextlib import ExitStack


def conv_then_focused_attention(
    nc: bass.Bass,
    x: bass.AP,
    conv_w: bass.AP,
    mlp_w1: bass.AP,
    mlp_b1: bass.AP,
    mlp_w2: bass.AP,
    mlp_b2: bass.AP,
    wqkv: bass.AP,
    bqkv: bass.AP,
    head_scale: bass.AP,
    wproj: bass.AP,
    bproj: bass.AP,
    dw_rows: bass.AP,
    dw_taps: bass.AP,
    dw_b: bass.AP,
    out: bass.AP,
):
    f32, f16, bf16 = mybir.dt.float32, mybir.dt.float16, mybir.dt.bfloat16
    ALU = mybir.AluOpType
    ACT = mybir.ActivationFunctionType
    AX = mybir.AxisListType
    RMAX = bass.bass_isa.ReduceOp.max

    B, C, N = x.shape
    P = 128
    HALVES = C // P
    IMG = 64
    UNIT = 512
    NU = N // UNIT
    TPU = UNIT // P
    NT = N // P
    HD = 32
    HEADS = C // HD
    HPH = HEADS // HALVES
    TAPS = 9
    STRIP = 16
    NS = IMG // STRIP
    SROWS, SCOLS = STRIP + 2, IMG + 2
    PROWS = SROWS // 2
    NPARTS = 2 * HALVES * NS
    CHUNKS = 2 * HALVES * NS
    PAIRS = 2 * NU
    XS = 64.0
    GN_EPS = 1e-5
    FOCUS_EPS = 1e-6
    TINY = 1e-30
    KVC = P + HPH
    QUARTER_PI = 0.7853981633974483
    HALF_PI = 1.5707963267948966

    ctx = ExitStack()
    with ctx:
        def sb(name, shape, dt=f32):
            return ctx.enter_context(nc.sbuf_tensor(name, shape, dt))

        def pb(name):
            return ctx.enter_context(nc.psum_tensor(name, [P, 512], f32))

        def sem(name):
            return ctx.enter_context(nc.semaphore(name))

        X = sb("X", [P, HALVES, N])
        XHL = sb("XHL", [P, 2, HALVES, N], f16)
        V = sb("V", [P, HD, 2, NT * HEADS], f16)
        FM = V[:, :, :, :].rearrange("p c a n -> p (c a n)").bitcast(f32).rearrange("p (c n) -> p c n", c=HD)
        TP = sb("TP", [P, HD, 3, 2, P], f16)
        WQ = sb("WQ", [P, 2, HALVES, 3 * C], f16)
        BQ = sb("BQ", [P, 3 * C], f16)
        ONES = sb("ONES", [P, P], f16)
        WP = sb("WP", [P, 2, HALVES, C], f16)
        FL = sb("FL", [P, C])
        BD = sb("BD", [P, 2, HALVES, TAPS, P], f16)
        ZEROS = BD[0:32, 0, 0, 0:2, 32:32 + P // 2 + 1]
        KB = sb("KB", [P, HALVES, TAPS, HD])
        W1 = sb("W1", [P, HALVES, P])
        W2 = sb("W2", [P, C])
        GM = sb("GM", [P, P])
        ID = sb("ID", [P, P])
        KVS = sb("KVS", [P, HALVES, KVC])
        COEF = sb("COEF", [P, TAPS, HALVES * TAPS])
        WK = sb("WK", [P, 3 * 1024])
        K0 = WK[:, 0:1024].rearrange("p (a n) -> p a n", a=2)
        K2 = WK[:, 1024:2048].rearrange("p (a n) -> p a n", a=2)
        K3 = WK[:, 2048:3072].rearrange("p (a n) -> p a n", a=2)
        SN = 2 * 2 * SROWS * SCOLS // 2
        S = WK[:, 0:SN].bitcast(f16).rearrange("p (g a r c) -> p g a r c", g=2, a=2, r=SROWS)
        VT = sb("VT", [P, 2, 2, HALVES, P + 2])
        QT = VT[:, :, :, :, :].rearrange("p a b c d -> p (a b c d)")[:, 0:1024].rearrange(
            "p (a h n) -> p a h n", a=2, h=HALVES)
        XN = sb("XN", [P, 2, PROWS * IMG])
        ROT = XN[:, 0, :].rearrange("p (h t o) -> p h t o", h=HALVES, t=TAPS)
        RTMP = XN[:, 1, :].rearrange("p (h t o) -> p h t o", h=HALVES, t=TAPS)
        O = sb("O", [P, 2, 2 * C])
        OT = sb("OT", [P, 2, HALVES, UNIT], f16)
        Y = sb("Y", [P, HALVES, UNIT])
        TR = sb("TR", [P, UNIT])
        B1 = sb("B1", [P, 1])
        B2 = sb("B2", [P, 2, HALVES])
        BP = sb("BP", [P, HALVES])
        DWB = sb("DWB", [P, HD])
        CK = sb("CK", [P, 2])
        XX = sb("XX", [P, 2, TAPS])
        ST = sb("ST", [P, HALVES, NU, 6])
        MV = sb("MV", [P, HALVES, 2])
        GS = sb("GS", [P, 8, HALVES])
        MEAN, DEV, SPREAD, VAR, ROOT, STD, RSTD, POOLED = (GS[:, i, :] for i in range(8))
        PR = sb("PR", [P, 9, HALVES])
        SC0, BI0, SC1, BI1, MODA, STDN, CBN, STDC, CBC = (PR[:, i, :] for i in range(9))
        HID = sb("HID", [P, 3])
        ZB = sb("ZB", [P, 4, HALVES])
        SIN = sb("SIN", [P, 3, HALVES])
        TT = sb("TT", [P, 2, HALVES, TAPS])
        TW = sb("TW", [P, 3, 2, HALVES * TAPS])
        S2 = sb("S2", [P, TPU])
        S6 = sb("S6", [P, TPU])
        RATIO = sb("RATIO", [P, 2, TPU])
        NORM = sb("NORM", [P, TPU])
        Z = sb("Z", [P, 2, HEADS])
        SCAL = sb("SCAL", [P, 24])

        def col(i):
            return SCAL[:, i:i + 1]
        (m_w, m_v, m_k, m_p) = (col(i) for i in range(4))
        (m_b, m_bv, m_db, s_t, m_t, a_w, inv_a, inv_a2, den_eps, a_v, v_fac, a_t, fm_fac, a_o, a_p, out_fac,
         a_r, conv_fac, v_bound, spare) = (col(4 + i) for i in range(20))

        F = [pb("F0"), pb("F1")]
        VA = [pb("VA0"), pb("VA1")]
        T = [pb("T0"), pb("T1")]
        PP = pb("PP")
        SM = pb("SM")

        w_in = sem("w_in")
        taps_in = sem("taps_in")
        x_in = sem("x_in")
        y_out = [sem("y_out0"), sem("y_out1")]
        set_dve = sem("set_dve")
        set_act = sem("set_act")
        soft_rdy = sem("soft_rdy")
        set_pool = sem("set_pool")
        rev_full = sem("rev_full")
        tp_act = sem("tp_act")
        tp_dve = sem("tp_dve")
        stats_rdy = sem("stats_rdy")
        z_rdy = sem("z_rdy")
        carried = sem("carried")
        ready = sem("ready")
        chain = sem("chain")
        mean_rdy, mean_mm = sem("mean_rdy"), sem("mean_mm")
        spread_rdy, spread_mm = sem("spread_rdy"), sem("spread_mm")
        var_rdy, root_rdy = sem("var_rdy"), sem("root_rdy")
        norm_rdy = sem("norm_rdy")
        pooled_rdy, hid_mm = sem("pooled_rdy"), sem("hid_mm")
        hid_rdy, z_mm = sem("hid_rdy"), sem("z_mm")
        zb_rdy, trig_rdy = sem("zb_rdy"), sem("trig_rdy")
        squash_rdy = sem("squash_rdy")
        rot_rdy, bd_hi, bd_lo = sem("rot_rdy"), sem("bd_hi"), sem("bd_lo")
        xn_rdy, h_rdy, l_rdy = sem("xn_rdy"), sem("h_rdy"), sem("l_rdy")
        border = sem("border")
        conv_full, x1_rdy = sem("conv_full"), sem("x1_rdy")
        f_full, f_max, f_sq = sem("f_full"), sem("f_max"), sem("f_sq")
        f_cube, f_six, f_ratio, f_root = sem("f_cube"), sem("f_six"), sem("f_ratio"), sem("f_root")
        k_scaled, cube_used = sem("k_scaled"), sem("cube_used")
        v_full, v_hi, v_true, v_lo = sem("v_full"), sem("v_hi"), sem("v_true"), sem("v_lo")
        ones_rdy = sem("ones_rdy")
        state_full, state_rdy = sem("state_full"), sem("state_rdy")
        dw_full, fm_rdy = sem("dw_full"), sem("fm_rdy")
        qt_rdy, attn_full, o_rdy = sem("qt_rdy"), sem("attn_full"), sem("o_rdy")
        ot_full, oh_rdy, ol_rdy = sem("ot_full"), sem("oh_rdy"), sem("ol_rdy")
        y_full, y_act, y_rdy = sem("y_full"), sem("y_act"), sem("y_rdy")
        tr_rdy, kept = sem("tr_rdy"), sem("kept")

        L_CR, X1_CR, MAX_CR, CUBE_CR, USED_CR, SIX_CR = 2, 2, 2, 2, 2, 4
        VLO_CR, FM_CR, O_CR, OL_CR, YA_CR = 2, 2, 2, 2, 2
        Y_CR, AT_CR, OUT_CR, QT_CR = 1, 1, 1, 1
        N_W = 12
        N_CHAIN = 59

        block = ctx.enter_context(nc.Block())

        VF = V[:, :, :, :].rearrange("p c a n -> p (c a n)").bitcast(f32)
        wq32 = VF[:, 0:1536].rearrange("p (h n) -> p h n", h=HALVES)
        bq32 = VF[:, 1536:2304]
        sc32 = VF[:, 2304:2560]
        wp32 = VF[:, 2560:3072].rearrange("p (h n) -> p h n", h=HALVES)
        dt32 = VF[:, 3072:3872]
        W_A, W_B, W_C, W_D, W_E, W_F = (VF[:, 4096 + 256 * i:4352 + 256 * i] for i in range(6))
        bh16 = VF[:, 6144:6528].bitcast(f16)
        bl16 = VF[:, 6528:6912].bitcast(f16)
        dsum = VF[:, 6912:6944]
        CH2 = HD // 2
        TS = XHL[:, :, :, :].rearrange("p a h n -> p (a h n)").bitcast(f32)[:, 0:CH2 * 3 * P].rearrange(
            "p (c k n) -> p c k n", c=CH2, k=3)

        REVS = CH2 * 3 * P // 512
        REV = XN[:, 1, 0:P]
        TPM = TP[:, :, :, :, :].rearrange("p c k a n -> p (c k) a n")

        def strip_rows(s, p):
            lo, hi = PROWS * p, PROWS * (p + 1)
            if s == 0 and p == 0:
                lo = 1
            if s == NS - 1 and p == 1:
                hi -= 1
            return lo, hi, STRIP * s - 1 + lo

        def alive(u):
            return lambda d: 0 <= 2 * u + d < PAIRS

        def always(d):
            return True

        def carry(eng):
            eng.sem_inc(carried, 1)

        @block.sync
        def _(sp):
            for h in range(HALVES):
                sp.sem_inc(y_out[h], 16 * OUT_CR)
            sp.dma_start(wq32, wqkv.rearrange("(h p) n -> p h n", p=P)).then_inc(w_in, 16)
            sp.dma_start(bq32, bqkv[0, :].partition_broadcast(P)).then_inc(w_in, 16)
            sp.dma_start(sc32, head_scale[0, :].partition_broadcast(P)).then_inc(w_in, 16)
            sp.dma_start(wp32, wproj.rearrange("(h p) n -> p h n", p=P)).then_inc(w_in, 16)
            sp.dma_start(dt32, dw_taps[0, :].partition_broadcast(P)).then_inc(w_in, 16)
            sp.dma_start(DWB[:, :], dw_b[0, :].partition_broadcast(P)).then_inc(w_in, 16)
            sp.dma_start(KB[:, :, :, :], conv_w.rearrange("(h p) t o -> p h t o", p=P)).then_inc(w_in, 16)
            sp.dma_start(W1[:, :, :], mlp_w1.rearrange("(h p) n -> p h n", p=P)).then_inc(w_in, 16)
            sp.dma_start(W2[:, :], mlp_w2).then_inc(w_in, 16)
            sp.dma_start(B1[:, :], mlp_b1).then_inc(w_in, 16)
            sp.dma_start(B2[:, :, :].rearrange("p k h -> p (k h)"), mlp_b2).then_inc(w_in, 16)
            sp.dma_start(BP[:, :], bproj).then_inc(w_in, 16)
            xv = x.rearrange("b (h p) n -> b p h n", p=P)
            ov = out.rearrange("b (h p) n -> b p h n", p=P)

            def load(c, u):
                sp.dma_start(X[:, :, bass.ds(u * UNIT, UNIT)],
                             xv[bass.ds(c, 1), :, :, bass.ds(u * UNIT, UNIT)].rearrange("b p h n -> p (b h) n")
                             ).then_inc(x_in, 16)

            def store(b, u):
                for h in range(HALVES):
                    sp.wait_ge(y_rdy, (b * NU + u) * HALVES + h + 1 + Y_CR)
                    sp.dma_start(ov[bass.ds(b, 1), :, h, bass.ds(u * UNIT, UNIT)].rearrange("b p n -> p (b n)"),
                                 Y[:, h, :]).then_inc(y_out[h], 16)

            def load_next(c, u):
                sp.wait_ge(xn_rdy, (c - 1) * 2 * NPARTS + NPARTS + HALVES * (u + 1))
                load(c, u)

            with sp.Fori(0, NU) as u:
                load(0, u)
            for rnd in range(2):
                if rnd == 1:
                    sp.wait_ge(rev_full, REVS)
                for rin in range(2):
                    for rout in range(2):
                        for k in range(3):
                            dy = 2 * (k - 1) + rin - rout + 3
                            src = bass.AP(dw_rows.tensor, (rnd * CH2 * 7 + dy) * P,
                                          [[1, IMG], [7 * P, CH2], [1, IMG]])
                            sp.dma_start(TS[IMG * rin:IMG * (rin + 1), :, k, IMG * rout:IMG * (rout + 1)],
                                         src).then_inc(taps_in, 16)
            with sp.Fori(0, NU) as u:
                load_next(1, u)
            with sp.Fori(0, B - 2) as b:
                with sp.Fori(0, NU) as u:
                    store(b, u)
                    load_next(b + 2, u)
            for b in (B - 2, B - 1):
                with sp.Fori(0, NU) as u:
                    store(b, u)
            for h in range(HALVES):
                sp.wait_ge(y_out[h], 16 * (B * NU + OUT_CR))

        @block.gpsimd
        def _(pool):
            g = nc.gpsimd
            g.memset(ID[:, :], 0.0).then_inc(set_pool, 1)
            g.memset(GM[:, :], 1.0 / 8).then_inc(set_pool, 1)
            pool.wait_ge(set_pool, 2)
            g.affine_select(out=ID[:, :], in_=ID[:, :], compare_op=ALU.not_equal, fill=1.0, base=0,
                            pattern=[[-1, P]], channel_multiplier=1).then_inc(set_pool, 1)
            gv = GM[:, :].rearrange("p (g e) -> p g e", e=8)
            g.affine_select(out=gv, in_=gv, compare_op=ALU.is_ge, fill=0.0, base=0,
                            pattern=[[-8, P // 8], [0, 8]], channel_multiplier=1).then_inc(set_pool, 1)
            pool.wait_ge(set_pool, 4)
            g.affine_select(out=gv, in_=gv, compare_op=ALU.is_ge, fill=0.0, base=7,
                            pattern=[[8, P // 8], [0, 8]], channel_multiplier=-1).then_inc(set_pool, 1)
            g.memset(REV, 0.0).then_inc(set_pool, 1)
            for k in (IMG - 1, 3 * IMG - 1):
                pool.wait_ge(set_pool, 6 + k // IMG // 2)
                g.affine_select(out=REV, in_=REV, compare_op=ALU.not_equal, fill=1.0, base=-k,
                                pattern=[[1, P]], channel_multiplier=1).then_inc(set_pool, 1)
            pool.wait_ge(set_dve, 1)
            g.partition_all_reduce(SCAL[:, 0:4], S6[:, 0:4], P, RMAX).then_inc(set_pool, 1)
            pool.sem_inc(l_rdy, L_CR)
            pool.wait_ge(ready, 1)

            def low(n, dst, hi, src):
                pool.wait_ge(xn_rdy, n + 1)
                pool.wait_ge(h_rdy, n + 1)
                carry(pool)
                g.tensor_tensor(dst, src, hi, ALU.subtract).then_inc(l_rdy, 1)

            def conv_inputs(c, first):
                if not first:
                    pool.wait_ge(cube_used, (c - 1) * 2 * PAIRS + PAIRS + USED_CR)
                    carry(pool)
                for h in range(HALVES):
                    for s in range(NS):
                        i = h * NS + s
                        gi = c * HALVES * NS + i
                        if not first or i >= 2:
                            pool.wait_ge(conv_full, 2 * gi - 2)
                            carry(pool)
                        buf = S[:, i % 2, :, :, :]
                        for e in (0, SCOLS - 1):
                            g.memset(buf[:, :, :, e:e + 1], 0.0).then_inc(border, 1)
                        if s in (0, NS - 1):
                            edge = 0 if s == 0 else SROWS - 1
                            g.memset(buf[:, :, edge, 1:SCOLS - 1], 0.0).then_inc(border, 1)
                        else:
                            pool.sem_inc(border, 1)
                        for p in range(2):
                            lo, hi, _ = strip_rows(s, p)
                            low(c * 2 * NPARTS + 2 * i + p, buf[:, 1, lo:hi, 1:SCOLS - 1],
                                buf[:, 0, lo:hi, 1:SCOLS - 1],
                                XN[:, p, 0:(hi - lo) * IMG].rearrange("p (r c) -> p r c", c=IMG))

            def attn_input(c, u, h, first):
                if not first:
                    pool.wait_ge(tr_rdy, ((c - 1) * NU + u) * HALVES + h + 1)
                    pool.wait_ge(f_full, (c - 1) * 2 * PAIRS + PAIRS + 2 * (u + 1))
                low(c * 2 * NPARTS + NPARTS + HALVES * u + h, XHL[:, 1, h, bass.ds(u * UNIT, UNIT)],
                    XHL[:, 0, h, bass.ds(u * UNIT, UNIT)], XN[:, h, 0:UNIT])

            def residual(b, u, h):
                pool.wait_ge(y_rdy, (b * NU + u) * HALVES + h + Y_CR)
                carry(pool)
                g.tensor_tensor(TR[:, :], XHL[:, 0, h, bass.ds(u * UNIT, UNIT)],
                                XHL[:, 1, h, bass.ds(u * UNIT, UNIT)], ALU.add).then_inc(tr_rdy, 1)

            def batch(b, last):
                pool.wait_ge(attn_full, b * NT + AT_CR)
                carry(pool)
                g.memset(VT[:, :, :, :, P:P + 1], 1.0).then_inc(ones_rdy, 1)
                if not last:
                    conv_inputs(b + 1, False)
                with pool.Fori(0, NU) as u:
                    for h in range(HALVES):
                        residual(b, u, h)
                        if not last:
                            attn_input(b + 1, u, h, False)

            conv_inputs(0, True)
            with pool.Fori(0, NU) as u:
                for h in range(HALVES):
                    attn_input(0, u, h, True)
            with pool.Fori(0, B - 1) as b:
                batch(b, False)
            batch(B - 1, True)

        @block.vector
        def _(dve):
            v = nc.vector
            steps = [0, 0]

            def setup(ins):
                steps[0] += 1
                ins.then_inc(chain, 1)
                dve.wait_ge(chain, steps[0])

            for t in (ONES, BQ, KVS, BD, HID):
                setup(v.memset(t[:], XS if t is ONES else 0.0))
            setup(v.memset(CK[:, :], HALF_PI))
            for t in range(TAPS):
                setup(v.memset(XX[:, 0, t:t + 1], float(t % 3 - 1)))
                setup(v.memset(XX[:, 1, t:t + 1], float(t // 3 - 1)))
            for s, n in ((x1_rdy, X1_CR), (f_max, MAX_CR), (f_cube, CUBE_CR), (v_lo, VLO_CR), (o_rdy, O_CR),
                         (ol_rdy, OL_CR), (cube_used, USED_CR),
                         (y_rdy, Y_CR), (attn_full, AT_CR), (qt_rdy, QT_CR)):
                dve.sem_inc(s, n)
            dve.wait_ge(w_in, 16 * N_W)
            setup(v.tensor_scalar(W_A, sc32, -1.0, None, ALU.mult))
            setup(v.tensor_tensor(W_A, W_A, sc32, ALU.min))
            dve.sem_inc(soft_rdy, 1)
            dve.wait_ge(set_act, 1)
            v.tensor_scalar(W_D, W_C, 1.0, None, ALU.add).then_inc(soft_rdy, 1)
            dve.wait_ge(soft_rdy, 2)
            setup(v.tensor_scalar(W_B, W_D, -1.0, None, ALU.add))
            setup(v.tensor_scalar(W_F, W_B, 0.0, None, ALU.is_equal))
            setup(v.tensor_tensor(W_B, W_B, W_F, ALU.add))
            setup(v.reciprocal(W_B, W_B))
            setup(v.tensor_tensor(W_B, W_B, W_C, ALU.mult))
            dve.wait_ge(set_act, 2)
            setup(v.tensor_tensor(W_B, W_B, W_E, ALU.mult))
            setup(v.tensor_tensor(W_F, W_F, W_C, ALU.mult))
            setup(v.tensor_tensor(W_B, W_B, W_F, ALU.add))
            setup(v.tensor_scalar(W_A, sc32, 0.0, None, ALU.max))
            setup(v.tensor_tensor(W_B, W_B, W_A, ALU.add))
            setup(v.reciprocal(W_B, W_B))
            for h in range(HALVES):
                for j in range(2):
                    cs = slice(j * C, (j + 1) * C)
                    setup(v.tensor_tensor(wq32[:, h, cs], wq32[:, h, cs], W_B, ALU.mult))
            for j in range(2):
                cs = slice(j * C, (j + 1) * C)
                setup(v.scalar_tensor_tensor(bq32[:, cs], bq32[:, cs], FOCUS_EPS, W_B, ALU.add, ALU.mult))
            for dst, src in ((S6[:, 0:1], wq32), (S6[:, 1:2], wq32[:, :, 2 * C:3 * C]), (S6[:, 3:4], wp32)):
                setup(v.tensor_reduce(dst, src, AX.XY, ALU.max, apply_absolute_value=True))
            setup(v.tensor_reduce(S6[:, 2:3], KB[:, :, :, :].rearrange("p h t o -> p (h t o)"), AX.X, ALU.max,
                                  apply_absolute_value=True))
            setup(v.tensor_reduce(m_b, bq32, AX.X, ALU.max, apply_absolute_value=True))
            setup(v.tensor_reduce(m_bv, bq32[:, 2 * C:3 * C], AX.X, ALU.max, apply_absolute_value=True))
            setup(v.tensor_reduce(m_db, DWB[:, :], AX.X, ALU.max, apply_absolute_value=True))
            setup(v.tensor_reduce(m_t, dt32, AX.X, ALU.max, apply_absolute_value=True))
            setup(v.tensor_reduce(dsum, dt32.rearrange("p (c t) -> p c t", c=HD), AX.X, ALU.add,
                                  apply_absolute_value=True))
            setup(v.tensor_reduce(s_t, dsum, AX.X, ALU.max))
            dve.sem_inc(set_dve, 1)
            dve.wait_ge(set_pool, 9)

            def over(dst, src, top):
                setup(v.tensor_scalar(dst, src, TINY, None, ALU.max))
                setup(v.reciprocal(dst, dst))
                if top != 1.0:
                    setup(v.tensor_scalar(dst, dst, top, None, ALU.mult))

            setup(v.tensor_tensor(m_w, m_w, m_b, ALU.max))
            over(a_w, m_w, 16384.0)
            setup(v.tensor_scalar(inv_a, a_w, XS, None, ALU.mult))
            setup(v.tensor_scalar(den_eps, inv_a, FOCUS_EPS, None, ALU.mult))
            setup(v.tensor_tensor(den_eps, den_eps, den_eps, ALU.mult))
            setup(v.reciprocal(inv_a, inv_a))
            setup(v.tensor_tensor(inv_a2, inv_a, inv_a, ALU.mult))
            setup(v.tensor_scalar(v_bound, m_v, 16600.0, m_bv, ALU.mult, ALU.add))
            over(a_v, v_bound, 32768.0)
            setup(v.tensor_tensor(v_fac, inv_a, a_v, ALU.mult))
            over(a_t, m_t, 16384.0)
            setup(v.tensor_tensor(fm_fac, a_v, a_t, ALU.mult))
            setup(v.reciprocal(fm_fac, fm_fac))
            setup(v.tensor_scalar(spare, s_t, 1.0, None, ALU.add))
            setup(v.tensor_scalar(spare, spare, v_bound, m_db, ALU.mult, ALU.add))
            over(a_o, spare, 32768.0)
            over(a_p, m_p, 16384.0)
            setup(v.tensor_tensor(out_fac, a_o, a_p, ALU.mult))
            setup(v.reciprocal(out_fac, out_fac))
            over(a_r, m_k, 4096.0)
            setup(v.tensor_scalar(conv_fac, a_r, XS, None, ALU.mult))
            setup(v.reciprocal(conv_fac, conv_fac))
            setup(v.tensor_scalar(spare, a_w, XS * FOCUS_EPS, None, ALU.mult))
            setup(v.tensor_scalar(FL[:, :], W_B, spare, None, ALU.mult))
            setup(v.tensor_scalar(KB[:, :, :, :], KB[:, :, :, :], a_r, None, ALU.mult))
            for src, hi, lo, a in ((wq32, WQ[:, 0], WQ[:, 1], a_w), (wp32, WP[:, 0], WP[:, 1], a_p),
                                   (bq32, bh16, bl16, a_w)):
                setup(v.tensor_scalar(src, src, a, None, ALU.mult))
                setup(v.tensor_copy(hi, src))
                setup(v.tensor_tensor(lo, src, hi, ALU.subtract))
            setup(v.tensor_copy(BQ[0:1, :], bh16[0:1, :]))
            setup(v.tensor_copy(BQ[32:33, :], bl16[32:33, :]))
            dve.sem_inc(ready, 1)
            for i in range(2 * REVS):
                dve.wait_ge(tp_act, i + 1)
                hi, lo = (TPM[:, 4 * i:4 * i + 4, j, :] for j in range(2))
                v.scalar_tensor_tensor(lo, F[i % 2][:, :].rearrange("p (m n) -> p m n", m=4), a_t, hi, ALU.mult,
                                       ALU.subtract).then_inc(tp_dve, 1)
            base = steps[0]

            def link(c, ins):
                steps[1] += 1
                ins.then_inc(chain, 1)
                dve.wait_ge(chain, c * N_CHAIN + base + steps[1])

            def means(c, layer):
                dve.wait_ge(stats_rdy, (2 * c + layer + 1) * HALVES * NU)
                carry(dve)
                steps[1] += 1
                v.bn_aggr(MV[:, 0, :], ST[:, 0, :, :].rearrange("p u s -> p (u s)")).then_inc(chain, 1)
                link(c, v.bn_aggr(MV[:, 1, :], ST[:, 1, :, :].rearrange("p u s -> p (u s)")))
                v.tensor_copy(DEV, MV[:, :, 0]).then_inc(mean_rdy, 1)

            def spreads(c, layer):
                dve.wait_ge(mean_mm, 2 * c + layer + 1)
                link(c, v.tensor_copy(MEAN, SM[:, 0:2]))
                link(c, v.tensor_tensor(DEV, DEV, MEAN, ALU.subtract))
                link(c, v.tensor_tensor(SPREAD, DEV, DEV, ALU.mult))
                v.tensor_tensor(SPREAD, SPREAD, MV[:, :, 1], ALU.add).then_inc(spread_rdy, 1)

            def variance(c, layer):
                dve.wait_ge(spread_mm, 2 * c + layer + 1)
                v.tensor_scalar(VAR, SM[:, 2:4], GN_EPS, None, ALU.add).then_inc(var_rdy, 1)

            def scale_and_bias(c, layer):
                dve.wait_ge(root_rdy, 2 * c + layer + 1)
                link(c, v.reciprocal(STD, ROOT))
                link(c, v.tensor_tensor(STD, STD, VAR, ALU.mult))
                link(c, v.tensor_tensor(STD, STD, ROOT, ALU.add))
                link(c, v.tensor_scalar(STD, STD, 0.5, None, ALU.mult))
                link(c, v.reciprocal(RSTD, STD))
                sc, bi = (SC0, BI0) if layer == 0 else (SC1, BI1)
                link(c, v.tensor_scalar(sc, RSTD, XS, None, ALU.mult))
                if layer == 1:
                    link(c, v.tensor_scalar(STDN, STD, 1.0 / XS, None, ALU.mult))
                    link(c, v.tensor_tensor(CBN, MEAN, BP[:, :], ALU.add))
                else:
                    v.tensor_tensor(POOLED, DEV, RSTD, ALU.mult).then_inc(pooled_rdy, 1)
                v.scalar_tensor_tensor(bi, MEAN, -1.0, sc, ALU.mult, ALU.mult).then_inc(norm_rdy, 1)

            def hidden(c):
                dve.wait_ge(hid_mm, c + 1)
                link(c, v.tensor_tensor(HID[:, 2:3], SM[:, 4:5], B1[:, :], ALU.add))
                for k in range(2):
                    r = slice(64 * k, 64 * k + 64)
                    v.tensor_scalar(HID[r, k:k + 1], HID[r, 2:3], 0.0, None, ALU.max).then_inc(hid_rdy, 1)

            def heads(c):
                dve.wait_ge(z_mm, c + 1)
                v.tensor_tensor(ZB[:, 0:2, :], SM[:, 8:12].rearrange("p (h k) -> p k h", k=2), B2[:, :, :],
                                ALU.add).then_inc(zb_rdy, 1)

            def rotation(c):
                dve.wait_ge(trig_rdy, 2 * (c + 1))
                link(c, v.tensor_scalar(MODA, ZB[:, 3, :], conv_fac, None, ALU.mult))
                link(c, v.tensor_scalar(SIN[:, 2, :], SIN[:, 0, :], -1.0, None, ALU.mult))
                for k in range(2):
                    for h in range(HALVES):
                        link(c, v.tensor_scalar(TT[:, k, h, :], XX[:, k, :], SIN[:, 1, h:h + 1], None, ALU.mult))
                for k in range(2):
                    for h in range(HALVES):
                        s = SIN[:, 0, h:h + 1] if k == 0 else SIN[:, 2, h:h + 1]
                        link(c, v.scalar_tensor_tensor(TT[:, k, h, :], XX[:, 1 - k, :], s, TT[:, k, h, :],
                                                       ALU.mult, ALU.add))
                tt = TT[:, :, :, :].rearrange("p k h t -> p k (h t)")
                link(c, v.tensor_scalar(TW[:, 0], tt, -1.0, 0.0, ALU.mult, ALU.max))
                link(c, v.tensor_scalar(TW[:, 2], tt, 0.0, None, ALU.max))
                link(c, v.tensor_tensor(TW[:, 1], TW[:, 0], TW[:, 2], ALU.add))
                link(c, v.tensor_scalar(TW[:, 1], TW[:, 1], -1.0, 1.0, ALU.mult, ALU.add))
                for jy in range(3):
                    wy = TW[:, jy, 1, :].unsqueeze(1).broadcast_to([P, 3, HALVES * TAPS])
                    link(c, v.tensor_tensor(COEF[:, 3 * jy:3 * jy + 3, :], wy, TW[:, :, 0, :], ALU.mult))
                for j in range(TAPS):
                    cj = COEF[:, j, :].rearrange("p (h t) -> p h t", h=HALVES).unsqueeze(3).broadcast_to(
                        [P, HALVES, TAPS, HD])
                    kj = KB[:, :, j, :].unsqueeze(2).broadcast_to([P, HALVES, TAPS, HD])
                    link(c, v.tensor_tensor(ROT if j == 0 else RTMP, cj, kj, ALU.mult))
                    if j:
                        link(c, v.tensor_tensor(ROT, ROT, RTMP, ALU.add))
                dve.sem_inc(rot_rdy, 1)
                dve.wait_ge(bd_hi, 4 * (c + 1))
                for q in range(4):
                    r = slice(32 * q, 32 * q + 32)
                    v.tensor_tensor(BD[r, 1, :, :, r], ROT[r], BD[r, 0, :, :, r], ALU.subtract).then_inc(bd_lo, 1)

            def x_stats(c, u):
                for h in range(HALVES):
                    v.bn_stats(ST[:, h, bass.ds(u, 1), :].rearrange("p u s -> p (u s)"),
                               X[:, h, bass.ds(u * UNIT, UNIT)]).then_inc(stats_rdy, 1)

            def conv_steps(c, first):
                if not first:
                    dve.wait_ge(cube_used, (c - 1) * 2 * PAIRS + PAIRS + USED_CR)

                def high(i):
                    s = i % NS
                    if not first or i >= 2:
                        dve.wait_ge(conv_full, 2 * (c * HALVES * NS + i) - 2)
                    for p in range(2):
                        n = c * 2 * NPARTS + 2 * i + p
                        lo, hi, _ = strip_rows(s, p)
                        dve.wait_ge(xn_rdy, n + 1)
                        v.tensor_copy(S[:, i % 2, 0, lo:hi, 1:SCOLS - 1],
                                      XN[:, p, 0:(hi - lo) * IMG].rearrange("p (r c) -> p r c", c=IMG)
                                      ).then_inc(h_rdy, 1)

                def evacuate(i):
                    h, s = divmod(i, NS)
                    for q in range(2):
                        n = c * CHUNKS + 2 * i + q
                        tok = slice((2 * s + q) * UNIT, (2 * s + q + 1) * UNIT)
                        dve.wait_ge(conv_full, n + 1)
                        v.scalar_tensor_tensor(X[:, h, tok], VA[q][:, :], MODA[:, h:h + 1], X[:, h, tok],
                                               ALU.mult, ALU.add).then_inc(x1_rdy, 1)
                        dve.wait_ge(x1_rdy, n + 1 + X1_CR)
                        v.bn_stats(ST[:, h, 2 * s + q, :], X[:, h, tok]).then_inc(stats_rdy, 1)

                high(0)
                for i in range(1, HALVES * NS):
                    high(i)
                    evacuate(i - 1)
                evacuate(HALVES * NS - 1)

            def attn_input(c, u, h, first):
                n = c * 2 * NPARTS + NPARTS + HALVES * u + h
                if not first:
                    dve.wait_ge(tr_rdy, ((c - 1) * NU + u) * HALVES + h + 1)
                    dve.wait_ge(f_full, (c - 1) * 2 * PAIRS + PAIRS + 2 * (u + 1))
                dve.wait_ge(xn_rdy, n + 1)
                v.tensor_copy(XHL[:, 0, h, bass.ds(u * UNIT, UNIT)], XN[:, h, 0:UNIT]).then_inc(h_rdy, 1)

            def floor_max(n, p):
                dve.wait_ge(f_full, n + 1)
                fl = FL[:, :].unsqueeze(1).broadcast_to([P, 2, C])
                v.tensor_tensor(K0[:, p, :].rearrange("p (t n) -> p t n", t=2),
                                F[p][:, :].rearrange("p (t n) -> p t n", t=2), fl, ALU.max).then_inc(f_max, 1)

            def cube(n, p):
                dve.wait_ge(f_sq, 2 * (n + 1))
                dve.wait_ge(cube_used, n + 1)
                dve.wait_ge(f_six, 2 * n + 2)
                v.tensor_tensor(K3[:, p, :], K2[:, p, :], K0[:, p, :], ALU.mult).then_inc(f_cube, 1)

            def ratio(n, p, a, b):
                cs = slice(2 * p, 2 * p + 2)
                dve.wait_ge(f_six, 2 * (n + 1) + SIX_CR)
                v.reciprocal(RATIO[:, 1, cs], b[:, cs]).then_inc(f_ratio, 1)
                dve.wait_ge(f_ratio, 2 * n + 1)
                v.tensor_tensor(RATIO[:, 0, cs], a[:, cs], RATIO[:, 1, cs], ALU.mult).then_inc(f_ratio, 1)

            def scale_k(n, p):
                dve.wait_ge(f_root, n + 1)
                for t in range(2):
                    ks = K3[:, p, t * C:(t + 1) * C]
                    v.tensor_scalar(ks, ks, NORM[:, 2 * p + t:2 * p + t + 1], None, ALU.mult).then_inc(k_scaled, 1)

            def low_v(b, u, p):
                m = b * PAIRS + 2 * u + p
                dve.wait_ge(v_hi, m + 1)
                dve.wait_ge(v_true, m + 1)
                for t in range(2):
                    dst = bass.ds((u * TPU + 2 * p + t) * HEADS, HEADS)
                    last = v.scalar_tensor_tensor(
                        V[:, :, 1, dst], VA[p][:, t * C:(t + 1) * C].rearrange("p (c h) -> p c h", c=HD), v_fac,
                        V[:, :, 0, dst], ALU.mult, ALU.subtract)
                last.then_inc(v_lo, 1)

            def step_kv(b, u, p, started):
                n = b * 2 * PAIRS + 2 * u + p
                if started:
                    ratio(n - 1, 1 - p, S2, S6)
                floor_max(n, p)
                if started:
                    scale_k(n - 1, 1 - p)
                    low_v(b, u - 1 + p, 1 - p)
                cube(n, p)

            def keep(b):
                dve.wait_ge(y_rdy, b * NU * HALVES + Y_CR)
                v.tensor_copy(PR[:, 7:9, :], PR[:, 5:7, :]).then_inc(kept, 1)

            def state(b):
                dve.wait_ge(state_full, b + 1)
                for h in range(HALVES):
                    o_v, o_d = (HPH, 0) if h == 0 else (0, P)
                    for q in range(HPH):
                        r = slice(32 * q, 32 * q + 32)
                        v.tensor_copy(KVS[r, h, o_v + q:o_v + P:HPH], T[h][r, q:P:HPH]).then_inc(state_rdy, 1)
                        v.tensor_copy(KVS[r, h, o_d + q:o_d + q + 1], T[h][r, P:P + 1]).then_inc(state_rdy, 1)

            def attend(b, u, t):
                i = b * NT + u * TPU + t
                p, a = t // 2, VA[t % 2]
                dve.wait_ge(attn_full, i + 1 + AT_CR)
                dve.wait_ge(f_root, b * 2 * PAIRS + PAIRS + 2 * u + p + 1)
                zt = Z[:, t % 2, :]
                zh = zt.rearrange("p (h f) -> p h f", h=HALVES)
                av = a[:, :]
                den = bass.AP(av.tensor, av.offset, [list(av.ap[0]), [KVC + P, HALVES], [1, HPH]])
                v.tensor_scalar(zh, den, NORM[:, t:t + 1], None, ALU.add).then_inc(z_rdy, 1)
                dve.wait_ge(z_rdy, 3 * i + 1)
                v.reciprocal(zt, zt).then_inc(z_rdy, 1)
                dve.wait_ge(z_rdy, 3 * i + 2)
                o = O[:, p, (t % 2) * C:(t % 2 + 1) * C]
                v.tensor_tensor(o.rearrange("p (c h f) -> p h c f", c=HD, h=HALVES),
                                a[:, HPH:HPH + C].rearrange("p (h c f) -> p h c f", h=HALVES, c=HD),
                                zh.unsqueeze(2).broadcast_to([P, HALVES, HD, HPH]), ALU.mult).then_inc(z_rdy, 1)
                dve.wait_ge(z_rdy, 3 * i + 3)
                oc = o.rearrange("p (c e) -> p c e", c=HD)
                v.tensor_tensor(oc, oc, FM[:, :, bass.ds((u * TPU + t) * HEADS, HEADS)], ALU.add).then_inc(o_rdy, 1)

            def finish(b, u, h):
                e = (b * NU + u) * HALVES + h
                dve.wait_ge(y_act, e + 1 + YA_CR)
                dve.wait_ge(tr_rdy, e + 1)
                v.scalar_tensor_tensor(Y[:, h, :], TR[:, :], STDC[:, h:h + 1], Y[:, h, :], ALU.mult,
                                       ALU.add).then_inc(y_rdy, 1)

            def low_out(b, u, p):
                m = b * PAIRS + 2 * u + p
                dve.wait_ge(oh_rdy, m + 1)
                hi, lo = (OT[:, i, :, 2 * P * p:2 * P * (p + 1)] for i in range(2))
                v.scalar_tensor_tensor(lo, T[1][:, :].rearrange("p (h n) -> p h n", h=HALVES), a_o, hi, ALU.mult,
                                       ALU.subtract).then_inc(ol_rdy, 1)

            def step_q(b, u, p, live, nxt):
                n = b * 2 * PAIRS + PAIRS + 2 * u + p
                if live(p):
                    floor_max(n, p)
                if live(p - 1):
                    ratio(n - 1, 1 - p, S6, S2)
                if live(p - 3):
                    low_out(b, u - 2 + p, 1 - p)
                if p == 1 and live(-4):
                    finish(b, u - 2, 0)
                if live(p - 2):
                    attend(b, u - 1, 2 * p)
                if live(p):
                    cube(n, p)
                if live(p - 2):
                    attend(b, u - 1, 2 * p + 1)
                if p == 1 and live(-4):
                    finish(b, u - 2, 1)
                if nxt:
                    attn_input(b + 1, u - 2, p, False)

            def batch(b, last):
                keep(b)
                for p in range(2):
                    step_kv(b, 0, p, p > 0)
                if not last:
                    dve.wait_ge(x_in, 16 * NU * (b + 2))
                    carry(dve)
                with dve.Fori(1, 5) as u:
                    for p in range(2):
                        step_kv(b, u, p, True)
                        if not last:
                            x_stats(b + 1, 2 * (u - 1) + p)
                steps[1] = 0
                small = iter((lambda: spreads(b + 1, 0), lambda: variance(b + 1, 0),
                              lambda: (scale_and_bias(b + 1, 0)), lambda: hidden(b + 1), lambda: heads(b + 1),
                              lambda: None))
                if not last:
                    means(b + 1, 0)
                for u in range(5, NU):
                    for p in range(2):
                        step_kv(b, u, p, True)
                        if not last:
                            next(small)()
                n = b * 2 * PAIRS + PAIRS - 1
                ratio(n, 1, S2, S6)
                scale_k(n, 1)
                low_v(b, NU - 1, 1)
                state(b)
                if not last:
                    dve.wait_ge(l_rdy, (b + 1) * 2 * NPARTS + L_CR)
                    rotation(b + 1)
                    conv_steps(b + 1, False)
                    means(b + 1, 1)
                small = iter((lambda: spreads(b + 1, 1), lambda: variance(b + 1, 1),
                              lambda: scale_and_bias(b + 1, 1), lambda: None))
                for u in range(2):
                    if u == 1:
                        dve.wait_ge(fm_rdy, HD * (b + 1) + FM_CR)
                    for p in range(2):
                        step_q(b, u, p, alive(u), False)
                        if not last:
                            next(small)()
                assert last or steps[1] == N_CHAIN, steps
                with dve.Fori(2, NU) as u:
                    for p in range(2):
                        step_q(b, u, p, always, not last)
                for u in (NU, NU + 1):
                    for p in range(2):
                        step_q(b, u, p, alive(u), not last)

            dve.wait_ge(x_in, 16 * NU)
            with dve.Fori(0, NU) as u:
                x_stats(0, u)
            steps[1] = 0
            for stage in (means, spreads, variance, scale_and_bias):
                stage(0, 0)
            hidden(0)
            heads(0)
            rotation(0)
            conv_steps(0, True)
            for stage in (means, spreads, variance, scale_and_bias):
                stage(0, 1)
            assert steps[1] == N_CHAIN, steps
            with dve.Fori(0, NU) as u:
                for h in range(HALVES):
                    attn_input(0, u, h, True)
            with dve.Fori(0, B - 1) as b:
                batch(b, False)
            batch(B - 1, True)

        @block.scalar
        def _(act):
            a = nc.scalar
            act.wait_ge(soft_rdy, 1)
            a.activation(W_C, W_A, ACT.Exp).then_inc(set_act, 1)
            act.wait_ge(soft_rdy, 2)
            a.activation(W_E, W_D, ACT.Ln).then_inc(set_act, 1)
            act.wait_ge(ready, 1)
            for s, n in ((f_six, SIX_CR), (fm_rdy, FM_CR), (y_act, YA_CR)):
                act.sem_inc(s, n)
            for i in range(2 * REVS):
                act.wait_ge(rev_full, i + 1)
                a.activation(TPM[:, 4 * i:4 * i + 4, 0, :], F[i % 2][:, :].rearrange("p (m n) -> p m n", m=4),
                             ACT.Copy, scale=a_t).then_inc(tp_act, 1)

            def root(n):
                act.wait_ge(var_rdy, n + 1)
                a.activation(ROOT, VAR, ACT.Sqrt).then_inc(root_rdy, 1)

            def squash(c):
                act.wait_ge(zb_rdy, c + 1)
                a.activation(ZB[:, 2, :], ZB[:, 0, :], ACT.Tanh).then_inc(squash_rdy, 1)
                a.activation(ZB[:, 3, :], ZB[:, 1, :], ACT.Sigmoid)
                act.wait_ge(squash_rdy, c + 1)
                a.activation(SIN[:, 0, :], ZB[:, 2, :], ACT.Sin, scale=QUARTER_PI).then_inc(trig_rdy, 1)
                a.activation(SIN[:, 1, :], ZB[:, 2, :], ACT.Sin, scale=QUARTER_PI, bias=CK[:, 0:1]
                             ).then_inc(trig_rdy, 1)

            def kernels(c):
                act.wait_ge(rot_rdy, c + 1)
                for q in range(4):
                    r = slice(32 * q, 32 * q + 32)
                    a.copy(BD[r, 0, :, :, r], ROT[r]).then_inc(bd_hi, 1)

            def conv_inputs(c):
                act.wait_ge(norm_rdy, 2 * c + 1)
                act.wait_ge(bd_lo, 4 * (c + 1))
                for h in range(HALVES):
                    for s in range(NS):
                        for p in range(2):
                            n = c * 2 * NPARTS + 2 * (h * NS + s) + p
                            lo, hi, row = strip_rows(s, p)
                            act.wait_ge(l_rdy, n + 1)
                            a.activation(XN[:, p, 0:(hi - lo) * IMG],
                                         X[:, h, row * IMG:(row + hi - lo) * IMG], ACT.Identity,
                                         scale=SC0[:, h:h + 1], bias=BI0[:, h:h + 1]).then_inc(xn_rdy, 1)

            def attn_input(c, u, h):
                act.wait_ge(l_rdy, c * 2 * NPARTS + NPARTS + HALVES * u + h + 1)
                a.activation(XN[:, h, 0:UNIT], X[:, h, bass.ds(u * UNIT, UNIT)], ACT.Identity,
                             scale=SC1[:, h:h + 1], bias=BI1[:, h:h + 1]).then_inc(xn_rdy, 1)

            def squares(n, p):
                act.wait_ge(f_max, n + 1 + MAX_CR)
                act.wait_ge(f_cube, n + 1)
                act.wait_ge(f_six, 2 * n + 2)
                for t in range(2):
                    ts = slice(t * C, (t + 1) * C)
                    a.activation(K2[:, p, ts], K0[:, p, ts], ACT.Square, scale=inv_a,
                                 accum_out=S2[:, 2 * p + t:2 * p + t + 1]).then_inc(f_sq, 1)

            def sixths(n, p):
                act.wait_ge(f_cube, n + 1 + CUBE_CR)
                for t in range(2):
                    a.activation(K2[:, p, t * C:(t + 1) * C], K3[:, p, t * C:(t + 1) * C], ACT.Square, scale=inv_a,
                                 accum_out=S6[:, 2 * p + t:2 * p + t + 1]).then_inc(f_six, 1)

            def norms(n, p, factor):
                cs = slice(2 * p, 2 * p + 2)
                act.wait_ge(f_ratio, 2 * (n + 1))
                a.activation(NORM[:, cs], RATIO[:, 0, cs], ACT.Sqrt, scale=factor).then_inc(f_root, 1)

            def step_kv(b, u, p, started):
                n, m = b * 2 * PAIRS + 2 * u + p, b * PAIRS + 2 * u + p
                if started:
                    norms(n - 1, 1 - p, inv_a2)
                squares(n, p)
                act.wait_ge(v_full, m + 1)
                for t in range(2):
                    last = a.activation(V[:, :, 0, bass.ds((u * TPU + 2 * p + t) * HEADS, HEADS)],
                                        VA[p][:, t * C:(t + 1) * C].rearrange("p (c h) -> p c h", c=HD),
                                        ACT.Copy, scale=v_fac)
                last.then_inc(v_hi, 1)
                act.wait_ge(cube_used, n + 1)
                for t in range(2):
                    last = a.activation(
                        VT[:, p, t, :, 0:P].rearrange("p h (c f) -> p h c f", c=HD),
                        VA[p][:, t * C:(t + 1) * C].rearrange("p (c h f) -> p h c f", c=HD, h=HALVES),
                        ACT.Copy, scale=inv_a)
                last.then_inc(v_true, 1)
                sixths(n, p)

            def depthwise(b):
                for c in range(HD):
                    act.wait_ge(dw_full, b * HD + c + 1)
                    a.activation(FM[:, c, :], F[c % 2][:, 0:NT * HEADS], ACT.Identity, scale=fm_fac,
                                 bias=DWB[:, c:c + 1]).then_inc(fm_rdy, 1)

            def transposed_q(b, u, p):
                act.wait_ge(cube_used, b * 2 * PAIRS + PAIRS + 2 * u + p + 1 + USED_CR)
                a.copy(QT[:, p, :, :], T[0][:, :].rearrange("p (h n) -> p h n", h=HALVES)).then_inc(qt_rdy, 1)

            def output(b, u, h):
                e = (b * NU + u) * HALVES + h
                act.wait_ge(y_full, e + 1)
                act.wait_ge(y_out[h], 16 * (b * NU + u + OUT_CR))
                a.activation(Y[:, h, :], (PP, SM)[h][:, :], ACT.Identity, scale=out_fac, bias=CBC[:, h:h + 1]
                             ).then_inc(y_act, 1)

            def high_out(b, u, p):
                act.wait_ge(ot_full, b * PAIRS + 2 * u + p + 1)
                a.activation(OT[:, 0, :, 2 * P * p:2 * P * (p + 1)],
                             T[1][:, :].rearrange("p (h n) -> p h n", h=HALVES), ACT.Copy, scale=a_o
                             ).then_inc(oh_rdy, 1)

            def step_q(b, u, p, live, nxt):
                n = b * 2 * PAIRS + PAIRS + 2 * u + p
                if p == 1 and live(-4):
                    output(b, u - 2, 1)
                if live(p - 3):
                    high_out(b, u - 2 + p, 1 - p)
                if live(p):
                    squares(n, p)
                if live(p - 1):
                    norms(n - 1, 1 - p, den_eps)
                if live(p - 1):
                    transposed_q(b, u - 1 + p, 1 - p)
                if live(p):
                    sixths(n, p)
                if nxt:
                    attn_input(b + 1, u - 2, p)
                if p == 0 and live(-4):
                    output(b, u - 2, 0)

            def batch(b, last):
                for p in range(2):
                    step_kv(b, 0, p, p > 0)
                with act.Fori(1, 5) as u:
                    for p in range(2):
                        step_kv(b, u, p, True)
                for u in range(5, NU):
                    for p in range(2):
                        step_kv(b, u, p, True)
                        if not last and 2 * u + p == 11:
                            root(2 * (b + 1))
                        if not last and 2 * u + p == 14:
                            squash(b + 1)
                norms(b * 2 * PAIRS + PAIRS - 1, 1, inv_a2)
                depthwise(b)
                if not last:
                    kernels(b + 1)
                    conv_inputs(b + 1)
                act.wait_ge(kept, b + 1)
                for u in range(2):
                    for p in range(2):
                        step_q(b, u, p, alive(u), False)
                        if not last and 2 * u + p == 1:
                            root(2 * (b + 1) + 1)
                if not last:
                    act.wait_ge(norm_rdy, 2 * (b + 1) + 2)
                with act.Fori(2, NU) as u:
                    for p in range(2):
                        step_q(b, u, p, always, not last)
                for u in (NU, NU + 1):
                    for p in range(2):
                        step_q(b, u, p, alive(u), not last)

            root(0)
            squash(0)
            kernels(0)
            conv_inputs(0)
            root(1)
            act.wait_ge(norm_rdy, 2)
            with act.Fori(0, NU) as u:
                for h in range(HALVES):
                    attn_input(0, u, h)
            with act.Fori(0, B - 1) as b:
                batch(b, False)
            batch(B - 1, True)

        @block.tensor
        def _(pe):
            t_ = nc.tensor

            def group_mean(c, layer):
                pe.wait_ge(mean_rdy, 2 * c + layer + 1)
                t_.matmul(SM[:, 0:2], GM[:, :], DEV, start=True, stop=True).then_inc(mean_mm, 1)

            def group_spread(c, layer):
                pe.wait_ge(spread_rdy, 2 * c + layer + 1)
                t_.matmul(SM[:, 2:4], GM[:, :], SPREAD, start=True, stop=True).then_inc(spread_mm, 1)

            def hidden(c):
                pe.wait_ge(pooled_rdy, c + 1)
                for h in range(HALVES):
                    last = t_.matmul(SM[:, 4:5], W1[:, h, :], POOLED[:, h:h + 1], start=(h == 0), stop=(h == 1))
                last.then_inc(hid_mm, 1)

            def heads(c):
                pe.wait_ge(hid_rdy, 2 * (c + 1))
                for h in range(HALVES):
                    o = 8 + 2 * h
                    last = t_.matmul(SM[:, o:o + 2], W2[:, h * P:(h + 1) * P], HID[:, 0:2], start=True, stop=True)
                last.then_inc(z_mm, 1)

            PASSES = ((0, 0), (0, 1), (1, 0))

            def convolution(c):
                with pe.Fori(0, HALVES) as h:
                    for s in range(NS):
                        i = h * NS + s
                        pe.wait_ge(h_rdy, c * 2 * NPARTS + 2 * i + 2)
                        pe.wait_ge(l_rdy, c * 2 * NPARTS + 2 * i + 2 + L_CR)
                        pe.wait_ge(border, 3 * (c * HALVES * NS + i + 1))
                        for q in range(2):
                            pe.wait_ge(x1_rdy, c * CHUNKS + 2 * i + q + 1)
                            k = 0
                            for wa, xa in PASSES:
                                for t in range(TAPS):
                                    y0 = 8 * q + t // 3
                                    last = t_.matmul(VA[q][:, :], BD[:, wa, bass.ds(h, 1), t, :].rearrange(
                                        "p h o -> p (h o)"), S[:, s % 2, xa, y0:y0 + 8, t % 3:t % 3 + IMG],
                                        start=(k == 0), stop=(k == 3 * TAPS - 1))
                                    k += 1
                            last.then_inc(conv_full, 1)

            def project(b, u, p, banks):
                for bank, c0 in banks:
                    for t in range(2):
                        at = bass.ds(u * UNIT + (2 * p + t) * P, P)
                        o = bank[p][:, t * C:(t + 1) * C]
                        k = 0
                        for h, xa in ((0, 0), (1, 0), (0, 1), (1, 1)):
                            for wa in (0, 1) if xa == 0 else (0,):
                                t_.matmul(o, XHL[:, xa, h, at], WQ[:, wa, h, c0:c0 + C], start=(k == 0), stop=False)
                                k += 1
                        last = t_.matmul(o, ONES[:, :], BQ[:, c0:c0 + C], start=False, stop=True)
                    last.then_inc(f_full if bank is F else v_full, 1)

            def accumulate_state(b, u, p):
                m = b * PAIRS + 2 * u + p
                pe.wait_ge(k_scaled, 2 * (m + 1))
                pe.wait_ge(v_true, m + 1)
                for t in range(2):
                    for h in range(HALVES):
                        last = t_.matmul(T[h][:, 0:P + 1], K3[:, p, t * C + h * P:t * C + (h + 1) * P],
                                         VT[:, p, t, h, 0:P + 1], start=False, stop=False)
                last.then_inc(cube_used, 1)

            def step_kv(b, u, p, started):
                pe.wait_ge(f_max, b * 2 * PAIRS + 2 * u + p + 1)
                pe.wait_ge(v_lo, b * PAIRS + 2 * u + p + 1)
                pe.wait_ge(h_rdy, b * 2 * NPARTS + NPARTS + HALVES * (u + 1))
                pe.wait_ge(l_rdy, b * 2 * NPARTS + NPARTS + HALVES * (u + 1) + L_CR)
                project(b, u, p, ((F, C), (VA, 2 * C)))
                if started:
                    accumulate_state(b, u - 1 + p, 1 - p)

            def depthwise(b):
                for c in range(HD):
                    pe.wait_ge(fm_rdy, b * HD + c + 1)
                    k = 0
                    for d in (1, 0, 2):
                        lo, hi = max(0, 1 - d) * HEADS, (NT - max(0, d - 1)) * HEADS
                        for ta, va in PASSES:
                            sh = (d - 1) * HEADS
                            last = t_.matmul(F[c % 2][:, lo:hi], TP[:, c, d, ta, :], V[:, c, va, lo + sh:hi + sh],
                                             start=(k == 0), stop=(k == 8))
                            k += 1
                    last.then_inc(dw_full, 1)

            def transpose_q(b, u, p):
                n = b * 2 * PAIRS + PAIRS + 2 * u + p
                pe.wait_ge(f_cube, n + 1 + CUBE_CR)
                pe.wait_ge(qt_rdy, b * PAIRS + 2 * u + p + QT_CR)
                for h in range(HALVES):
                    for t in range(2):
                        last = t_.transpose(T[0][:, (2 * h + t) * P:(2 * h + t + 1) * P],
                                            K3[:, p, t * C + h * P:t * C + (h + 1) * P], ID[:, :])
                last.then_inc(cube_used, 1)

            def attention(b, u, p):
                pe.wait_ge(qt_rdy, b * PAIRS + 2 * u + p + 1 + QT_CR)
                for t in range(2):
                    pe.wait_ge(o_rdy, b * NT + u * TPU + 2 * p + t + 1)
                    for h in range(HALVES):
                        last = t_.matmul(VA[t][:, h * KVC:(h + 1) * KVC], QT[:, p, h, t * P:(t + 1) * P],
                                         KVS[:, h, :], start=True, stop=True)
                    last.then_inc(attn_full, 1)

            def transpose_o(b, u, p):
                pe.wait_ge(o_rdy, b * NT + u * TPU + 2 * p + 2 + O_CR)
                pe.wait_ge(ol_rdy, b * PAIRS + 2 * u + p + OL_CR)
                for h in range(HALVES):
                    for t in range(2):
                        last = t_.transpose(T[1][:, (2 * h + t) * P:(2 * h + t + 1) * P],
                                            O[:, p, t * C + h * P:t * C + (h + 1) * P], ID[:, :])
                last.then_inc(ot_full, 1)

            def output(b, u, h):
                pe.wait_ge(ol_rdy, b * PAIRS + 2 * (u + 1) + OL_CR)
                pe.wait_ge(y_act, (b * NU + u) * HALVES + h + 1)
                k = 0
                for kk in range(HALVES):
                    for wa, xa in PASSES:
                        last = t_.matmul((PP, SM)[h][:, :], WP[:, wa, kk, h * P:(h + 1) * P], OT[:, xa, kk, :],
                                         start=(k == 0), stop=(k == 5))
                        k += 1
                last.then_inc(y_full, 1)

            def step_q(b, u, p, live):
                if live(p):
                    pe.wait_ge(f_max, b * 2 * PAIRS + PAIRS + 2 * u + p + 1)
                    project(b, u, p, ((F, 0),))
                if live(p - 3):
                    transpose_o(b, u - 2 + p, 1 - p)
                if live(p - 1):
                    transpose_q(b, u - 1 + p, 1 - p)
                if live(p - 2):
                    attention(b, u - 1, p)
                if p == 0 and live(-4):
                    for h in range(HALVES):
                        output(b, u - 2, h)

            def batch(b, last):
                pe.wait_ge(ol_rdy, b * PAIRS + OL_CR)
                pe.wait_ge(qt_rdy, b * PAIRS + QT_CR)
                for h in range(HALVES):
                    t_.matmul(T[h][:, 0:P + 2], ONES[0:32, :], ZEROS, start=True, stop=False)
                pe.wait_ge(ones_rdy, b + 1)
                carry(pe)
                for p in range(2):
                    step_kv(b, 0, p, p > 0)
                with pe.Fori(1, 5) as u:
                    for p in range(2):
                        step_kv(b, u, p, True)
                small = {10: lambda: group_mean(b + 1, 0), 11: lambda: group_spread(b + 1, 0),
                         12: lambda: hidden(b + 1), 13: lambda: heads(b + 1)}
                for u in range(5, NU):
                    for p in range(2):
                        step_kv(b, u, p, True)
                        if not last and 2 * u + p in small:
                            small[2 * u + p]()
                accumulate_state(b, NU - 1, 1)
                for h in range(HALVES):
                    fin = t_.matmul(T[h][:, 0:P + 2], ONES[0:32, :], ZEROS, start=False, stop=True)
                fin.then_inc(state_full, 1)
                pe.wait_ge(v_lo, PAIRS * (b + 1) + VLO_CR)
                pe.wait_ge(f_max, b * 2 * PAIRS + PAIRS + MAX_CR)
                carry(pe)
                depthwise(b)
                if not last:
                    pe.wait_ge(bd_lo, 4 * (b + 2))
                    carry(pe)
                    convolution(b + 1)
                    pe.wait_ge(x1_rdy, CHUNKS * (b + 2) + X1_CR)
                pe.wait_ge(fm_rdy, HD * (b + 1) + FM_CR)
                pe.wait_ge(state_rdy, 4 * HPH * (b + 1))
                for u in range(2):
                    for p in range(2):
                        step_q(b, u, p, alive(u))
                        if not last and u == 0:
                            (group_mean, group_spread)[p](b + 1, 1)
                with pe.Fori(2, NU) as u:
                    for p in range(2):
                        step_q(b, u, p, always)
                for u in (NU, NU + 1):
                    for p in range(2):
                        step_q(b, u, p, alive(u))

            pe.wait_ge(ready, 1)
            pe.wait_ge(set_pool, 8)
            tsm = XHL[:, :, :, :].rearrange("p a h n -> p (a h n)").bitcast(f32)
            for i in range(2 * REVS):
                pe.wait_ge(taps_in, 16 * 12 * (i // REVS + 1))
                if i >= 2:
                    pe.wait_ge(tp_dve, i - 1)
                j = i % REVS
                t_.matmul(F[i % 2][:, :], REV, tsm[:, 512 * j:512 * j + 512], start=True, stop=True
                          ).then_inc(rev_full, 1)
            group_mean(0, 0)
            group_spread(0, 0)
            hidden(0)
            heads(0)
            pe.wait_ge(bd_lo, 4)
            convolution(0)
            group_mean(0, 1)
            group_spread(0, 1)
            pe.wait_ge(tp_dve, 2 * REVS)
            with pe.Fori(0, B - 1) as b:
                batch(b, False)
            batch(B - 1, True)


def kernel(x, L0_conv_base_kernel, L0_conv_ap_w1, L0_conv_ap_b1, L0_conv_ap_w2, L0_conv_ap_b2, L0_conv_meta_w1,
           L0_conv_meta_b1, L0_conv_meta_w2, L0_conv_meta_b2, L1_conv_Wq, L1_conv_bq, L1_conv_Wkv, L1_conv_bkv,
           L1_conv_Wproj, L1_conv_bproj, L1_conv_dwc_w, L1_conv_dwc_b, L1_conv_scale_param):
    import numpy as np
    import concourse.bacc as bacc
    from concourse import mybir as mb
    from concourse.bass_utils import run_bass_kernel_spmd

    B, C, H, W = x.shape
    G, HD = L0_conv_base_kernel.shape[0:2]
    order = np.arange(C).reshape(G, HD).T.reshape(-1)
    wkv, bkv = np.asarray(L1_conv_Wkv), np.asarray(L1_conv_bkv)
    taps = np.asarray(L1_conv_dwc_w).reshape(HD, 5, 5)
    arrays = {
        "x": np.asarray(x).reshape(B, C, H * W),
        "conv_w": np.asarray(L0_conv_base_kernel).transpose(0, 2, 3, 4, 1).reshape(C, 9, HD),
        "mlp_w1": np.concatenate([np.asarray(L0_conv_ap_w1), np.asarray(L0_conv_meta_w1)], 0).T,
        "mlp_b1": np.concatenate([np.asarray(L0_conv_ap_b1), np.asarray(L0_conv_meta_b1)]).reshape(-1, 1),
        "mlp_w2": np.concatenate([np.repeat(np.asarray(L0_conv_ap_w2).T, HD, axis=1),
                                  np.asarray(L0_conv_meta_w2).T], 0),
        "mlp_b2": np.concatenate([np.repeat(np.asarray(L0_conv_ap_b2), HD), np.asarray(L0_conv_meta_b2)]
                                 ).reshape(4, C // 2).T,
        "wqkv": np.concatenate([np.asarray(L1_conv_Wq), wkv[:C], wkv[C:][order]], 0).T,
        "bqkv": np.concatenate([np.asarray(L1_conv_bq), bkv[:C], bkv[C:][order]]).reshape(1, -1),
        "head_scale": np.asarray(L1_conv_scale_param).reshape(1, C),
        "wproj": np.asarray(L1_conv_Wproj).T[order],
        "bproj": np.asarray(L1_conv_bproj).reshape(2, C // 2).T,
        "dw_rows": np.pad(taps[:, :, ::-1], ((0, 0), (1, 1), (61, 62))),
        "dw_taps": taps.reshape(1, -1),
        "dw_b": np.asarray(L1_conv_dwc_b).reshape(1, HD),
    }
    arrays = {n: np.ascontiguousarray(v) for n, v in arrays.items()}
    nc = bacc.Bacc("TRN2", target_bir_lowering=False, num_devices=1)
    args = [nc.dram_tensor(n, v.shape, mb.dt.from_np(v.dtype), kind="ExternalInput").ap() for n, v in arrays.items()]
    out = nc.dram_tensor("out", (B, C, H * W), mb.dt.float32, kind="ExternalOutput").ap()
    conv_then_focused_attention(nc, *args, out)
    r = run_bass_kernel_spmd(nc, [arrays], core_ids=[0])
    return r.results[0]["out"].reshape(B, C, H, W)
```

```python
import concourse.bass as bass
from concourse import mybir
from contextlib import ExitStack


def conv_then_focused_attention(
    nc: bass.Bass,
    x: bass.AP,
    conv_w: bass.AP,
    mlp_w1: bass.AP,
    mlp_b1: bass.AP,
    mlp_w2: bass.AP,
    mlp_b2: bass.AP,
    wqkv: bass.AP,
    bqkv: bass.AP,
    head_scale: bass.AP,
    wproj: bass.AP,
    bproj: bass.AP,
    dw_rows: bass.AP,
    dw_taps: bass.AP,
    dw_b: bass.AP,
    out: bass.AP,
):
    f32, f16 = mybir.dt.float32, mybir.dt.float16
    ALU = mybir.AluOpType
    ACT = mybir.ActivationFunctionType
    AX = mybir.AxisListType
    RMAX = bass.bass_isa.ReduceOp.max

    B, C, N = x.shape
    P = 128
    HALVES = C // P
    IMG = 64
    UNIT = 512
    NU = N // UNIT
    TPU = UNIT // P
    NT = N // P
    HD = 32
    HEADS = C // HD
    HPH = HEADS // HALVES
    TAPS = 9
    STRIP = 16
    NS = IMG // STRIP
    SROWS, SCOLS = STRIP + 2, IMG + 2
    PROWS = SROWS // 2
    NPARTS = 2 * HALVES * NS
    CHUNKS = 2 * HALVES * NS
    PAIRS = 2 * NU
    XS = 64.0
    GN_EPS = 1e-5
    FOCUS_EPS = 1e-6
    TINY = 1e-30
    KVC = P + HPH
    QUARTER_PI = 0.7853981633974483
    HALF_PI = 1.5707963267948966

    ctx = ExitStack()
    with ctx:
        def sb(name, shape, dt=f32):
            return ctx.enter_context(nc.sbuf_tensor(name, shape, dt))

        def pb(name):
            return ctx.enter_context(nc.psum_tensor(name, [P, 512], f32))

        def sem(name):
            return ctx.enter_context(nc.semaphore(name))

        X = sb("X", [P, HALVES, N])
        XHL = sb("XHL", [P, 2, HALVES, N], f16)
        V = sb("V", [P, HD, 2, NT * HEADS], f16)
        FM = V[:, :, :, :].rearrange("p c a n -> p (c a n)").bitcast(f32).rearrange("p (c n) -> p c n", c=HD)
        TP = sb("TP", [P, HD, 3, 2, P], f16)
        WQ = sb("WQ", [P, 2, HALVES, 3 * C], f16)
        BQ = sb("BQ", [P, 3 * C], f16)
        ONES = sb("ONES", [P, P], f16)
        WP = sb("WP", [P, 2, HALVES, C], f16)
        FL = sb("FL", [P, C])
        BD = sb("BD", [P, 2, HALVES, TAPS, P], f16)
        ZEROS = BD[0:32, 0, 0, 0:2, 32:32 + P // 2 + 1]
        KB = sb("KB", [P, HALVES, TAPS, HD])
        W1 = sb("W1", [P, HALVES, P])
        W2 = sb("W2", [P, C])
        GM = sb("GM", [P, P])
        ID = sb("ID", [P, P])
        KVS = sb("KVS", [P, HALVES, KVC])
        COEF = sb("COEF", [P, TAPS, HALVES * TAPS])
        WK = sb("WK", [P, 3 * 1024])
        K0 = WK[:, 0:1024].rearrange("p (a n) -> p a n", a=2)
        K2 = WK[:, 1024:2048].rearrange("p (a n) -> p a n", a=2)
        K3 = WK[:, 2048:3072].rearrange("p (a n) -> p a n", a=2)
        SN = 2 * 2 * SROWS * SCOLS // 2
        S = WK[:, 0:SN].bitcast(f16).rearrange("p (g a r c) -> p g a r c", g=2, a=2, r=SROWS)
        VT = sb("VT", [P, 2, 2, HALVES, P + 2])
        QT = VT[:, :, :, :, :].rearrange("p a b c d -> p (a b c d)")[:, 0:1024].rearrange(
            "p (a h n) -> p a h n", a=2, h=HALVES)
        XN = sb("XN", [P, 2, PROWS * IMG])
        ROT = XN[:, 0, :].rearrange("p (h t o) -> p h t o", h=HALVES, t=TAPS)
        RTMP = XN[:, 1, :].rearrange("p (h t o) -> p h t o", h=HALVES, t=TAPS)
        O = sb("O", [P, 2, 2 * C])
        OT = sb("OT", [P, 2, HALVES, UNIT], f16)
        Y = sb("Y", [P, HALVES, UNIT])
        TR = sb("TR", [P, UNIT])
        B1 = sb("B1", [P, 1])
        B2 = sb("B2", [P, 2, HALVES])
        BP = sb("BP", [P, HALVES])
        DWB = sb("DWB", [P, HD])
        CK = sb("CK", [P, 2])
        XX = sb("XX", [P, 2, TAPS])
        ST = sb("ST", [P, HALVES, NU, 6])
        MV = sb("MV", [P, HALVES, 2])
        GS = sb("GS", [P, 8, HALVES])
        MEAN, DEV, SPREAD, VAR, ROOT, STD, RSTD, POOLED = (GS[:, i, :] for i in range(8))
        PR = sb("PR", [P, 9, HALVES])
        SC0, BI0, SC1, BI1, MODA, STDN, CBN, STDC, CBC = (PR[:, i, :] for i in range(9))
        HID = sb("HID", [P, 3])
        ZB = sb("ZB", [P, 4, HALVES])
        SIN = sb("SIN", [P, 3, HALVES])
        TT = sb("TT", [P, 2, HALVES, TAPS])
        TW = sb("TW", [P, 3, 2, HALVES * TAPS])
        S2 = sb("S2", [P, TPU])
        S6 = sb("S6", [P, TPU])
        RATIO = sb("RATIO", [P, 2, TPU])
        NORM = sb("NORM", [P, TPU])
        Z = sb("Z", [P, 2, HEADS])
        SCAL = sb("SCAL", [P, 24])

        def col(i):
            return SCAL[:, i:i + 1]
        (m_w, m_v, m_k, m_p) = (col(i) for i in range(4))
        (m_b, m_bv, m_db, s_t, m_t, a_w, inv_a, inv_a2, den_eps, a_v, v_fac, a_t, fm_fac, a_o, a_p, out_fac,
         a_r, conv_fac, v_bound, spare) = (col(4 + i) for i in range(20))

        F = [pb("F0"), pb("F1")]
        VAB = ctx.enter_context(nc.psum_tensor("VAB", [P, 2, 512], f32))
        VA = [VAB[:, 0, :], VAB[:, 1, :]]
        T = [pb("T0"), pb("T1")]
        PP = pb("PP")
        DW = [F[0], F[1], VA[0], VA[1]]
        SM = pb("SM")

        w_in = sem("w_in")
        taps_in = sem("taps_in")
        x_in = sem("x_in")
        y_out = [sem("y_out0"), sem("y_out1")]
        set_dve = sem("set_dve")
        set_act = sem("set_act")
        soft_rdy = sem("soft_rdy")
        set_pool = sem("set_pool")
        rev_full = sem("rev_full")
        tp_act = sem("tp_act")
        tp_dve = sem("tp_dve")
        stats_rdy = sem("stats_rdy")
        z_rdy = sem("z_rdy")
        carried = sem("carried")
        ready = sem("ready")
        chain = sem("chain")
        mean_rdy, mean_mm = sem("mean_rdy"), sem("mean_mm")
        spread_rdy, spread_mm = sem("spread_rdy"), sem("spread_mm")
        var_rdy, root_rdy = sem("var_rdy"), sem("root_rdy")
        norm_rdy = sem("norm_rdy")
        pooled_rdy, hid_mm = sem("pooled_rdy"), sem("hid_mm")
        hid_rdy, z_mm = sem("hid_rdy"), sem("z_mm")
        zb_rdy, trig_rdy = sem("zb_rdy"), sem("trig_rdy")
        squash_rdy = sem("squash_rdy")
        rot_rdy, bd_hi, bd_lo = sem("rot_rdy"), sem("bd_hi"), sem("bd_lo")
        xn_rdy, h_rdy, l_rdy = sem("xn_rdy"), sem("h_rdy"), sem("l_rdy")
        border = sem("border")
        conv_full, x1_rdy = sem("conv_full"), sem("x1_rdy")
        f_full, f_max, f_sq = sem("f_full"), sem("f_max"), sem("f_sq")
        f_cube, f_six, f_ratio, f_root = sem("f_cube"), sem("f_six"), sem("f_ratio"), sem("f_root")
        k_scaled, cube_used = sem("k_scaled"), sem("cube_used")
        v_full, v_hi, v_true, v_lo = sem("v_full"), sem("v_hi"), sem("v_true"), sem("v_lo")
        ones_rdy = sem("ones_rdy")
        state_full, state_rdy = sem("state_full"), sem("state_rdy")
        dw_full, fm_rdy = sem("dw_full"), sem("fm_rdy")
        qt_rdy, attn_full, o_rdy = sem("qt_rdy"), sem("attn_full"), sem("o_rdy")
        ot_full, oh_rdy, ol_rdy = sem("ot_full"), sem("oh_rdy"), sem("ol_rdy")
        y_full, y_act, y_rdy = sem("y_full"), sem("y_act"), sem("y_rdy")
        tr_rdy, kept = sem("tr_rdy"), sem("kept")

        L_CR, X1_CR, MAX_CR, CUBE_CR, USED_CR, SIX_CR = 2, 2, 2, 2, 2, 4
        VLO_CR, FM_CR, O_CR, OL_CR, YA_CR = 2, 4, 2, 2, 2
        Y_CR, AT_CR, OUT_CR, QT_CR = 1, 1, 1, 1
        N_W = 12
        N_CHAIN = 59

        block = ctx.enter_context(nc.Block())

        VF = V[:, :, :, :].rearrange("p c a n -> p (c a n)").bitcast(f32)
        wq32 = VF[:, 0:1536].rearrange("p (h n) -> p h n", h=HALVES)
        bq32 = VF[:, 1536:2304]
        sc32 = VF[:, 2304:2560]
        wp32 = VF[:, 2560:3072].rearrange("p (h n) -> p h n", h=HALVES)
        dt32 = VF[:, 3072:3872]
        W_A, W_B, W_C, W_D, W_E, W_F = (VF[:, 4096 + 256 * i:4352 + 256 * i] for i in range(6))
        bh16 = VF[:, 6144:6528].bitcast(f16)
        bl16 = VF[:, 6528:6912].bitcast(f16)
        dsum = VF[:, 6912:6944]
        CH2 = HD // 2
        TS = XHL[:, :, :, :].rearrange("p a h n -> p (a h n)").bitcast(f32)[:, 0:CH2 * 3 * P].rearrange(
            "p (c k n) -> p c k n", c=CH2, k=3)

        REVS = CH2 * 3 * P // 512
        REV = XN[:, 1, 0:P]
        TPM = TP[:, :, :, :, :].rearrange("p c k a n -> p (c k) a n")

        def strip_rows(s, p):
            lo, hi = PROWS * p, PROWS * (p + 1)
            if s == 0 and p == 0:
                lo = 1
            if s == NS - 1 and p == 1:
                hi -= 1
            return lo, hi, STRIP * s - 1 + lo

        def alive(u):
            return lambda d: 0 <= 2 * u + d < PAIRS

        def always(d):
            return True

        def carry(eng):
            eng.sem_inc(carried, 1)

        @block.sync
        def _(sp):
            for h in range(HALVES):
                sp.sem_inc(y_out[h], 16 * OUT_CR)
            sp.dma_start(wq32, wqkv.rearrange("(h p) n -> p h n", p=P)).then_inc(w_in, 16)
            sp.dma_start(bq32, bqkv[0, :].partition_broadcast(P)).then_inc(w_in, 16)
            sp.dma_start(sc32, head_scale[0, :].partition_broadcast(P)).then_inc(w_in, 16)
            sp.dma_start(wp32, wproj.rearrange("(h p) n -> p h n", p=P)).then_inc(w_in, 16)
            sp.dma_start(dt32, dw_taps[0, :].partition_broadcast(P)).then_inc(w_in, 16)
            sp.dma_start(DWB[:, :], dw_b[0, :].partition_broadcast(P)).then_inc(w_in, 16)
            sp.dma_start(KB[:, :, :, :], conv_w.rearrange("(h p) t o -> p h t o", p=P)).then_inc(w_in, 16)
            sp.dma_start(W1[:, :, :], mlp_w1.rearrange("(h p) n -> p h n", p=P)).then_inc(w_in, 16)
            sp.dma_start(W2[:, :], mlp_w2).then_inc(w_in, 16)
            sp.dma_start(B1[:, :], mlp_b1).then_inc(w_in, 16)
            sp.dma_start(B2[:, :, :].rearrange("p k h -> p (k h)"), mlp_b2).then_inc(w_in, 16)
            sp.dma_start(BP[:, :], bproj).then_inc(w_in, 16)
            xv = x.rearrange("b (h p) n -> b p h n", p=P)
            ov = out.rearrange("b (h p) n -> b p h n", p=P)

            def load(c, u):
                sp.dma_start(X[:, :, bass.ds(u * UNIT, UNIT)],
                             xv[bass.ds(c, 1), :, :, bass.ds(u * UNIT, UNIT)].rearrange("b p h n -> p (b h) n")
                             ).then_inc(x_in, 16)

            def store(b, u):
                for h in range(HALVES):
                    sp.wait_ge(y_rdy, (b * NU + u) * HALVES + h + 1 + Y_CR)
                    sp.dma_start(ov[bass.ds(b, 1), :, h, bass.ds(u * UNIT, UNIT)].rearrange("b p n -> p (b n)"),
                                 Y[:, h, :]).then_inc(y_out[h], 16)

            def load_next(c, u):
                sp.wait_ge(xn_rdy, (c - 1) * 2 * NPARTS + NPARTS + HALVES * (u + 1))
                load(c, u)

            with sp.Fori(0, NU) as u:
                load(0, u)
            for rnd in range(2):
                if rnd == 1:
                    sp.wait_ge(rev_full, REVS)
                for rin in range(2):
                    for rout in range(2):
                        for k in range(3):
                            dy = 2 * (k - 1) + rin - rout + 3
                            src = bass.AP(dw_rows.tensor, (rnd * CH2 * 7 + dy) * P,
                                          [[1, IMG], [7 * P, CH2], [1, IMG]])
                            sp.dma_start(TS[IMG * rin:IMG * (rin + 1), :, k, IMG * rout:IMG * (rout + 1)],
                                         src).then_inc(taps_in, 16)
            with sp.Fori(0, NU) as u:
                load_next(1, u)
            with sp.Fori(0, B - 2) as b:
                with sp.Fori(0, NU) as u:
                    store(b, u)
                    load_next(b + 2, u)
            for b in (B - 2, B - 1):
                with sp.Fori(0, NU) as u:
                    store(b, u)
            for h in range(HALVES):
                sp.wait_ge(y_out[h], 16 * (B * NU + OUT_CR))

        @block.gpsimd
        def _(pool):
            g = nc.gpsimd
            g.memset(ID[:, :], 0.0).then_inc(set_pool, 1)
            g.memset(GM[:, :], 1.0 / 8).then_inc(set_pool, 1)
            pool.wait_ge(set_pool, 2)
            g.affine_select(out=ID[:, :], in_=ID[:, :], compare_op=ALU.not_equal, fill=1.0, base=0,
                            pattern=[[-1, P]], channel_multiplier=1).then_inc(set_pool, 1)
            gv = GM[:, :].rearrange("p (g e) -> p g e", e=8)
            g.affine_select(out=gv, in_=gv, compare_op=ALU.is_ge, fill=0.0, base=0,
                            pattern=[[-8, P // 8], [0, 8]], channel_multiplier=1).then_inc(set_pool, 1)
            pool.wait_ge(set_pool, 4)
            g.affine_select(out=gv, in_=gv, compare_op=ALU.is_ge, fill=0.0, base=7,
                            pattern=[[8, P // 8], [0, 8]], channel_multiplier=-1).then_inc(set_pool, 1)
            g.memset(REV, 0.0).then_inc(set_pool, 1)
            for k in (IMG - 1, 3 * IMG - 1):
                pool.wait_ge(set_pool, 6 + k // IMG // 2)
                g.affine_select(out=REV, in_=REV, compare_op=ALU.not_equal, fill=1.0, base=-k,
                                pattern=[[1, P]], channel_multiplier=1).then_inc(set_pool, 1)
            pool.wait_ge(set_dve, 1)
            g.partition_all_reduce(SCAL[:, 0:4], S6[:, 0:4], P, RMAX).then_inc(set_pool, 1)
            pool.sem_inc(l_rdy, L_CR)
            pool.wait_ge(ready, 1)

            def low(n, dst, hi, src):
                pool.wait_ge(xn_rdy, n + 1)
                pool.wait_ge(h_rdy, n + 1)
                carry(pool)
                g.tensor_tensor(dst, src, hi, ALU.subtract).then_inc(l_rdy, 1)

            def conv_inputs(c, first):
                if not first:
                    pool.wait_ge(cube_used, (c - 1) * 2 * PAIRS + PAIRS + USED_CR)
                    carry(pool)
                for h in range(HALVES):
                    for s in range(NS):
                        i = h * NS + s
                        gi = c * HALVES * NS + i
                        if not first or i >= 2:
                            pool.wait_ge(conv_full, 2 * gi - 2)
                            carry(pool)
                        buf = S[:, i % 2, :, :, :]
                        for e in (0, SCOLS - 1):
                            g.memset(buf[:, :, :, e:e + 1], 0.0).then_inc(border, 1)
                        if s in (0, NS - 1):
                            edge = 0 if s == 0 else SROWS - 1
                            g.memset(buf[:, :, edge, 1:SCOLS - 1], 0.0).then_inc(border, 1)
                        else:
                            pool.sem_inc(border, 1)
                        for p in range(2):
                            lo, hi, _ = strip_rows(s, p)
                            low(c * 2 * NPARTS + 2 * i + p, buf[:, 1, lo:hi, 1:SCOLS - 1],
                                buf[:, 0, lo:hi, 1:SCOLS - 1],
                                XN[:, p, 0:(hi - lo) * IMG].rearrange("p (r c) -> p r c", c=IMG))

            def attn_input(c, u, h):
                low(c * 2 * NPARTS + NPARTS + HALVES * u + h, XHL[:, 1, h, bass.ds(u * UNIT, UNIT)],
                    XHL[:, 0, h, bass.ds(u * UNIT, UNIT)], XN[:, h, 0:UNIT])

            def add_depthwise(b, u, p):
                m = b * PAIRS + 2 * u + p
                pool.wait_ge(z_rdy, 4 * m + 4)
                carry(pool)
                o = O[:, p, :].rearrange("p (t c e) -> p t c e", t=2, c=HD)
                fm = FM[:, :, bass.ds((u * TPU + 2 * p) * HEADS, 2 * HEADS)].rearrange("p c (t e) -> p t c e", t=2)
                g.tensor_tensor(o, o, fm, ALU.add).then_inc(o_rdy, 2)

            def residual(b, u, h):
                pool.wait_ge(y_rdy, (b * NU + u) * HALVES + h + Y_CR)
                carry(pool)
                g.tensor_tensor(TR[:, :], XHL[:, 0, h, bass.ds(u * UNIT, UNIT)],
                                XHL[:, 1, h, bass.ds(u * UNIT, UNIT)], ALU.add).then_inc(tr_rdy, 1)

            def ones():
                g.memset(VT[:, :, :, :, P:P + 1], 1.0).then_inc(ones_rdy, 1)

            def batch(b, last):
                if not last:
                    conv_inputs(b + 1, False)

                def step(u, add, rest, end=False):
                    for p in range(2):
                        if rest and not (end and p == 1):
                            residual(b, u - 3 + p, 1 - p)
                        if add:
                            add_depthwise(b, u - 1, p)
                        if rest and not last:
                            attn_input(b + 1, u - 3, p)

                residual(b, 0, 0)
                pool.wait_ge(fm_rdy, HD * (b + 1) + FM_CR)
                for u in (1, 2):
                    step(u, True, False)
                with pool.Fori(3, NU + 1) as u:
                    step(u, True, True)
                if not last:
                    pool.wait_ge(attn_full, (b + 1) * NT + AT_CR)
                    carry(pool)
                    ones()
                for u in (NU + 1, NU + 2):
                    step(u, False, True, u == NU + 2)

            ones()
            conv_inputs(0, True)
            with pool.Fori(0, NU) as u:
                for h in range(HALVES):
                    attn_input(0, u, h)
            with pool.Fori(0, B - 1) as b:
                batch(b, False)
            batch(B - 1, True)

        @block.vector
        def _(dve):
            v = nc.vector
            steps = [0, 0]

            def setup(ins):
                steps[0] += 1
                ins.then_inc(chain, 1)
                dve.wait_ge(chain, steps[0])

            for t in (ONES, BQ, KVS, BD, HID):
                setup(v.memset(t[:], XS if t is ONES else 0.0))
            setup(v.memset(CK[:, :], HALF_PI))
            for t in range(TAPS):
                setup(v.memset(XX[:, 0, t:t + 1], float(t % 3 - 1)))
                setup(v.memset(XX[:, 1, t:t + 1], float(t // 3 - 1)))
            for s, n in ((x1_rdy, X1_CR), (f_max, MAX_CR), (f_cube, CUBE_CR), (v_lo, VLO_CR), (o_rdy, O_CR),
                         (ol_rdy, OL_CR), (cube_used, USED_CR),
                         (y_rdy, Y_CR), (attn_full, AT_CR), (qt_rdy, QT_CR)):
                dve.sem_inc(s, n)
            dve.wait_ge(w_in, 16 * N_W)
            setup(v.tensor_scalar(W_A, sc32, -1.0, None, ALU.mult))
            setup(v.tensor_tensor(W_A, W_A, sc32, ALU.min))
            dve.sem_inc(soft_rdy, 1)
            dve.wait_ge(set_act, 1)
            v.tensor_scalar(W_D, W_C, 1.0, None, ALU.add).then_inc(soft_rdy, 1)
            dve.wait_ge(soft_rdy, 2)
            setup(v.tensor_scalar(W_B, W_D, -1.0, None, ALU.add))
            setup(v.tensor_scalar(W_F, W_B, 0.0, None, ALU.is_equal))
            setup(v.tensor_tensor(W_B, W_B, W_F, ALU.add))
            setup(v.reciprocal(W_B, W_B))
            setup(v.tensor_tensor(W_B, W_B, W_C, ALU.mult))
            dve.wait_ge(set_act, 2)
            setup(v.tensor_tensor(W_B, W_B, W_E, ALU.mult))
            setup(v.tensor_tensor(W_F, W_F, W_C, ALU.mult))
            setup(v.tensor_tensor(W_B, W_B, W_F, ALU.add))
            setup(v.tensor_scalar(W_A, sc32, 0.0, None, ALU.max))
            setup(v.tensor_tensor(W_B, W_B, W_A, ALU.add))
            setup(v.reciprocal(W_B, W_B))
            for h in range(HALVES):
                for j in range(2):
                    cs = slice(j * C, (j + 1) * C)
                    setup(v.tensor_tensor(wq32[:, h, cs], wq32[:, h, cs], W_B, ALU.mult))
            for j in range(2):
                cs = slice(j * C, (j + 1) * C)
                setup(v.scalar_tensor_tensor(bq32[:, cs], bq32[:, cs], FOCUS_EPS, W_B, ALU.add, ALU.mult))
            for dst, src in ((S6[:, 0:1], wq32), (S6[:, 1:2], wq32[:, :, 2 * C:3 * C]), (S6[:, 3:4], wp32)):
                setup(v.tensor_reduce(dst, src, AX.XY, ALU.max, apply_absolute_value=True))
            setup(v.tensor_reduce(S6[:, 2:3], KB[:, :, :, :].rearrange("p h t o -> p (h t o)"), AX.X, ALU.max,
                                  apply_absolute_value=True))
            setup(v.tensor_reduce(m_b, bq32, AX.X, ALU.max, apply_absolute_value=True))
            setup(v.tensor_reduce(m_bv, bq32[:, 2 * C:3 * C], AX.X, ALU.max, apply_absolute_value=True))
            setup(v.tensor_reduce(m_db, DWB[:, :], AX.X, ALU.max, apply_absolute_value=True))
            setup(v.tensor_reduce(m_t, dt32, AX.X, ALU.max, apply_absolute_value=True))
            setup(v.tensor_reduce(dsum, dt32.rearrange("p (c t) -> p c t", c=HD), AX.X, ALU.add,
                                  apply_absolute_value=True))
            setup(v.tensor_reduce(s_t, dsum, AX.X, ALU.max))
            dve.sem_inc(set_dve, 1)
            dve.wait_ge(set_pool, 9)

            def over(dst, src, top):
                setup(v.tensor_scalar(dst, src, TINY, None, ALU.max))
                setup(v.reciprocal(dst, dst))
                if top != 1.0:
                    setup(v.tensor_scalar(dst, dst, top, None, ALU.mult))

            setup(v.tensor_tensor(m_w, m_w, m_b, ALU.max))
            over(a_w, m_w, 16384.0)
            setup(v.tensor_scalar(inv_a, a_w, XS, None, ALU.mult))
            setup(v.tensor_scalar(den_eps, inv_a, FOCUS_EPS, None, ALU.mult))
            setup(v.tensor_tensor(den_eps, den_eps, den_eps, ALU.mult))
            setup(v.reciprocal(inv_a, inv_a))
            setup(v.tensor_tensor(inv_a2, inv_a, inv_a, ALU.mult))
            setup(v.tensor_scalar(v_bound, m_v, 16600.0, m_bv, ALU.mult, ALU.add))
            over(a_v, v_bound, 32768.0)
            setup(v.tensor_tensor(v_fac, inv_a, a_v, ALU.mult))
            over(a_t, m_t, 16384.0)
            setup(v.tensor_tensor(fm_fac, a_v, a_t, ALU.mult))
            setup(v.reciprocal(fm_fac, fm_fac))
            setup(v.tensor_scalar(spare, s_t, 1.0, None, ALU.add))
            setup(v.tensor_scalar(spare, spare, v_bound, m_db, ALU.mult, ALU.add))
            over(a_o, spare, 32768.0)
            over(a_p, m_p, 16384.0)
            setup(v.tensor_tensor(out_fac, a_o, a_p, ALU.mult))
            setup(v.reciprocal(out_fac, out_fac))
            over(a_r, m_k, 4096.0)
            setup(v.tensor_scalar(conv_fac, a_r, XS, None, ALU.mult))
            setup(v.reciprocal(conv_fac, conv_fac))
            setup(v.tensor_scalar(spare, a_w, XS * FOCUS_EPS, None, ALU.mult))
            setup(v.tensor_scalar(FL[:, :], W_B, spare, None, ALU.mult))
            setup(v.tensor_scalar(KB[:, :, :, :], KB[:, :, :, :], a_r, None, ALU.mult))
            for src, hi, lo, a in ((wq32, WQ[:, 0], WQ[:, 1], a_w), (wp32, WP[:, 0], WP[:, 1], a_p),
                                   (bq32, bh16, bl16, a_w)):
                setup(v.tensor_scalar(src, src, a, None, ALU.mult))
                setup(v.tensor_copy(hi, src))
                setup(v.tensor_tensor(lo, src, hi, ALU.subtract))
            setup(v.tensor_copy(BQ[0:1, :], bh16[0:1, :]))
            setup(v.tensor_copy(BQ[32:33, :], bl16[32:33, :]))
            dve.sem_inc(ready, 1)
            for i in range(2 * REVS):
                dve.wait_ge(tp_act, i + 1)
                hi, lo = (TPM[:, 4 * i:4 * i + 4, j, :] for j in range(2))
                v.scalar_tensor_tensor(lo, F[i % 2][:, :].rearrange("p (m n) -> p m n", m=4), a_t, hi, ALU.mult,
                                       ALU.subtract).then_inc(tp_dve, 1)
            base = steps[0]

            def link(c, ins):
                steps[1] += 1
                ins.then_inc(chain, 1)
                dve.wait_ge(chain, c * N_CHAIN + base + steps[1])

            def means(c, layer):
                dve.wait_ge(stats_rdy, (2 * c + layer + 1) * HALVES * NU)
                carry(dve)
                steps[1] += 1
                v.bn_aggr(MV[:, 0, :], ST[:, 0, :, :].rearrange("p u s -> p (u s)")).then_inc(chain, 1)
                link(c, v.bn_aggr(MV[:, 1, :], ST[:, 1, :, :].rearrange("p u s -> p (u s)")))
                v.tensor_copy(DEV, MV[:, :, 0]).then_inc(mean_rdy, 1)

            def spreads(c, layer):
                dve.wait_ge(mean_mm, 2 * c + layer + 1)
                link(c, v.tensor_copy(MEAN, SM[:, 0:2]))
                link(c, v.tensor_tensor(DEV, DEV, MEAN, ALU.subtract))
                link(c, v.tensor_tensor(SPREAD, DEV, DEV, ALU.mult))
                v.tensor_tensor(SPREAD, SPREAD, MV[:, :, 1], ALU.add).then_inc(spread_rdy, 1)

            def variance(c, layer):
                dve.wait_ge(spread_mm, 2 * c + layer + 1)
                v.tensor_scalar(VAR, SM[:, 2:4], GN_EPS, None, ALU.add).then_inc(var_rdy, 1)

            def scale_and_bias(c, layer):
                dve.wait_ge(root_rdy, 2 * c + layer + 1)
                link(c, v.reciprocal(STD, ROOT))
                link(c, v.tensor_tensor(STD, STD, VAR, ALU.mult))
                link(c, v.tensor_tensor(STD, STD, ROOT, ALU.add))
                link(c, v.tensor_scalar(STD, STD, 0.5, None, ALU.mult))
                link(c, v.reciprocal(RSTD, STD))
                sc, bi = (SC0, BI0) if layer == 0 else (SC1, BI1)
                link(c, v.tensor_scalar(sc, RSTD, XS, None, ALU.mult))
                if layer == 1:
                    link(c, v.tensor_scalar(STDN, STD, 1.0 / XS, None, ALU.mult))
                    link(c, v.tensor_tensor(CBN, MEAN, BP[:, :], ALU.add))
                else:
                    v.tensor_tensor(POOLED, DEV, RSTD, ALU.mult).then_inc(pooled_rdy, 1)
                v.scalar_tensor_tensor(bi, MEAN, -1.0, sc, ALU.mult, ALU.mult).then_inc(norm_rdy, 1)

            def hidden(c):
                dve.wait_ge(hid_mm, c + 1)
                link(c, v.tensor_tensor(HID[:, 2:3], SM[:, 4:5], B1[:, :], ALU.add))
                for k in range(2):
                    r = slice(64 * k, 64 * k + 64)
                    v.tensor_scalar(HID[r, k:k + 1], HID[r, 2:3], 0.0, None, ALU.max).then_inc(hid_rdy, 1)

            def heads(c):
                dve.wait_ge(z_mm, c + 1)
                v.tensor_tensor(ZB[:, 0:2, :], SM[:, 8:12].rearrange("p (h k) -> p k h", k=2), B2[:, :, :],
                                ALU.add).then_inc(zb_rdy, 1)

            def rotation(c):
                dve.wait_ge(trig_rdy, 2 * (c + 1))
                link(c, v.tensor_scalar(MODA, ZB[:, 3, :], conv_fac, None, ALU.mult))
                link(c, v.tensor_scalar(SIN[:, 2, :], SIN[:, 0, :], -1.0, None, ALU.mult))
                for k in range(2):
                    for h in range(HALVES):
                        link(c, v.tensor_scalar(TT[:, k, h, :], XX[:, k, :], SIN[:, 1, h:h + 1], None, ALU.mult))
                for k in range(2):
                    for h in range(HALVES):
                        s = SIN[:, 0, h:h + 1] if k == 0 else SIN[:, 2, h:h + 1]
                        link(c, v.scalar_tensor_tensor(TT[:, k, h, :], XX[:, 1 - k, :], s, TT[:, k, h, :],
                                                       ALU.mult, ALU.add))
                tt = TT[:, :, :, :].rearrange("p k h t -> p k (h t)")
                link(c, v.tensor_scalar(TW[:, 0], tt, -1.0, 0.0, ALU.mult, ALU.max))
                link(c, v.tensor_scalar(TW[:, 2], tt, 0.0, None, ALU.max))
                link(c, v.tensor_tensor(TW[:, 1], TW[:, 0], TW[:, 2], ALU.add))
                link(c, v.tensor_scalar(TW[:, 1], TW[:, 1], -1.0, 1.0, ALU.mult, ALU.add))
                for jy in range(3):
                    wy = TW[:, jy, 1, :].unsqueeze(1).broadcast_to([P, 3, HALVES * TAPS])
                    link(c, v.tensor_tensor(COEF[:, 3 * jy:3 * jy + 3, :], wy, TW[:, :, 0, :], ALU.mult))
                for j in range(TAPS):
                    cj = COEF[:, j, :].rearrange("p (h t) -> p h t", h=HALVES).unsqueeze(3).broadcast_to(
                        [P, HALVES, TAPS, HD])
                    kj = KB[:, :, j, :].unsqueeze(2).broadcast_to([P, HALVES, TAPS, HD])
                    link(c, v.tensor_tensor(ROT if j == 0 else RTMP, cj, kj, ALU.mult))
                    if j:
                        link(c, v.tensor_tensor(ROT, ROT, RTMP, ALU.add))
                dve.sem_inc(rot_rdy, 1)
                dve.wait_ge(bd_hi, 4 * (c + 1))
                for q in range(4):
                    r = slice(32 * q, 32 * q + 32)
                    v.tensor_tensor(BD[r, 1, :, :, r], ROT[r], BD[r, 0, :, :, r], ALU.subtract).then_inc(bd_lo, 1)

            def x_stats(c, u):
                for h in range(HALVES):
                    v.bn_stats(ST[:, h, bass.ds(u, 1), :].rearrange("p u s -> p (u s)"),
                               X[:, h, bass.ds(u * UNIT, UNIT)]).then_inc(stats_rdy, 1)

            def conv_steps(c, first):
                if not first:
                    dve.wait_ge(cube_used, (c - 1) * 2 * PAIRS + PAIRS + USED_CR)

                def high(i):
                    s = i % NS
                    if not first or i >= 2:
                        dve.wait_ge(conv_full, 2 * (c * HALVES * NS + i) - 2)
                    for p in range(2):
                        n = c * 2 * NPARTS + 2 * i + p
                        lo, hi, _ = strip_rows(s, p)
                        dve.wait_ge(xn_rdy, n + 1)
                        v.tensor_copy(S[:, i % 2, 0, lo:hi, 1:SCOLS - 1],
                                      XN[:, p, 0:(hi - lo) * IMG].rearrange("p (r c) -> p r c", c=IMG)
                                      ).then_inc(h_rdy, 1)

                def evacuate(i):
                    h, s = divmod(i, NS)
                    for q in range(2):
                        n = c * CHUNKS + 2 * i + q
                        tok = slice((2 * s + q) * UNIT, (2 * s + q + 1) * UNIT)
                        dve.wait_ge(conv_full, n + 1)
                        v.scalar_tensor_tensor(X[:, h, tok], VA[q][:, :], MODA[:, h:h + 1], X[:, h, tok],
                                               ALU.mult, ALU.add).then_inc(x1_rdy, 1)
                        dve.wait_ge(x1_rdy, n + 1 + X1_CR)
                        v.bn_stats(ST[:, h, 2 * s + q, :], X[:, h, tok]).then_inc(stats_rdy, 1)

                high(0)
                for i in range(1, HALVES * NS):
                    high(i)
                    evacuate(i - 1)
                evacuate(HALVES * NS - 1)

            def attn_input(c, u, h, first):
                n = c * 2 * NPARTS + NPARTS + HALVES * u + h
                if not first:
                    dve.wait_ge(tr_rdy, ((c - 1) * NU + u) * HALVES + h + 1)
                    dve.wait_ge(f_full, (c - 1) * 2 * PAIRS + PAIRS + 2 * (u + 1))
                dve.wait_ge(xn_rdy, n + 1)
                v.tensor_copy(XHL[:, 0, h, bass.ds(u * UNIT, UNIT)], XN[:, h, 0:UNIT]).then_inc(h_rdy, 1)

            def floor_max(n, p):
                dve.wait_ge(f_full, n + 1)
                fl = FL[:, :].unsqueeze(1).broadcast_to([P, 2, C])
                v.tensor_tensor(K0[:, p, :].rearrange("p (t n) -> p t n", t=2),
                                F[p][:, :].rearrange("p (t n) -> p t n", t=2), fl, ALU.max).then_inc(f_max, 1)

            def cube(n, p):
                dve.wait_ge(f_sq, 2 * (n + 1))
                dve.wait_ge(cube_used, n + 1)
                dve.wait_ge(f_six, 2 * n + 2)
                v.tensor_tensor(K3[:, p, :], K2[:, p, :], K0[:, p, :], ALU.mult).then_inc(f_cube, 1)

            def ratio(n, p, a, b):
                cs = slice(2 * p, 2 * p + 2)
                dve.wait_ge(f_six, 2 * (n + 1) + SIX_CR)
                v.reciprocal(RATIO[:, 1, cs], b[:, cs]).then_inc(f_ratio, 1)
                dve.wait_ge(f_ratio, 2 * n + 1)
                v.tensor_tensor(RATIO[:, 0, cs], a[:, cs], RATIO[:, 1, cs], ALU.mult).then_inc(f_ratio, 1)

            def scale_k(n, p):
                dve.wait_ge(f_root, n + 1)
                for t in range(2):
                    ks = K3[:, p, t * C:(t + 1) * C]
                    v.tensor_scalar(ks, ks, NORM[:, 2 * p + t:2 * p + t + 1], None, ALU.mult).then_inc(k_scaled, 1)

            def low_v(b, u, p):
                m = b * PAIRS + 2 * u + p
                dve.wait_ge(v_hi, m + 1)
                dve.wait_ge(v_true, m + 1)
                for t in range(2):
                    dst = bass.ds((u * TPU + 2 * p + t) * HEADS, HEADS)
                    last = v.scalar_tensor_tensor(
                        V[:, :, 1, dst], VA[p][:, t * C:(t + 1) * C].rearrange("p (c h) -> p c h", c=HD), v_fac,
                        V[:, :, 0, dst], ALU.mult, ALU.subtract)
                last.then_inc(v_lo, 1)

            def step_kv(b, u, p):
                n = b * 2 * PAIRS + 2 * u + p
                floor_max(n, p)
                ratio(n - 1, 1 - p, S2, S6)
                low_v(b, u - 1 + p, 1 - p)
                scale_k(n - 1, 1 - p)
                cube(n, p)

            def keep(b):
                dve.wait_ge(y_rdy, b * NU * HALVES + Y_CR)
                v.tensor_copy(PR[:, 7:9, :], PR[:, 5:7, :]).then_inc(kept, 1)

            def state(b):
                dve.wait_ge(state_full, b + 1)
                for h in range(HALVES):
                    o_v, o_d = (HPH, 0) if h == 0 else (0, P)
                    for q in range(HPH):
                        r = slice(32 * q, 32 * q + 32)
                        v.tensor_copy(KVS[r, h, o_v + q:o_v + P:HPH], T[h][r, q:P:HPH]).then_inc(state_rdy, 1)
                        v.tensor_copy(KVS[r, h, o_d + q:o_d + q + 1], T[h][r, P:P + 1]).then_inc(state_rdy, 1)

            zh = Z[:, :, :].rearrange("p t (h f) -> p t h f", h=HALVES)

            def denominators(b, u, p):
                m = b * PAIRS + 2 * u + p
                dve.wait_ge(attn_full, 2 * (m + 1) + AT_CR)
                dve.wait_ge(f_root, b * 2 * PAIRS + PAIRS + 2 * u + p + 1)
                av = VAB[:, :, :]
                den = bass.AP(av.tensor, av.offset, [list(av.ap[0]), [512, 2], [KVC + P, HALVES], [1, HPH]])
                eps = NORM[:, 2 * p:2 * p + 2].unsqueeze(2).unsqueeze(3).broadcast_to([P, 2, HALVES, HPH])
                v.tensor_tensor(zh, den, eps, ALU.add).then_inc(z_rdy, 1)

            def inverses(b, u, p):
                m = b * PAIRS + 2 * u + p
                dve.wait_ge(z_rdy, 4 * m + 1)
                v.reciprocal(Z[:, :, :], Z[:, :, :]).then_inc(z_rdy, 1)

            def quotients(b, u, p):
                m = b * PAIRS + 2 * u + p
                dve.wait_ge(z_rdy, 4 * m + 2)
                for t in range(2):
                    v.tensor_tensor(O[:, p, t * C:(t + 1) * C].rearrange("p (c h f) -> p h c f", c=HD, h=HALVES),
                                    VA[t][:, HPH:HPH + C].rearrange("p (h c f) -> p h c f", h=HALVES, c=HD),
                                    zh[:, t].unsqueeze(2).broadcast_to([P, HALVES, HD, HPH]), ALU.mult
                                    ).then_inc(z_rdy, 1)

            def finish(b, u, h):
                e = (b * NU + u) * HALVES + h
                dve.wait_ge(y_act, e + 1 + YA_CR)
                dve.wait_ge(tr_rdy, e + 1)
                v.scalar_tensor_tensor(Y[:, h, :], TR[:, :], STDC[:, h:h + 1], Y[:, h, :], ALU.mult,
                                       ALU.add).then_inc(y_rdy, 1)

            def low_out(b, u, p):
                m = b * PAIRS + 2 * u + p
                dve.wait_ge(oh_rdy, m + 1)
                hi, lo = (OT[:, i, :, 2 * P * p:2 * P * (p + 1)] for i in range(2))
                v.scalar_tensor_tensor(lo, T[1][:, :].rearrange("p (h n) -> p h n", h=HALVES), a_o, hi, ALU.mult,
                                       ALU.subtract).then_inc(ol_rdy, 1)

            def step_q(b, u, p, live, nxt, keys=False):
                n = b * 2 * PAIRS + PAIRS + 2 * u + p
                if live(p - 4):
                    low_out(b, u - 2, p)
                if live(p) or keys:
                    floor_max(n, p)
                if live(p - 1):
                    ratio(n - 1, 1 - p, S6, S2)
                elif keys:
                    ratio(n - 1, 1 - p, S2, S6)
                if live(-6):
                    finish(b, u - 3, p)
                if live(p - 2):
                    denominators(b, u - 1, p)
                if live(p) or keys:
                    cube(n, p)
                if live(p - 2):
                    inverses(b, u - 1, p)
                if live(p - 2):
                    quotients(b, u - 1, p)
                if nxt:
                    attn_input(b + 1, u - 3, p, False)
                if keys and p == 1:
                    scale_k(n - 1, 0)

            def batch(b, last):
                keep(b)
                low_v(b, 0, 0)
                if not last:
                    dve.wait_ge(x_in, 16 * NU * (b + 2))
                    carry(dve)
                with dve.Fori(1, 5) as u:
                    for p in range(2):
                        step_kv(b, u, p)
                        if not last:
                            x_stats(b + 1, 2 * (u - 1) + p)
                steps[1] = 0
                small = iter((lambda: spreads(b + 1, 0), lambda: variance(b + 1, 0),
                              lambda: scale_and_bias(b + 1, 0), lambda: hidden(b + 1), lambda: heads(b + 1),
                              lambda: None))
                if not last:
                    means(b + 1, 0)
                for u in range(5, NU):
                    for p in range(2):
                        step_kv(b, u, p)
                        if not last:
                            next(small)()
                n = b * 2 * PAIRS + PAIRS - 1
                ratio(n, 1, S2, S6)
                scale_k(n, 1)
                low_v(b, NU - 1, 1)
                state(b)
                if not last:
                    dve.wait_ge(l_rdy, (b + 1) * 2 * NPARTS + L_CR)
                    rotation(b + 1)
                    conv_steps(b + 1, False)
                    means(b + 1, 1)
                small = iter((lambda: spreads(b + 1, 1), lambda: variance(b + 1, 1),
                              lambda: scale_and_bias(b + 1, 1), lambda: None))
                for u in range(2):
                    for p in range(2):
                        step_q(b, u, p, alive(u), False)
                        if not last:
                            next(small)()
                assert last or steps[1] == N_CHAIN, steps
                for p in range(2):
                    step_q(b, 2, p, alive(2), False)
                with dve.Fori(3, NU) as u:
                    for p in range(2):
                        step_q(b, u, p, always, not last)
                for u in range(NU, NU + 3):
                    for p in range(2):
                        step_q(b, u, p, alive(u), not last, not last and u == NU)

            dve.wait_ge(x_in, 16 * NU)
            with dve.Fori(0, NU) as u:
                x_stats(0, u)
            steps[1] = 0
            for stage in (means, spreads, variance, scale_and_bias):
                stage(0, 0)
            hidden(0)
            heads(0)
            rotation(0)
            conv_steps(0, True)
            for stage in (means, spreads, variance, scale_and_bias):
                stage(0, 1)
            assert steps[1] == N_CHAIN, steps
            with dve.Fori(0, NU) as u:
                for h in range(HALVES):
                    attn_input(0, u, h, True)
            floor_max(0, 0)
            cube(0, 0)
            floor_max(1, 1)
            ratio(0, 0, S2, S6)
            scale_k(0, 0)
            cube(1, 1)
            with dve.Fori(0, B - 1) as b:
                batch(b, False)
            batch(B - 1, True)

        @block.scalar
        def _(act):
            a = nc.scalar
            act.wait_ge(soft_rdy, 1)
            a.activation(W_C, W_A, ACT.Exp).then_inc(set_act, 1)
            act.wait_ge(soft_rdy, 2)
            a.activation(W_E, W_D, ACT.Ln).then_inc(set_act, 1)
            act.wait_ge(ready, 1)
            for s, n in ((f_six, SIX_CR), (fm_rdy, FM_CR), (y_act, YA_CR)):
                act.sem_inc(s, n)
            for i in range(2 * REVS):
                act.wait_ge(rev_full, i + 1)
                a.activation(TPM[:, 4 * i:4 * i + 4, 0, :], F[i % 2][:, :].rearrange("p (m n) -> p m n", m=4),
                             ACT.Copy, scale=a_t).then_inc(tp_act, 1)

            def root(n):
                act.wait_ge(var_rdy, n + 1)
                a.activation(ROOT, VAR, ACT.Sqrt).then_inc(root_rdy, 1)

            def squash(c):
                act.wait_ge(zb_rdy, c + 1)
                a.activation(ZB[:, 2, :], ZB[:, 0, :], ACT.Tanh).then_inc(squash_rdy, 1)
                a.activation(ZB[:, 3, :], ZB[:, 1, :], ACT.Sigmoid)
                act.wait_ge(squash_rdy, c + 1)
                a.activation(SIN[:, 0, :], ZB[:, 2, :], ACT.Sin, scale=QUARTER_PI).then_inc(trig_rdy, 1)
                a.activation(SIN[:, 1, :], ZB[:, 2, :], ACT.Sin, scale=QUARTER_PI, bias=CK[:, 0:1]
                             ).then_inc(trig_rdy, 1)

            def kernel_block(c, q):
                act.wait_ge(rot_rdy, c + 1)
                r = slice(32 * q, 32 * q + 32)
                a.copy(BD[r, 0, :, :, r], ROT[r]).then_inc(bd_hi, 1)

            def conv_input(c, h, s, p):
                n = c * 2 * NPARTS + 2 * (h * NS + s) + p
                lo, hi, row = strip_rows(s, p)
                act.wait_ge(l_rdy, n + 1)
                a.activation(XN[:, p, 0:(hi - lo) * IMG],
                             X[:, h, row * IMG:(row + hi - lo) * IMG], ACT.Identity,
                             scale=SC0[:, h:h + 1], bias=BI0[:, h:h + 1]).then_inc(xn_rdy, 1)

            def strip_inputs(c, i):
                if i == 0:
                    act.wait_ge(norm_rdy, 2 * c + 1)
                    act.wait_ge(bd_lo, 4 * (c + 1))
                for p in range(2):
                    conv_input(c, i // NS, i % NS, p)

            def conv_inputs(c):
                for i in range(2, HALVES * NS):
                    strip_inputs(c, i)

            def attn_input(c, u, h):
                act.wait_ge(l_rdy, c * 2 * NPARTS + NPARTS + HALVES * u + h + 1)
                a.activation(XN[:, h, 0:UNIT], X[:, h, bass.ds(u * UNIT, UNIT)], ACT.Identity,
                             scale=SC1[:, h:h + 1], bias=BI1[:, h:h + 1]).then_inc(xn_rdy, 1)

            def squares(n, p):
                act.wait_ge(f_max, n + 1 + MAX_CR)
                act.wait_ge(f_cube, n + 1)
                act.wait_ge(f_six, 2 * n + 2)
                for t in range(2):
                    ts = slice(t * C, (t + 1) * C)
                    a.activation(K2[:, p, ts], K0[:, p, ts], ACT.Square, scale=inv_a,
                                 accum_out=S2[:, 2 * p + t:2 * p + t + 1]).then_inc(f_sq, 1)

            def sixths(n, p):
                act.wait_ge(f_cube, n + 1 + CUBE_CR)
                for t in range(2):
                    a.activation(K2[:, p, t * C:(t + 1) * C], K3[:, p, t * C:(t + 1) * C], ACT.Square, scale=inv_a,
                                 accum_out=S6[:, 2 * p + t:2 * p + t + 1]).then_inc(f_six, 1)

            def norms(n, p, factor):
                cs = slice(2 * p, 2 * p + 2)
                act.wait_ge(f_ratio, 2 * (n + 1))
                a.activation(NORM[:, cs], RATIO[:, 0, cs], ACT.Sqrt, scale=factor).then_inc(f_root, 1)

            def copy_v(b, u, p):
                m = b * PAIRS + 2 * u + p
                act.wait_ge(v_full, m + 1)
                for t in range(2):
                    last = a.activation(V[:, :, 0, bass.ds((u * TPU + 2 * p + t) * HEADS, HEADS)],
                                        VA[p][:, t * C:(t + 1) * C].rearrange("p (c h) -> p c h", c=HD),
                                        ACT.Copy, scale=v_fac)
                last.then_inc(v_hi, 1)
                act.wait_ge(cube_used, b * 2 * PAIRS + 2 * u + p + 1)
                for t in range(2):
                    last = a.activation(
                        VT[:, p, t, :, 0:P].rearrange("p h (c f) -> p h c f", c=HD),
                        VA[p][:, t * C:(t + 1) * C].rearrange("p (c h f) -> p h c f", c=HD, h=HALVES),
                        ACT.Copy, scale=inv_a)
                last.then_inc(v_true, 1)

            def step_kv(b, u, p):
                n = b * 2 * PAIRS + 2 * u + p
                squares(n, p)
                norms(n - 1, 1 - p, inv_a2)
                copy_v(b, u, p)
                sixths(n, p)

            def depthwise(b, last):
                for c in range(HD):
                    act.wait_ge(dw_full, b * HD + c + 1)
                    a.activation(FM[:, c, :], DW[c % 4][:, 0:NT * HEADS], ACT.Identity, scale=fm_fac,
                                 bias=DWB[:, c:c + 1]).then_inc(fm_rdy, 1)
                    if not last and c in (18, 19, 20, 21):
                        kernel_block(b + 1, c - 18)
                    if not last and c in (25, 29):
                        strip_inputs(b + 1, (c - 25) // 4)

            def transposed_q(b, u, p):
                act.wait_ge(cube_used, b * 2 * PAIRS + PAIRS + 2 * u + p + 1 + USED_CR)
                a.copy(QT[:, p, :, :], T[0][:, :].rearrange("p (h n) -> p h n", h=HALVES)).then_inc(qt_rdy, 1)

            def output(b, u, h):
                e = (b * NU + u) * HALVES + h
                act.wait_ge(y_full, e + 1)
                act.wait_ge(y_out[h], 16 * (b * NU + u + OUT_CR))
                a.activation(Y[:, h, :], (PP, SM)[h][:, :], ACT.Identity, scale=out_fac, bias=CBC[:, h:h + 1]
                             ).then_inc(y_act, 1)

            def high_out(b, u, p):
                act.wait_ge(ot_full, b * PAIRS + 2 * u + p + 1)
                a.activation(OT[:, 0, :, 2 * P * p:2 * P * (p + 1)],
                             T[1][:, :].rearrange("p (h n) -> p h n", h=HALVES), ACT.Copy, scale=a_o
                             ).then_inc(oh_rdy, 1)

            def step_q(b, u, p, live, nxt, keys=False):
                n = b * 2 * PAIRS + PAIRS + 2 * u + p
                if p == 0 and live(-4):
                    high_out(b, u - 2, 0)
                if p == 0 and live(-6):
                    for h in range(HALVES):
                        output(b, u - 3, h)
                if live(p) or keys:
                    squares(n, p)
                if live(p - 1):
                    norms(n - 1, 1 - p, den_eps)
                elif keys:
                    norms(n - 1, 1 - p, inv_a2)
                if live(p - 1):
                    transposed_q(b, u - 1 + p, 1 - p)
                if nxt:
                    attn_input(b + 1, u - 3, p)
                if p == 0 and live(-3):
                    high_out(b, u - 2, 1)
                if live(p) or keys:
                    sixths(n, p)

            def batch(b, last):
                for p in range(2):
                    copy_v(b, 0, p)
                with act.Fori(1, 5) as u:
                    for p in range(2):
                        step_kv(b, u, p)
                for u in range(5, NU):
                    for p in range(2):
                        step_kv(b, u, p)
                        if not last and 2 * u + p == 11:
                            root(2 * (b + 1))
                norms(b * 2 * PAIRS + PAIRS - 1, 1, inv_a2)
                if not last:
                    squash(b + 1)
                depthwise(b, last)
                if not last:
                    conv_inputs(b + 1)
                act.wait_ge(kept, b + 1)
                for u in range(2):
                    for p in range(2):
                        step_q(b, u, p, alive(u), False)
                        if not last and 2 * u + p == 1:
                            root(2 * (b + 1) + 1)
                for p in range(2):
                    step_q(b, 2, p, alive(2), False)
                if not last:
                    act.wait_ge(norm_rdy, 2 * (b + 1) + 2)
                with act.Fori(3, NU) as u:
                    for p in range(2):
                        step_q(b, u, p, always, not last)
                for u in range(NU, NU + 3):
                    for p in range(2):
                        step_q(b, u, p, alive(u), not last, not last and u == NU)

            root(0)
            squash(0)
            for q in range(4):
                kernel_block(0, q)
            for i in range(2):
                strip_inputs(0, i)
            conv_inputs(0)
            root(1)
            act.wait_ge(norm_rdy, 2)
            with act.Fori(0, NU) as u:
                for h in range(HALVES):
                    attn_input(0, u, h)
            squares(0, 0)
            sixths(0, 0)
            squares(1, 1)
            norms(0, 0, inv_a2)
            sixths(1, 1)
            with act.Fori(0, B - 1) as b:
                batch(b, False)
            batch(B - 1, True)

        @block.tensor
        def _(pe):
            t_ = nc.tensor

            def group_mean(c, layer):
                pe.wait_ge(mean_rdy, 2 * c + layer + 1)
                t_.matmul(SM[:, 0:2], GM[:, :], DEV, start=True, stop=True).then_inc(mean_mm, 1)

            def group_spread(c, layer):
                pe.wait_ge(spread_rdy, 2 * c + layer + 1)
                t_.matmul(SM[:, 2:4], GM[:, :], SPREAD, start=True, stop=True).then_inc(spread_mm, 1)

            def hidden(c):
                pe.wait_ge(pooled_rdy, c + 1)
                for h in range(HALVES):
                    last = t_.matmul(SM[:, 4:5], W1[:, h, :], POOLED[:, h:h + 1], start=(h == 0), stop=(h == 1))
                last.then_inc(hid_mm, 1)

            def heads(c):
                pe.wait_ge(hid_rdy, 2 * (c + 1))
                for h in range(HALVES):
                    o = 8 + 2 * h
                    last = t_.matmul(SM[:, o:o + 2], W2[:, h * P:(h + 1) * P], HID[:, 0:2], start=True, stop=True)
                last.then_inc(z_mm, 1)

            PASSES = ((0, 0), (0, 1), (1, 0))

            def convolution(c):
                with pe.Fori(0, HALVES) as h:
                    for s in range(NS):
                        i = h * NS + s
                        pe.wait_ge(h_rdy, c * 2 * NPARTS + 2 * i + 2)
                        pe.wait_ge(l_rdy, c * 2 * NPARTS + 2 * i + 2 + L_CR)
                        pe.wait_ge(border, 3 * (c * HALVES * NS + i + 1))
                        for q in range(2):
                            pe.wait_ge(x1_rdy, c * CHUNKS + 2 * i + q + 1)
                            k = 0
                            for wa, xa in PASSES:
                                for t in range(TAPS):
                                    y0 = 8 * q + t // 3
                                    last = t_.matmul(VA[q][:, :], BD[:, wa, bass.ds(h, 1), t, :].rearrange(
                                        "p h o -> p (h o)"), S[:, s % 2, xa, y0:y0 + 8, t % 3:t % 3 + IMG],
                                        start=(k == 0), stop=(k == 3 * TAPS - 1))
                                    k += 1
                            last.then_inc(conv_full, 1)

            def project(b, u, p, bank, c0):
                for t in range(2):
                    at = bass.ds(u * UNIT + (2 * p + t) * P, P)
                    o = bank[p][:, t * C:(t + 1) * C]
                    k = 0
                    for h, xa in ((0, 0), (1, 0), (0, 1), (1, 1)):
                        for wa in (0, 1) if xa == 0 else (0,):
                            t_.matmul(o, XHL[:, xa, h, at], WQ[:, wa, h, c0:c0 + C], start=(k == 0), stop=False)
                            k += 1
                    last = t_.matmul(o, ONES[:, :], BQ[:, c0:c0 + C], start=False, stop=True)
                last.then_inc(f_full if bank is F else v_full, 1)

            def accumulate_state(b, u, p):
                m = b * PAIRS + 2 * u + p
                pe.wait_ge(k_scaled, 2 * (m + 1))
                pe.wait_ge(v_true, m + 1)
                for t in range(2):
                    for h in range(HALVES):
                        last = t_.matmul(T[h][:, 0:P + 1], K3[:, p, t * C + h * P:t * C + (h + 1) * P],
                                         VT[:, p, t, h, 0:P + 1], start=False, stop=False)
                last.then_inc(cube_used, 1)

            def keys(b, u, p):
                pe.wait_ge(f_max, b * 2 * PAIRS + 2 * u + p + 1)
                pe.wait_ge(h_rdy, b * 2 * NPARTS + NPARTS + HALVES * (u + 1))
                pe.wait_ge(l_rdy, b * 2 * NPARTS + NPARTS + HALVES * (u + 1) + L_CR)
                project(b, u, p, F, C)

            def values(b, u, p):
                pe.wait_ge(v_lo, b * PAIRS + 2 * u + p + 1)
                project(b, u, p, VA, 2 * C)

            def step_kv(b, u, p):
                keys(b, u, p)
                accumulate_state(b, u - 1, p)
                values(b, u, p)

            def depthwise(b):
                for c in range(HD):
                    pe.wait_ge(fm_rdy, b * HD + c + 1)
                    bank = DW[c % 4]
                    k = 0
                    for d in (1, 0, 2):
                        lo, hi = max(0, 1 - d) * HEADS, (NT - max(0, d - 1)) * HEADS
                        for ta, va in PASSES:
                            sh = (d - 1) * HEADS
                            last = t_.matmul(bank[:, lo:hi], TP[:, c, d, ta, :], V[:, c, va, lo + sh:hi + sh],
                                             start=(k == 0), stop=(k == 8))
                            k += 1
                    last.then_inc(dw_full, 1)

            def transpose_q(b, u, p):
                n = b * 2 * PAIRS + PAIRS + 2 * u + p
                pe.wait_ge(f_cube, n + 1 + CUBE_CR)
                pe.wait_ge(qt_rdy, b * PAIRS + 2 * u + p + QT_CR)
                for h in range(HALVES):
                    for t in range(2):
                        last = t_.transpose(T[0][:, (2 * h + t) * P:(2 * h + t + 1) * P],
                                            K3[:, p, t * C + h * P:t * C + (h + 1) * P], ID[:, :])
                last.then_inc(cube_used, 1)

            def attention(b, u, p):
                pe.wait_ge(qt_rdy, b * PAIRS + 2 * u + p + 1 + QT_CR)
                pe.wait_ge(o_rdy, 2 * (b * PAIRS + 2 * u + p) + O_CR)
                for t in range(2):
                    for h in range(HALVES):
                        last = t_.matmul(VA[t][:, h * KVC:(h + 1) * KVC], QT[:, p, h, t * P:(t + 1) * P],
                                         KVS[:, h, :], start=True, stop=True)
                    last.then_inc(attn_full, 1)

            def transpose_o(b, u, p):
                pe.wait_ge(o_rdy, b * NT + u * TPU + 2 * p + 2 + O_CR)
                pe.wait_ge(ol_rdy, b * PAIRS + 2 * u + p + OL_CR)
                for h in range(HALVES):
                    for t in range(2):
                        last = t_.transpose(T[1][:, (2 * h + t) * P:(2 * h + t + 1) * P],
                                            O[:, p, t * C + h * P:t * C + (h + 1) * P], ID[:, :])
                last.then_inc(ot_full, 1)

            def output(b, u, h):
                pe.wait_ge(ol_rdy, b * PAIRS + 2 * (u + 1) + OL_CR)
                pe.wait_ge(y_act, (b * NU + u) * HALVES + h + 1)
                k = 0
                for kk in range(HALVES):
                    for wa, xa in PASSES:
                        last = t_.matmul((PP, SM)[h][:, :], WP[:, wa, kk, h * P:(h + 1) * P], OT[:, xa, kk, :],
                                         start=(k == 0), stop=(k == 5))
                        k += 1
                last.then_inc(y_full, 1)

            def step_q(b, u, p, live):
                if live(p):
                    pe.wait_ge(f_max, b * 2 * PAIRS + PAIRS + 2 * u + p + 1)
                    project(b, u, p, F, 0)
                if live(p - 1):
                    transpose_q(b, u - 1 + p, 1 - p)
                if live(p - 2):
                    attention(b, u - 1, p)
                if p == 1 and live(-4):
                    for h in range(HALVES):
                        output(b, u - 2, h)
                if live(p - 3):
                    transpose_o(b, u - 2 + p, 1 - p)

            def batch(b, last):
                pe.wait_ge(ol_rdy, b * PAIRS + OL_CR)
                pe.wait_ge(qt_rdy, b * PAIRS + QT_CR)
                for h in range(HALVES):
                    t_.matmul(T[h][:, 0:P + 2], ONES[0:32, :], ZEROS, start=True, stop=False)
                pe.wait_ge(ones_rdy, b + 1)
                carry(pe)
                with pe.Fori(1, 5) as u:
                    for p in range(2):
                        step_kv(b, u, p)
                small = {10: lambda: group_mean(b + 1, 0), 11: lambda: group_spread(b + 1, 0),
                         13: lambda: hidden(b + 1), 14: lambda: heads(b + 1)}
                for u in range(5, NU):
                    for p in range(2):
                        step_kv(b, u, p)
                        if not last and 2 * u + p in small:
                            small[2 * u + p]()
                for p in range(2):
                    accumulate_state(b, NU - 1, p)
                for h in range(HALVES):
                    fin = t_.matmul(T[h][:, 0:P + 2], ONES[0:32, :], ZEROS, start=False, stop=True)
                fin.then_inc(state_full, 1)
                pe.wait_ge(v_lo, PAIRS * (b + 1) + VLO_CR)
                pe.wait_ge(f_max, b * 2 * PAIRS + PAIRS + MAX_CR)
                carry(pe)
                depthwise(b)
                pe.wait_ge(fm_rdy, HD * (b + 1) + FM_CR)
                carry(pe)
                if not last:
                    pe.wait_ge(bd_lo, 4 * (b + 2))
                    carry(pe)
                    convolution(b + 1)
                    pe.wait_ge(x1_rdy, CHUNKS * (b + 2) + X1_CR)
                pe.wait_ge(state_rdy, 4 * HPH * (b + 1))
                for u in range(2):
                    for p in range(2):
                        step_q(b, u, p, alive(u))
                        if not last and u == 0:
                            (group_mean, group_spread)[p](b + 1, 1)
                with pe.Fori(2, NU) as u:
                    for p in range(2):
                        step_q(b, u, p, always)
                for u in (NU, NU + 1):
                    for p in range(2):
                        if not last and u == NU:
                            keys(b + 1, 0, p)
                        if not last and u == NU + 1 and p == 1:
                            pe.wait_ge(o_rdy, 2 * PAIRS * (b + 1) + O_CR)
                            carry(pe)
                            values(b + 1, 0, 0)
                        step_q(b, u, p, alive(u))
                if not last:
                    values(b + 1, 0, 1)

            pe.wait_ge(ready, 1)
            pe.wait_ge(set_pool, 8)
            tsm = XHL[:, :, :, :].rearrange("p a h n -> p (a h n)").bitcast(f32)
            for i in range(2 * REVS):
                pe.wait_ge(taps_in, 16 * 12 * (i // REVS + 1))
                if i >= 2:
                    pe.wait_ge(tp_dve, i - 1)
                j = i % REVS
                t_.matmul(F[i % 2][:, :], REV, tsm[:, 512 * j:512 * j + 512], start=True, stop=True
                          ).then_inc(rev_full, 1)
            group_mean(0, 0)
            group_spread(0, 0)
            hidden(0)
            heads(0)
            pe.wait_ge(bd_lo, 4)
            convolution(0)
            group_mean(0, 1)
            group_spread(0, 1)
            pe.wait_ge(tp_dve, 2 * REVS)
            for p in range(2):
                keys(0, 0, p)
                values(0, 0, p)
            with pe.Fori(0, B - 1) as b:
                batch(b, False)
            batch(B - 1, True)


def kernel(x, L0_conv_base_kernel, L0_conv_ap_w1, L0_conv_ap_b1, L0_conv_ap_w2, L0_conv_ap_b2, L0_conv_meta_w1,
           L0_conv_meta_b1, L0_conv_meta_w2, L0_conv_meta_b2, L1_conv_Wq, L1_conv_bq, L1_conv_Wkv, L1_conv_bkv,
           L1_conv_Wproj, L1_conv_bproj, L1_conv_dwc_w, L1_conv_dwc_b, L1_conv_scale_param):
    import numpy as np
    import concourse.bacc as bacc
    from concourse import mybir as mb
    from concourse.bass_utils import run_bass_kernel_spmd

    B, C, H, W = x.shape
    G, HD = L0_conv_base_kernel.shape[0:2]
    order = np.arange(C).reshape(G, HD).T.reshape(-1)
    wkv, bkv = np.asarray(L1_conv_Wkv), np.asarray(L1_conv_bkv)
    taps = np.asarray(L1_conv_dwc_w).reshape(HD, 5, 5)
    arrays = {
        "x": np.asarray(x).reshape(B, C, H * W),
        "conv_w": np.asarray(L0_conv_base_kernel).transpose(0, 2, 3, 4, 1).reshape(C, 9, HD),
        "mlp_w1": np.concatenate([np.asarray(L0_conv_ap_w1), np.asarray(L0_conv_meta_w1)], 0).T,
        "mlp_b1": np.concatenate([np.asarray(L0_conv_ap_b1), np.asarray(L0_conv_meta_b1)]).reshape(-1, 1),
        "mlp_w2": np.concatenate([np.repeat(np.asarray(L0_conv_ap_w2).T, HD, axis=1),
                                  np.asarray(L0_conv_meta_w2).T], 0),
        "mlp_b2": np.concatenate([np.repeat(np.asarray(L0_conv_ap_b2), HD), np.asarray(L0_conv_meta_b2)]
                                 ).reshape(4, C // 2).T,
        "wqkv": np.concatenate([np.asarray(L1_conv_Wq), wkv[:C], wkv[C:][order]], 0).T,
        "bqkv": np.concatenate([np.asarray(L1_conv_bq), bkv[:C], bkv[C:][order]]).reshape(1, -1),
        "head_scale": np.asarray(L1_conv_scale_param).reshape(1, C),
        "wproj": np.asarray(L1_conv_Wproj).T[order],
        "bproj": np.asarray(L1_conv_bproj).reshape(2, C // 2).T,
        "dw_rows": np.pad(taps[:, :, ::-1], ((0, 0), (1, 1), (61, 62))),
        "dw_taps": taps.reshape(1, -1),
        "dw_b": np.asarray(L1_conv_dwc_b).reshape(1, HD),
    }
    arrays = {n: np.ascontiguousarray(v) for n, v in arrays.items()}
    nc = bacc.Bacc("TRN2", target_bir_lowering=False, num_devices=1)
    args = [nc.dram_tensor(n, v.shape, mb.dt.from_np(v.dtype), kind="ExternalInput").ap() for n, v in arrays.items()]
    out = nc.dram_tensor("out", (B, C, H * W), mb.dt.float32, kind="ExternalOutput").ap()
    conv_then_focused_attention(nc, *args, out)
    r = run_bass_kernel_spmd(nc, [arrays], core_ids=[0])
    return r.results[0]["out"].reshape(B, C, H, W)
```
